# Optimizing a Trainium2 kernel written in Bass

```python
import numpy as np
import jax
import jax.numpy as jnp

def _softmax(x, axis=-1):
    return jax.nn.softmax(x, axis=axis)

def _gelu(x):
    return jax.nn.gelu(x, approximate=True)

def _silu(x):
    return jax.nn.silu(x)

def _sigmoid(x):
    return jax.nn.sigmoid(x)

def _layernorm(x, axis=-1, eps=1e-05):
    m = jnp.mean(x, axis=axis, keepdims=True)
    v = jnp.var(x, axis=axis, keepdims=True)
    return (x - m) / jnp.sqrt(v + eps)

def _scatter_add(tgt, idx, src, axis=0):
    return tgt.at[idx].add(src)

def _segment_sum(src, seg, n):
    return jax.ops.segment_sum(src, seg, n)
kernel_name = 'mk_early_fusion_d1_tok_img256_r4_07d63d'

def setup_inputs(seed: int=0):
    np.random.seed(seed)
    _w = jnp.asarray

    def _rec_inputs():
        import jax
        import jax.numpy as jnp
        _rk = jax.random.key(seed)
        x = 7.22013e-05 + 1.00017 * jax.random.normal(jax.random.fold_in(_rk, 1), (8, 1, 1024, 64), jnp.float32)
        txt = 10 + 10 * jax.random.normal(jax.random.fold_in(_rk, 2), (8, 512, 64), jnp.float32)
        return (x, txt)
    x, txt = _rec_inputs()

    def _L0_tok_setup():
        import jax, jax.numpy as jnp
        import numpy as np
        T, D_IN, D_INT, D_OUT, B = (1024, 64, 64, 64, 8)
        key = jax.random.key(seed)
        ks = jax.random.split(key, 12)
        s_in = 1.0 / np.sqrt(D_IN)
        s_int = 1.0 / np.sqrt(D_INT)
        return {'x_batched': jax.random.normal(ks[0], (B, 1, T, D_IN), dtype=jnp.float32), 'd_gamma_batched': jax.random.uniform(ks[1], (T, T), dtype=jnp.float32), 'Wq': jax.random.uniform(ks[2], (D_IN, D_INT), jnp.float32, -s_in, s_in), 'bq': jax.random.uniform(ks[3], (D_INT,), jnp.float32, -s_in, s_in), 'Wk': jax.random.uniform(ks[4], (D_IN, D_INT), jnp.float32, -s_in, s_in), 'bk': jax.random.uniform(ks[5], (D_INT,), jnp.float32, -s_in, s_in), 'Wv': jax.random.uniform(ks[6], (D_IN, D_INT), jnp.float32, -s_in, s_in), 'bv': jax.random.uniform(ks[7], (D_INT,), jnp.float32, -s_in, s_in), 'Wo': jax.random.uniform(ks[8], (D_INT, D_OUT), jnp.float32, -s_int, s_int), 'bo': jax.random.uniform(ks[9], (D_OUT,), jnp.float32, -s_int, s_int), 'prelu_a': jnp.float32(0.25)}
    _L0_tok_all = _L0_tok_setup()
    _L0_tok_in = {k: v for k, v in _L0_tok_all.items() if k in ('d_gamma_batched', 'Wq', 'bq', 'Wk', 'bk', 'Wv', 'bv', 'Wo', 'bo', 'prelu_a')}
    del _L0_tok_all

    def _L0_attn_setup():
        import jax, jax.numpy as jnp
        import numpy as np
        import math
        D_MODEL = 64
        D_STATE = 16
        D_CONV = 4
        EXPAND = 2
        D_INNER = EXPAND * D_MODEL
        DT_RANK = math.ceil(D_MODEL / 16)
        EPS = 1e-05

        def rmsnorm(x, w):
            return x * jax.lax.rsqrt(jnp.mean(x * x, axis=-1, keepdims=True) + EPS) * w

        def mamba_mixer(x, in_proj, conv_w, conv_b, x_proj, dt_w, dt_b, A_log, Dp, out_proj):
            Bsz, L, _ = x.shape
            xz = x @ in_proj.T
            xh, z = jnp.split(xz, 2, axis=-1)
            xp = jnp.pad(xh, ((0, 0), (D_CONV - 1, 0), (0, 0)))
            xc = sum((xp[:, k:k + L, :] * conv_w[:, k] for k in range(D_CONV))) + conv_b
            xc = jax.nn.silu(xc)
            x_dbl = xc @ x_proj.T
            dt, Bm, Cm = jnp.split(x_dbl, [DT_RANK, DT_RANK + D_STATE], axis=-1)
            delta = jax.nn.softplus(dt @ dt_w.T + dt_b)
            A = -jnp.exp(A_log)
            dA = jnp.exp(jnp.einsum('bld,dn->lbdn', delta, A))
            dBu = jnp.einsum('bld,bln,bld->lbdn', delta, Bm, xc)

            def step(h, inp):
                a, b = inp
                h = a * h + b
                return (h, h)
            h0 = jnp.zeros((Bsz, D_INNER, D_STATE), xc.dtype)
            _, hs = jax.lax.scan(step, h0, (dA, dBu))
            y = jnp.einsum('lbdn,bln->bld', hs, Cm) + xc * Dp
            y = y * jax.nn.silu(z)
            return y @ out_proj.T

        def block(x, norm_w, in_proj, conv_w, conv_b, x_proj, dt_w, dt_b, A_log, Dp, out_proj):
            residual = x
            h = mamba_mixer(rmsnorm(x, norm_w), in_proj, conv_w, conv_b, x_proj, dt_w, dt_b, A_log, Dp, out_proj)
            return h + residual
        key = jax.random.key(seed)
        ks = jax.random.split(key, 16)
        B, L = (4, 512)

        def n(k, shape, s=0.02):
            return jax.random.normal(k, shape, jnp.float32) * s
        inp = {'x': jax.random.normal(ks[0], (B, L, D_MODEL), jnp.float32)}
        i = 1
        for pre in ('fw', 'bw'):
            inp[pre + '_norm'] = jnp.ones((D_MODEL,), jnp.float32)
            inp[pre + '_in_proj'] = n(ks[i], (2 * D_INNER, D_MODEL))
            i += 1
            inp[pre + '_conv_w'] = n(ks[i], (D_INNER, D_CONV), 0.1)
            i += 1
            inp[pre + '_conv_b'] = jnp.zeros((D_INNER,), jnp.float32)
            inp[pre + '_x_proj'] = n(ks[i], (DT_RANK + 2 * D_STATE, D_INNER))
            i += 1
            inp[pre + '_dt_w'] = n(ks[i], (D_INNER, DT_RANK), 0.1)
            i += 1
            inp[pre + '_dt_b'] = n(ks[i], (D_INNER,), 0.1)
            i += 1
            inp[pre + '_A_log'] = jnp.log(jnp.tile(jnp.arange(1, D_STATE + 1, dtype=jnp.float32), (D_INNER, 1)))
            inp[pre + '_D'] = jnp.ones((D_INNER,), jnp.float32)
            inp[pre + '_out_proj'] = n(ks[i], (D_MODEL, D_INNER))
            i += 1
        return inp
    _L0_attn_all = _L0_attn_setup()
    _L0_attn_in = {k: v for k, v in _L0_attn_all.items() if k in ('fw_norm', 'fw_in_proj', 'fw_conv_w', 'fw_conv_b', 'fw_x_proj', 'fw_dt_w', 'fw_dt_b', 'fw_A_log', 'fw_D', 'fw_out_proj', 'bw_norm', 'bw_in_proj', 'bw_conv_w', 'bw_conv_b', 'bw_x_proj', 'bw_dt_w', 'bw_dt_b', 'bw_A_log', 'bw_D', 'bw_out_proj')}
    del _L0_attn_all

    def _L0_ffn_setup():
        import jax, jax.numpy as jnp
        import numpy as np
        B, S, D = (8, 1024, 64)
        H = 4 * D
        CAPACITY = 0.5
        key = jax.random.key(seed)
        ks = jax.random.split(key, 6)
        x = jax.random.normal(ks[0], (B, S, D), dtype=jnp.float32)
        attention_mask = jnp.zeros((B, 1, 1, S), dtype=jnp.float32)
        wr = jax.random.normal(ks[1], (D, 1), dtype=jnp.float32) * 0.02
        br = jnp.zeros((1,), dtype=jnp.float32)
        w1 = jax.random.normal(ks[2], (D, H), dtype=jnp.float32) * 0.02
        b1 = jnp.zeros((H,), dtype=jnp.float32)
        w2 = jax.random.normal(ks[3], (H, D), dtype=jnp.float32) * 0.02
        b2 = jnp.zeros((D,), dtype=jnp.float32)
        return {'x': x, 'attention_mask': attention_mask, 'wr': wr, 'br': br, 'w1': w1, 'b1': b1, 'w2': w2, 'b2': b2}
    _L0_ffn_all = _L0_ffn_setup()
    _L0_ffn_in = {k: v for k, v in _L0_ffn_all.items() if k in ('attention_mask', 'wr', 'br', 'w1', 'b1', 'w2', 'b2')}
    del _L0_ffn_all
    return {'x': x, 'txt': txt, 'L0_tok_d_gamma_batched': _L0_tok_in['d_gamma_batched'], 'L0_tok_Wq': _L0_tok_in['Wq'], 'L0_tok_bq': _L0_tok_in['bq'], 'L0_tok_Wk': _L0_tok_in['Wk'], 'L0_tok_bk': _L0_tok_in['bk'], 'L0_tok_Wv': _L0_tok_in['Wv'], 'L0_tok_bv': _L0_tok_in['bv'], 'L0_tok_Wo': _L0_tok_in['Wo'], 'L0_tok_bo': _L0_tok_in['bo'], 'L0_tok_prelu_a': _L0_tok_in['prelu_a'], 'L0_attn_fw_norm': _L0_attn_in['fw_norm'], 'L0_attn_fw_in_proj': _L0_attn_in['fw_in_proj'], 'L0_attn_fw_conv_w': _L0_attn_in['fw_conv_w'], 'L0_attn_fw_conv_b': _L0_attn_in['fw_conv_b'], 'L0_attn_fw_x_proj': _L0_attn_in['fw_x_proj'], 'L0_attn_fw_dt_w': _L0_attn_in['fw_dt_w'], 'L0_attn_fw_dt_b': _L0_attn_in['fw_dt_b'], 'L0_attn_fw_A_log': _L0_attn_in['fw_A_log'], 'L0_attn_fw_D': _L0_attn_in['fw_D'], 'L0_attn_fw_out_proj': _L0_attn_in['fw_out_proj'], 'L0_attn_bw_norm': _L0_attn_in['bw_norm'], 'L0_attn_bw_in_proj': _L0_attn_in['bw_in_proj'], 'L0_attn_bw_conv_w': _L0_attn_in['bw_conv_w'], 'L0_attn_bw_conv_b': _L0_attn_in['bw_conv_b'], 'L0_attn_bw_x_proj': _L0_attn_in['bw_x_proj'], 'L0_attn_bw_dt_w': _L0_attn_in['bw_dt_w'], 'L0_attn_bw_dt_b': _L0_attn_in['bw_dt_b'], 'L0_attn_bw_A_log': _L0_attn_in['bw_A_log'], 'L0_attn_bw_D': _L0_attn_in['bw_D'], 'L0_attn_bw_out_proj': _L0_attn_in['bw_out_proj'], 'L0_ffn_attention_mask': _L0_ffn_in['attention_mask'], 'L0_ffn_wr': _L0_ffn_in['wr'], 'L0_ffn_br': _L0_ffn_in['br'], 'L0_ffn_w1': _L0_ffn_in['w1'], 'L0_ffn_b1': _L0_ffn_in['b1'], 'L0_ffn_w2': _L0_ffn_in['w2'], 'L0_ffn_b2': _L0_ffn_in['b2']}

def reference(x, txt, L0_tok_d_gamma_batched, L0_tok_Wq, L0_tok_bq, L0_tok_Wk, L0_tok_bk, L0_tok_Wv, L0_tok_bv, L0_tok_Wo, L0_tok_bo, L0_tok_prelu_a, L0_attn_fw_norm, L0_attn_fw_in_proj, L0_attn_fw_conv_w, L0_attn_fw_conv_b, L0_attn_fw_x_proj, L0_attn_fw_dt_w, L0_attn_fw_dt_b, L0_attn_fw_A_log, L0_attn_fw_D, L0_attn_fw_out_proj, L0_attn_bw_norm, L0_attn_bw_in_proj, L0_attn_bw_conv_w, L0_attn_bw_conv_b, L0_attn_bw_x_proj, L0_attn_bw_dt_w, L0_attn_bw_dt_b, L0_attn_bw_A_log, L0_attn_bw_D, L0_attn_bw_out_proj, L0_ffn_attention_mask, L0_ffn_wr, L0_ffn_br, L0_ffn_w1, L0_ffn_b1, L0_ffn_w2, L0_ffn_b2):
    import jax
    import jax.numpy as jnp

    def _L0_tok_ref(x_batched, d_gamma_batched, Wq, bq, Wk, bk, Wv, bv, Wo, bo, prelu_a):
        import jax, jax.numpy as jnp
        import numpy as np
        T, D_IN, D_INT, D_OUT, B = (1024, 64, 64, 64, 8)
        x = x_batched.reshape(x_batched.shape[0], T, D_IN)
        q = x @ Wq + bq
        k = x @ Wk + bk
        v = x @ Wv + bv
        scores = jnp.einsum('btd,bsd->bts', q, k)
        retained = jnp.einsum('bts,bsd->btd', d_gamma_batched * scores, v)
        y = retained @ Wo + bo
        out = jnp.where(y >= 0, y, prelu_a * y)
        return out

    def _L0_attn_ref(x, fw_norm, fw_in_proj, fw_conv_w, fw_conv_b, fw_x_proj, fw_dt_w, fw_dt_b, fw_A_log, fw_D, fw_out_proj, bw_norm, bw_in_proj, bw_conv_w, bw_conv_b, bw_x_proj, bw_dt_w, bw_dt_b, bw_A_log, bw_D, bw_out_proj):
        import jax, jax.numpy as jnp
        import numpy as np
        import math
        D_MODEL = 64
        D_STATE = 16
        D_CONV = 4
        EXPAND = 2
        D_INNER = EXPAND * D_MODEL
        DT_RANK = math.ceil(D_MODEL / 16)
        EPS = 1e-05

        def rmsnorm(x, w):
            return x * jax.lax.rsqrt(jnp.mean(x * x, axis=-1, keepdims=True) + EPS) * w

        def mamba_mixer(x, in_proj, conv_w, conv_b, x_proj, dt_w, dt_b, A_log, Dp, out_proj):
            Bsz, L, _ = x.shape
            xz = x @ in_proj.T
            xh, z = jnp.split(xz, 2, axis=-1)
            xp = jnp.pad(xh, ((0, 0), (D_CONV - 1, 0), (0, 0)))
            xc = sum((xp[:, k:k + L, :] * conv_w[:, k] for k in range(D_CONV))) + conv_b
            xc = jax.nn.silu(xc)
            x_dbl = xc @ x_proj.T
            dt, Bm, Cm = jnp.split(x_dbl, [DT_RANK, DT_RANK + D_STATE], axis=-1)
            delta = jax.nn.softplus(dt @ dt_w.T + dt_b)
            A = -jnp.exp(A_log)
            dA = jnp.exp(jnp.einsum('bld,dn->lbdn', delta, A))
            dBu = jnp.einsum('bld,bln,bld->lbdn', delta, Bm, xc)

            def step(h, inp):
                a, b = inp
                h = a * h + b
                return (h, h)
            h0 = jnp.zeros((Bsz, D_INNER, D_STATE), xc.dtype)
            _, hs = jax.lax.scan(step, h0, (dA, dBu))
            y = jnp.einsum('lbdn,bln->bld', hs, Cm) + xc * Dp
            y = y * jax.nn.silu(z)
            return y @ out_proj.T

        def block(x, norm_w, in_proj, conv_w, conv_b, x_proj, dt_w, dt_b, A_log, Dp, out_proj):
            residual = x
            h = mamba_mixer(rmsnorm(x, norm_w), in_proj, conv_w, conv_b, x_proj, dt_w, dt_b, A_log, Dp, out_proj)
            return h + residual
        fwd = block(x, fw_norm, fw_in_proj, fw_conv_w, fw_conv_b, fw_x_proj, fw_dt_w, fw_dt_b, fw_A_log, fw_D, fw_out_proj)
        xb = jnp.flip(x, axis=1)
        bwd = block(xb, bw_norm, bw_in_proj, bw_conv_w, bw_conv_b, bw_x_proj, bw_dt_w, bw_dt_b, bw_A_log, bw_D, bw_out_proj)
        bwd = jnp.flip(bwd, axis=1)
        return fwd + bwd

    def _L0_ffn_ref(x, attention_mask, wr, br, w1, b1, w2, b2):
        import jax, jax.numpy as jnp
        import numpy as np
        B, S, D = (8, 1024, 64)
        H = 4 * D
        CAPACITY = 0.5
        b, s, d = x.shape
        weights = (jnp.einsum('bsd,do->bso', x, wr) + br)[..., 0]
        k = max(1, int(CAPACITY * s))
        kk = k - 1 if k > 1 else 1
        _, idx = jax.lax.top_k(weights, k)
        sel_idx = idx[:, :kk]
        sel = jnp.take_along_axis(x, sel_idx[:, :, None], axis=1)
        h = jax.nn.gelu(jnp.einsum('bkd,dh->bkh', sel, w1) + b1)
        y = jnp.einsum('bkh,hd->bkd', h, w2) + b2
        w_sel = jnp.take_along_axis(weights, sel_idx, axis=1)
        y = y * w_sel[..., None]
        batch_idx = jnp.arange(b)[:, None]
        processed = jnp.zeros_like(x).at[batch_idx, sel_idx].set(y)
        return processed + x
    h = _L0_tok_ref(x, L0_tok_d_gamma_batched, L0_tok_Wq, L0_tok_bq, L0_tok_Wk, L0_tok_bk, L0_tok_Wv, L0_tok_bv, L0_tok_Wo, L0_tok_bo, L0_tok_prelu_a)
    h = jnp.concatenate([h, txt], axis=1)
    h = h + _L0_attn_ref(_layernorm(h, axis=-1), L0_attn_fw_norm, L0_attn_fw_in_proj, L0_attn_fw_conv_w, L0_attn_fw_conv_b, L0_attn_fw_x_proj, L0_attn_fw_dt_w, L0_attn_fw_dt_b, L0_attn_fw_A_log, L0_attn_fw_D, L0_attn_fw_out_proj, L0_attn_bw_norm, L0_attn_bw_in_proj, L0_attn_bw_conv_w, L0_attn_bw_conv_b, L0_attn_bw_x_proj, L0_attn_bw_dt_w, L0_attn_bw_dt_b, L0_attn_bw_A_log, L0_attn_bw_D, L0_attn_bw_out_proj)
    h = h + _L0_ffn_ref(_layernorm(h, axis=-1), L0_ffn_attention_mask, L0_ffn_wr, L0_ffn_br, L0_ffn_w1, L0_ffn_b1, L0_ffn_w2, L0_ffn_b2)
    return h

_drawn_inputs = setup_inputs


def setup_inputs(seed=0):
    import zlib

    import numpy as np

    out = dict(_drawn_inputs(seed))
    spreads = {'L0_attn_fw_norm': (1.0, 0.6),
     'L0_attn_fw_conv_b': (0.0, 0.8),
     'L0_attn_fw_D': (1.0, 0.6),
     'L0_attn_bw_norm': (1.0, 0.6),
     'L0_attn_bw_conv_b': (0.0, 0.8),
     'L0_attn_bw_D': (1.0, 0.6),
     'L0_ffn_b1': (0.0, 2.0),
     'L0_ffn_b2': (0.0, 2.0)}
    factors = {'L0_tok_bo': 23.79,
     'L0_attn_fw_in_proj': 8.0,
     'L0_attn_fw_conv_w': 8.0,
     'L0_attn_fw_x_proj': 8.0,
     'L0_attn_fw_dt_b': 8.0,
     'L0_attn_fw_A_log': 8.0,
     'L0_attn_fw_out_proj': 8.0,
     'L0_attn_bw_in_proj': 8.0,
     'L0_attn_bw_conv_w': 8.0,
     'L0_attn_bw_x_proj': 8.0,
     'L0_attn_bw_dt_b': 8.0,
     'L0_attn_bw_A_log': 8.0,
     'L0_attn_bw_out_proj': 8.0,
     'L0_ffn_wr': 64.0,
     'L0_ffn_w1': 64.0,
     'L0_ffn_w2': 64.0}
    for name, (base, spread) in spreads.items():
        noise = np.random.default_rng([zlib.crc32(name.encode()), seed]).standard_normal(out[name].shape)
        drawn = base * np.exp(spread * noise) if base else spread * noise
        out[name] = jnp.asarray(drawn.astype(out[name].dtype))
    for name, factor in factors.items():
        out[name] = (out[name] * factor).astype(out[name].dtype)
    return out
```

```python
from contextlib import ExitStack

import concourse.bass as bass
import concourse.mybir as mybir
from concourse.alu_op_type import AluOpType as ALU

F32 = mybir.dt.float32
BF16 = mybir.dt.bfloat16
ACT = mybir.ActivationFunctionType
AX_X = mybir.AxisListType.X

P = 128
NB = 8
DM = 64
TI = 1024
TX = 512
L = TI + TX
NT = L // P
NI = TI // P
DI = 128
NS = 16
RK = 4
CH = 512
NC = L // CH
NU = 2 * NC
BL = 8
NJ = CH // BL
NG = NJ // 4
HID = 4 * DM
KK = L // 2 - 1
EPS = 1e-5
assert NS * BL == P and NG == NS

HEAD, TAIL, PROJ = list(range(5)), list(range(5, 20)), [20]
ACT_HEAD = ["x0", "x0u", "x1", "x1u", "q0", "k0", "q1", "k1", "v", "r0", "r1"]
ACT_TAIL = [f"X{i}{h}" for i in range(3) for h in "lu"] + [f"s{i}" for i in range(12)]
LAST_READ = {0: "x0u", 1: "x1u", 2: "k0", 3: "k1", 4: "v", **{5 + i: f"X{i}u" for i in range(3)},
             **{8 + i: f"s{i}" for i in range(12)}}
LN_OPS = 16
RANK_OPS = 4 * NT - 2
P3_OPS = 11 + RANK_OPS + 5
PREP = 15


def at_least(eng, sem, value):
    if isinstance(value, int) and value <= 0:
        return
    eng.wait_ge(sem, value)


def uses(where):
    return {"first": HEAD + PROJ, "mid": HEAD + TAIL + PROJ, "after": TAIL}[where]


def where_is(b):
    return {0: "first", NB: "after"}.get(b, "mid") if isinstance(b, int) else "mid"


def g_index(b, k):
    w = where_is(b)
    before = 0 if w == "first" else len(uses("first")) + len(uses("mid")) * (b - 1)
    return before + uses(w).index(k)


def act_value(b, name):
    w = where_is(b)
    if w == "first":
        return ACT_HEAD.index(name) + 1
    base = len(ACT_HEAD) + (len(ACT_HEAD) + len(ACT_TAIL)) * (b - 1)
    names = ACT_TAIL if w == "after" else ACT_HEAD + ACT_TAIL
    return base + names.index(name) + 1


def unit_of(k):
    d, c = divmod(k % NU, NC)
    return d, (c if d == 0 else NC - 1 - c)


def build(nc, T, out):
    with ExitStack() as ctx:
        def sb(name, shape, dt=F32):
            return ctx.enter_context(nc.sbuf_tensor(name, shape, dt))

        def sem(name):
            return ctx.enter_context(nc.semaphore(name))

        bank = [ctx.enter_context(nc.psum_tensor(f"bank{i}", [P, 512], F32)) for i in range(8)]
        conv_dram = nc.dram_tensor("conv_scratch", (NB, 2, DI, L), F32, kind="Internal").ap()
        gate_dram = nc.dram_tensor("gate_scratch", (NB, 2, DI, L), F32, kind="Internal").ap()

        resid = sb("resid", [P, NB, NT, DM])
        ident = sb("ident", [P, P])
        arena = sb("arena", [P, 2, NS * CH])
        w_qk = sb("w_qk", [DM + 1, 2 * DM])
        w_v = sb("w_v", [DM + 1, DM])
        w_o = sb("w_o", [DM + 1, DM])
        slope = sb("slope", [P, 1])
        ones_row = sb("ones_row", [1, P])
        conv_t = sb("conv_t", [P, 2, 2, DI])
        gate_t = sb("gate_t", [DM, 2, DI])
        b_rep = sb("b_rep", [DI, 2, 96])
        c_sel = sb("c_sel", [DI, 2, BL, P])
        delta_t = sb("delta_t", [DI, 2, DI])
        out_t = sb("out_t", [DI, 2, DM])
        a_neg = sb("a_neg", [DI, 2, NS])
        vecs = sb("vecs", [P, 2, 8])
        CB, DTB, DSK, NRM, CW = range(5)
        pick = sb("pick", [96, NS, P], BF16)
        block_mask = sb("block_mask", [P, BL])
        w_1 = sb("w_1", [DM, HID])
        b_1 = sb("b_1", [P, 2])
        w_2 = sb("w_2", [P, 2, DM])
        b_2 = sb("b_2", [1, DM])
        w_r = sb("w_r", [DM + 1, 1])
        w_rr = sb("w_rr", [DM + 1, P])
        before = sb("before", [P, P])
        ones_b = sb("ones_b", [P, P], BF16)
        xc_in = sb("xc_in", [P, NU, CH])
        zs_in = sb("zs_in", [P, 3, CH])
        delta = sb("delta", [P, 2, CH])
        du = sb("du", [P, 2, CH])
        soft = sb("soft", [P, CH])
        relu = sb("relu", [P, CH])
        b_parts = sb("b_parts", [96, 2, CH], BF16)
        b_rest = sb("b_rest", [96, CH])
        b_high = sb("b_high", [96, CH], BF16)
        part_mask = sb("part_mask", [96, 2])
        decay = sb("decay", [P, 4, CH])
        drive = sb("drive", [P, 4, CH])
        h_t = sb("h_t", [P, 4, CH])
        c_col = sb("c_col", [P, 2, NJ])
        c_mat = sb("c_mat", [P, 2, NJ, BL])
        y_skip = sb("y_skip", [P, 2, CH])
        y_gated = sb("y_gated", [P, 2, CH])
        gamma_t = arena[:, 0, :].rearrange("p (s t) -> p s t", s=NI)
        A1 = arena[:, 1, :]
        x_t = A1[:, 0:1024]
        q_t = A1[0:DM, 1024:2048]
        k_t = A1[0:DM, 2048:3072]
        v_sb = A1[:, 3072:3584].rearrange("p (t d) -> p t d", t=NI)
        mixed = A1[:, 3584:5632].rearrange("p (r t) -> p r t", r=4)
        r_t = A1[:, 5632:6656]
        x_in = A1[:, 6656:7168].rearrange("p (t d) -> p t d", t=NI)
        staged = decay
        drive_flat = drive[:, :, :].rearrange("p r t -> p (r t)")
        gamma_in = drive_flat.rearrange("p (r t) -> p r t", r=2)
        x_mid = drive_flat[:, 0:768].rearrange("p (t d) -> p t d", t=NT)
        x_sq = drive_flat[:, 768:1536].rearrange("p (t d) -> p t d", t=NT)
        x_rms = h_t[:, :, :].rearrange("p r t -> p (r t)")[:, 0:NT * 2 * DM].rearrange(
            "p (t a d) -> p t a d", t=NT, a=2)
        x_pair = sb("x_pair", [P, L + 8])
        zero_b = sb("zero_b", [P, NT], BF16)
        stat = sb("stat", [P, 10, NT])
        neg_part = sb("neg_part", [P, NI * DM])
        in_w = sb("in_w", [P, 2, 2, DM])
        tap_w = sb("tap_w", [P, 2, 4, DM])
        xp_w = sb("xp_w", [RK + 2 * NS, 2, DI])
        dt_w = sb("dt_w", [DI, 2, RK])
        dtw_t = sb("dtw_t", [RK, 2, DI])
        op_w = sb("op_w", [DM, 2, DI])
        a_log = sb("a_log", [DI, 2, NS])
        conv_w = sb("conv_w", [P, 2, 4])
        slope_in = sb("slope_in", [1, 1])
        A0 = arena[:, 0, :]
        xl = A0[:, 0:768].rearrange("p (t d) -> p t d", t=NT)
        sq3 = A0[:, 768:1536].rearrange("p (t d) -> p t d", t=NT)
        xl_t = A0[:, 1536:3072]
        w_row = A0[:, 3072:4608]
        w_diag = A0[:, 4608:6144]
        y_out = A0[:, 6144:6912].rearrange("p (t d) -> p t d", t=NT)
        hid = xc_in[:, :, :].rearrange("p r t -> p (r t)").rearrange("p (g t) -> p g t", g=2)
        w_eq = sb("w_eq", [P, 2, P])
        A1b = arena[:, 1, :].bitcast(BF16)
        higher_a = A1b[:, 0:10 * L].rearrange("p (j t) -> p j t", j=10)
        higher_b = decay[:, :, :].rearrange("p r t -> p (r t)").bitcast(BF16)[:, 0:2 * L].rearrange(
            "p (j t) -> p j t", j=2)

        def higher_of(j):
            return higher_a[:, j, :] if j < 10 else higher_b[:, j - 10, :]

        wl = sem("weights_loaded")
        s_id = sem("ident_ready")
        const = sem("constants_ready")
        prep_v = sem("prep_vector")
        prep_a = sem("prep_scalar")
        prep_p = sem("prep_tensor")
        prep_e = sem("prep_exp")
        masks = sem("masks_ready")
        gamma_ld = [sem(f"gamma_loaded{i}") for i in range(2)]
        x_loaded = sem("x_loaded")
        txt_loaded = sem("txt_loaded")
        g_full = sem("generic_bank_full")
        act_read = sem("act_read")
        sc_full = sem("scores_full")
        mix_done = sem("mixed_ready")
        ret_mm = sem("retained_added")
        prelu_done = sem("prelu_done")
        ln = sem("norm_step")
        sq_root = sem("square_root")
        neg_done = sem("prelu_negative_part")
        gamma_turned = sem("gamma_turned")
        gamma_a = sem("gamma_copied_scalar")
        gamma_v = sem("gamma_copied_vector")
        stored = [sem(f"stored{i}") for i in range(4)]
        phase_end = sem("phase_end")
        xc_ld = [sem(f"xc_loaded{i}") for i in range(NU)]
        zs_ld = [sem(f"zs_loaded{i}") for i in range(3)]
        raw_full = sem("raw_delta_full")
        abs_done = sem("abs_done")
        exp_done = sem("softplus_exp_done")
        ln_done = sem("softplus_ln_done")
        relu_done = sem("relu_done")
        delta_ready = sem("delta_ready")
        du_ready = sem("du_ready")
        brep_full = sem("b_rep_full")
        part1 = sem("b_part1")
        rest_done = sem("b_rest")
        part2 = sem("b_part2")
        parts_ready = sem("b_parts_ready")
        c_full = sem("c_full")
        c_copied = sem("c_copied")
        c_ready = sem("c_mat_ready")
        b_full = sem("b_broadcast")
        decay_ready = sem("decay_ready")
        drive_done = sem("drive_done")
        scanned = sem("scanned")
        turned = sem("turned")
        turn_copied = sem("turn_copied")
        contracted = sem("contracted")
        skip_done = sem("skip_added")
        gated = sem("gated")
        out_full = sem("out_full")
        added = sem("added")
        v3 = sem("vector_step3")
        root3 = sem("root3")
        t3 = sem("turned3")
        xt3 = sem("xl_turned_copied")
        w3 = sem("router_full")
        wc3 = sem("router_copied")
        h3 = sem("hidden_full")
        g3 = sem("gelu_done")
        y3 = sem("ffn_full")
        rk3 = sem("rank_full")
        o3 = sem("out_stored")

        block = ctx.enter_context(nc.Block())

        def tok(b):
            if isinstance(b, int):
                return resid[:, b, :, :]
            return resid[:, bass.ds(b, 1), :, :].rearrange("p o t d -> p (o t) d")

        def dram_batch(ap, b):
            if isinstance(b, int):
                return ap[b]
            return ap[bass.ds(b, 1)].rearrange("o a p t -> (o a) p t")

        def dram_b3(ap, b):
            if isinstance(b, int):
                return ap[b]
            return ap[bass.ds(b, 1)].rearrange("o t d -> (o t) d")

        def end_phase(eng, n):
            eng.sem_inc(phase_end, 1)
            eng.wait_ge(phase_end, 5 * n)

        G = bank[5:8]
        RT = bank[4]

        def wait_bank(eng, b, k):
            w = where_is(b)
            earlier = [j for j in uses(w) if j < k and j % 3 == k % 3]
            if earlier:
                bb, j = b, earlier[-1]
            elif w == "first":
                return
            else:
                bb = b - 1
                ww = "first" if (w == "mid" and isinstance(b, int) and b == 1) else "mid"
                j = [i for i in uses(ww) if i % 3 == k % 3][-1]
            if j == PROJ[0]:
                at_least(eng, prelu_done, bb + 1)
            else:
                at_least(eng, act_read, act_value(bb, LAST_READ[j]))

        PRE = ("fw", "bw")
        WEIGHTS = 38

        def at(b, k, step):
            return b + (k + step) // NU, (k + step) % NU

        def num(b, k):
            return NU * b + k

        @block.sync
        def _(sp):
            jobs = [
                (w_qk[0:DM, 0:DM], T["L0_tok_Wq"]), (w_qk[0:DM, DM:2 * DM], T["L0_tok_Wk"]),
                (w_qk[DM:DM + 1, 0:DM], T["L0_tok_bq"].rearrange("(a d) -> a d", a=1)),
                (w_qk[DM:DM + 1, DM:2 * DM], T["L0_tok_bk"].rearrange("(a d) -> a d", a=1)),
                (w_v[0:DM, :], T["L0_tok_Wv"]),
                (w_v[DM:DM + 1, :], T["L0_tok_bv"].rearrange("(a d) -> a d", a=1)),
                (w_o[0:DM, :], T["L0_tok_Wo"]),
                (w_o[DM:DM + 1, :], T["L0_tok_bo"].rearrange("(a d) -> a d", a=1)),
                (slope_in[:, :], T["L0_tok_prelu_a"]),
                (w_1[:, :], T["L0_ffn_w1"]),
                (b_1[:, 0:1], T["L0_ffn_b1"][0:P].rearrange("(p a) -> p a", a=1)),
                (b_1[:, 1:2], T["L0_ffn_b1"][P:HID].rearrange("(p a) -> p a", a=1)),
                (w_2[:, :, :], T["L0_ffn_w2"].rearrange("(g p) d -> p g d", p=P)),
                (b_2[:, :], T["L0_ffn_b2"].rearrange("(a d) -> a d", a=1)),
                (w_r[0:DM, :], T["L0_ffn_wr"]),
                (w_r[DM:DM + 1, :], T["L0_ffn_br"].rearrange("(a d) -> a d", a=1)),
            ]
            for d, pre in enumerate(PRE):
                def t(name):
                    return T[f"L0_attn_{pre}_{name}"]

                def col(ap):
                    return ap.rearrange("(p a) -> p a", a=1)

                jobs += [
                    (in_w[:, d, :, :], t("in_proj").rearrange("(h p) i -> p h i", p=DI)),
                    (conv_w[:, d, :], t("conv_w")),
                    (vecs[:, d, CB:CB + 1], col(t("conv_b"))),
                    (vecs[:, d, DTB:DTB + 1], col(t("dt_b"))),
                    (vecs[:, d, DSK:DSK + 1], col(t("D"))),
                    (vecs[0:DM, d, NRM:NRM + 1], col(t("norm"))),
                    (vecs[DM:P, d, NRM:NRM + 1], col(t("norm"))),
                    (a_log[:, d, :], t("A_log")),
                    (xp_w[:, d, :], t("x_proj")),
                    (dt_w[:, d, :], t("dt_w")),
                    (op_w[:, d, :], t("out_proj")),
                ]
            for dst, src in jobs:
                sp.dma_start(dst, src).then_inc(wl, 16)
            assert len(jobs) == WEIGHTS
            for t in range(NI):
                if t >= 2:
                    sp.wait_ge(gamma_turned, 2 * (t - 1))
                sp.dma_start(gamma_in[:, t % 2, :], T["L0_tok_d_gamma_batched"][t * P:(t + 1) * P, :])\
                    .then_inc(gamma_ld[t % 2], 16)

            def x_load(b):
                src = T["x"][b, 0] if isinstance(b, int) else \
                    T["x"][bass.ds(b, 1)].rearrange("o a t d -> (o a t) d")
                if not (isinstance(b, int) and b == 0):
                    sp.wait_ge(g_full, g_index(b - 1, 1) + 1)
                sp.dma_start(x_in, src.rearrange("(t p) d -> p t d", p=P)).then_inc(x_loaded, 16)

            def stores(b):
                for q in range(12):
                    d, c, z = q // 6, (q % 6) // 2, q % 2
                    sp.wait_ge(act_read, act_value(b + 1, f"s{q}"))
                    dst = dram_batch(gate_dram if z else conv_dram, b)[d, :, c * CH:(c + 1) * CH]
                    sp.dma_start(dst, staged[:, q % 4, :]).then_inc(stored[q % 4], 16)

            x_load(0)
            x_load(1)
            x_load(2)
            stores(0)
            with sp.Fori(3, NB) as b:
                x_load(b)
                stores(b - 2)
            stores(NB - 2)
            stores(NB - 1)
            for s in stored:
                sp.wait_ge(s, 16 * 3 * NB)
            end_phase(sp, 1)

            def unit_load(b, k):
                d, c = unit_of(k)
                at_least(sp, skip_done, num(b, k) - NU + 1)
                sp.dma_start(xc_in[:, k, :], dram_batch(conv_dram, b)[d, :, c * CH:(c + 1) * CH])\
                    .then_inc(xc_ld[k], 16)

            def gate_load(b, k):
                d, c = unit_of(k)
                at_least(sp, gated, num(b, k) - 2)
                sp.dma_start(zs_in[:, k % 3, :], dram_batch(gate_dram, b)[d, :, c * CH:(c + 1) * CH])\
                    .then_inc(zs_ld[k % 3], 16)

            for k in range(3):
                unit_load(0, k)
            for k in range(NU):
                gate_load(0, k)
                unit_load(*at(0, k, 3))
            with sp.Fori(1, NB - 1) as b:
                for k in range(NU):
                    gate_load(b, k)
                    unit_load(*at(b, k, 3))
            for k in range(NU):
                gate_load(NB - 1, k)
                if k < 3:
                    unit_load(NB - 1, k + 3)
            end_phase(sp, 2)

            sp.sem_inc(o3, 1)
            with sp.Fori(0, NB) as b:
                sp.wait_ge(v3, P3_OPS * b + P3_OPS)
                sp.dma_start(dram_b3(out, b).rearrange("(t p) d -> p t d", p=P), y_out)\
                    .then_inc(o3, 16)
            sp.wait_ge(o3, 16 * NB + 1)

        @block.gpsimd
        def _(pool):
            g = nc.gpsimd
            g.memset(ident[:, :], 0.0).then_inc(s_id, 1)
            pool.wait_ge(s_id, 1)
            g.affine_select(out=ident[:, :], in_=ident[:, :], compare_op=ALU.not_equal, fill=1.0,
                            base=0, pattern=[[-1, P]], channel_multiplier=1).then_inc(s_id, 1)
            for b in range(NB):
                pool.dma_start(resid[:, b, NI:NT, :], T["txt"][b].rearrange("(t p) d -> p t d", p=P))\
                    .then_inc(txt_loaded, 16)
            g.memset(b_rep[:, :, :], 0.0)
            g.memset(c_sel[:, :, :, :], 0.0)
            g.memset(ones_row[:, :], 1.0).then_inc(const, 1)
            g.memset(x_pair[:, :], 0.0)
            g.memset(ones_b[:, :], 1.0)
            g.memset(zero_b[:, :], 0.0)
            g.memset(pick[:, :, :], 0.0)
            g.memset(before[:, :], 1.0)
            g.memset(decay[:, 0, 0:P], 0.0).then_inc(const, 1)
            pool.wait_ge(const, 2)
            steps = decay[:, 0, 0:P].rearrange("p (n e) -> p n e", n=NS)
            g.affine_select(out=steps, in_=steps, compare_op=ALU.not_equal, fill=1.0, base=0,
                            pattern=[[-BL, NS], [-1, BL]], channel_multiplier=1).then_inc(const, 1)
            g.affine_select(out=before[:, :], in_=before[:, :], compare_op=ALU.is_gt, fill=0.0,
                            base=0, pattern=[[1, P]], channel_multiplier=-1).then_inc(const, 1)
            for part in range(3):
                g.affine_select(out=pick[:, :, :], in_=pick[:, :, :], compare_op=ALU.not_equal,
                                fill=1.0, base=-32 * part, pattern=[[-1, NS], [0, P]],
                                channel_multiplier=1).then_inc(const, 1)
                pool.wait_ge(const, 5 + part)
            pool.wait_ge(txt_loaded, 16 * NB)
            end_phase(pool, 1)

            def pre(b, k):
                u = num(b, k)
                pool.wait_ge(ln_done, u + 1)
                pool.wait_ge(relu_done, u + 1)
                at_least(pool, decay_ready, NS * (u - 1))
                g.tensor_tensor(delta[:, k % 2, :], relu[:, :], soft[:, :], ALU.add)\
                    .then_inc(delta_ready, 1)
                pool.wait_ge(delta_ready, u + 1)
                pool.wait_ge(xc_ld[k], 16 * (b + 1))
                pool.wait_ge(rest_done, u + 1)
                at_least(pool, drive_done, NS * (u - 1))
                g.tensor_tensor(du[:, k % 2, :], delta[:, k % 2, :], xc_in[:, k, :], ALU.mult)\
                    .then_inc(du_ready, 1)
                g.tensor_tensor(b_high[:, :], b_rest[:, :], part_mask[:, 1:2].to_broadcast([96, CH]),
                                ALU.mult).then_inc(part2, 1)
                pool.wait_ge(part2, u + 1)
                at_least(pool, b_full, NS * (u - 1))
                g.tensor_tensor(b_parts[:, k % 2, :], b_rest[:, :], b_high[:, :], ALU.subtract)\
                    .then_inc(parts_ready, 1)

            def gate(b, k):
                u = num(b, k)
                pool.wait_ge(skip_done, u + 1)
                pool.wait_ge(zs_ld[k % 3], 16 * (2 * b + k // 3 + 1))
                at_least(pool, out_full, u - 1)
                g.tensor_tensor(y_gated[:, k % 2, :], y_skip[:, k % 2, :], zs_in[:, k % 3, :],
                                ALU.mult).then_inc(gated, 1)

            def c_matrix(b, k):
                u = num(b, k)
                pool.wait_ge(c_copied, u + 1)
                at_least(pool, contracted, NG * (u - 1))
                g.tensor_tensor(
                    c_mat[:, k % 2, :, :],
                    c_col[:, k % 2, :].rearrange("p (j o) -> p j o", o=1).to_broadcast([P, NJ, BL]),
                    block_mask[:, :].rearrange("p (o e) -> p o e", o=1).to_broadcast([P, NJ, BL]),
                    ALU.mult).then_inc(c_ready, 1)

            def unit(b, k, back=True, ahead=True):
                if back:
                    gate(*at(b, k, -2))
                c_matrix(b, k)
                if ahead:
                    pre(*at(b, k, 1))

            pre(0, 0)
            for k in range(NU):
                unit(0, k, back=k >= 2)
            with pool.Fori(1, NB - 1) as b:
                for k in range(NU):
                    unit(b, k)
            for k in range(NU):
                unit(NB - 1, k, ahead=k < NU - 1)
            gate(NB - 1, NU - 2)
            gate(NB - 1, NU - 1)
            pool.wait_ge(gated, NU * NB)
            end_phase(pool, 2)

        @block.scalar
        def _(act):
            a = nc.scalar
            act.wait_ge(wl, 16 * WEIGHTS)
            act.wait_ge(masks, 2)
            a.activation(a_neg[:, :, :], a_log[:, :, :], ACT.Exp).then_inc(prep_e, 1)
            act.wait_ge(const, 1)

            def tiles_of(ap, i, odd):
                return ap[0:DM, i * 512:(i + 1) * 512].rearrange("p (t o q) -> p t o q", o=2, q=P)[:, :, odd, :]

            def paired(ps, odd):
                return ps[DM * odd:DM * (odd + 1), 0:2 * P].rearrange("p (t q) -> p t q", q=P)

            def item(i, dst, src, scale=None):
                act.wait_ge(prep_p, i + 1)
                if scale is None:
                    return a.activation(dst, src, ACT.Copy)
                return a.activation(dst, src, ACT.Copy, scale=scale)

            for d in range(2):
                i = 7 * d
                bk = [bank[4 + (i + e) % 4] for e in range(7)]
                for p in range(2):
                    item(i + p, conv_t[:, d, p, :], bk[p][:, 0:P], vecs[:, d, NRM:NRM + 1]).then_inc(prep_a, 1)
                item(i + 2, gate_t[:, d, :], bk[2][0:DM, 0:P], vecs[0:DM, d, NRM:NRM + 1]).then_inc(prep_a, 1)
                for part in range(3):
                    item(i + 3, b_rep[:, d, 32 * part:32 * part + NS], bk[3][:, RK:RK + NS])
                for e in range(BL):
                    last = item(i + 3, c_sel[:, d, e, :].rearrange("p (n e) -> p n e", e=BL)[:, :, e],
                                bk[3][:, RK + NS:RK + 2 * NS])
                last.then_inc(prep_a, 1)
                item(i + 4, dtw_t[:, d, :], bk[4][0:RK, 0:P]).then_inc(prep_a, 1)
                item(i + 5, delta_t[:, d, :], bk[5][:, 0:P]).then_inc(prep_a, 1)
                item(i + 6, out_t[:, d, :], bk[6][:, 0:DM]).then_inc(prep_a, 1)
            item(14, slope[:, :], bank[4 + 14 % 4][:, 0:1]).then_inc(prep_a, 1)
            for t in range(NI):
                act.wait_ge(gamma_turned, 2 * t + 1)
                a.activation(gamma_t[:, 0:4, t * P:(t + 1) * P],
                             bank[2 * t % 4][:, :].rearrange("p (s t) -> p s t", s=4), ACT.Copy)\
                    .then_inc(gamma_a, 1)

            def head(b):
                for k in range(2):
                    act.wait_ge(g_full, g_index(b, k) + 1)
                    for odd in range(2):
                        a.activation(tiles_of(x_t, k, odd), paired(G[k % 3], odd), ACT.Copy)\
                            .then_inc(act_read, 1)
                for k in range(2, 4):
                    c = k - 2
                    act.wait_ge(g_full, g_index(b, k) + 1)
                    a.activation(q_t[:, c * 512:(c + 1) * 512], G[k % 3][0:DM, :], ACT.Copy)\
                        .then_inc(act_read, 1)
                    a.activation(k_t[:, c * 512:(c + 1) * 512], G[k % 3][DM:P, :], ACT.Copy)\
                        .then_inc(act_read, 1)
                act.wait_ge(g_full, g_index(b, 4) + 1)
                a.activation(v_sb, G[4 % 3][:, :].rearrange("p (t d) -> p t d", t=NI), ACT.Copy)\
                    .then_inc(act_read, 1)

            def roots(b):
                act.wait_ge(ln, LN_OPS * b + 8)
                a.activation(stat[:, 4, :], stat[:, 3, :], ACT.Sqrt).then_inc(sq_root, 1)
                act.wait_ge(ln, LN_OPS * b + 12)
                a.activation(stat[:, 8, :], stat[:, 7, :], ACT.Sqrt).then_inc(sq_root, 1)

            def retained(b):
                for h in range(2):
                    act.wait_ge(ret_mm, 2 * NI * b + NI * (h + 1))
                    a.activation(r_t[0:DM, h * 512:(h + 1) * 512], RT[0:DM, :], ACT.Copy)\
                        .then_inc(act_read, 1)

            def tail(b, prev):
                for i in range(3):
                    k = 5 + i
                    act.wait_ge(g_full, g_index(b, k) + 1)
                    a.activation(x_pair[0:DM, 3 + i * 512:3 + (i + 1) * 512], G[k % 3][0:DM, :], ACT.Copy)\
                        .then_inc(act_read, 1)
                    a.activation(x_pair[DM:P, 2 + i * 512:2 + (i + 1) * 512], G[k % 3][DM:P, :], ACT.Copy)\
                        .then_inc(act_read, 1)
                for q in range(12):
                    k, d = 8 + q, q // 6
                    act.wait_ge(g_full, g_index(b, k) + 1)
                    at_least(act, stored[q % 4], 16 * (3 * prev + q // 4))
                    bias = 0.0 if q % 2 else vecs[:, d, CB:CB + 1]
                    a.activation(staged[:, q % 4, :], G[k % 3][:, :], ACT.Silu, bias=bias)\
                        .then_inc(act_read, 1)

            head(0)
            retained(0)
            head(1)
            roots(0)
            retained(1)
            tail(1, 0)
            with act.Fori(2, NB) as b:
                head(b)
                roots(b - 1)
                retained(b)
                tail(b, b - 1)
            roots(NB - 1)
            tail(NB, NB - 1)
            act.wait_ge(act_read, act_value(NB, "s11"))
            end_phase(act, 1)

            def pre(b, k):
                u, d = num(b, k), k // NC
                act.wait_ge(raw_full, u + 1)
                at_least(act, delta_ready, u)
                a.activation(soft[:, :], bank[7][:, :], ACT.Abs, bias=vecs[:, d, DTB:DTB + 1])\
                    .then_inc(abs_done, 1)
                act.wait_ge(abs_done, u + 1)
                a.activation(soft[:, :], soft[:, :], ACT.Exp, scale=-1.0).then_inc(exp_done, 1)
                act.wait_ge(exp_done, u + 1)
                a.activation(soft[:, :], soft[:, :], ACT.Ln, bias=1.0).then_inc(ln_done, 1)

            def part(b, k):
                u = num(b, k)
                act.wait_ge(brep_full, u + 1)
                at_least(act, parts_ready, u)
                a.activation(b_high[:, :], bank[6][0:96, :], ACT.Copy, scale=part_mask[:, 0:1])\
                    .then_inc(part1, 1)

            def unit(b, k, back=True, ahead=True, scans=True):
                u, d = num(b, k), k // NC
                for n in range(NS):
                    i = NS * u + n
                    if scans:
                        if n == 0:
                            act.wait_ge(delta_ready, u + 1)
                        at_least(act, scanned, i - 3)
                        a.activation(decay[:, n % 4, :], delta[:, k % 2, :], ACT.Exp,
                                     scale=a_neg[:, d, n:n + 1]).then_inc(decay_ready, 1)
                    if back:
                        j = i - NS
                        act.wait_ge(turned, j + 1)
                        at_least(act, contracted, j - 3)
                        a.activation(h_t[:, n % 4, :], bank[2 + n % 2][:, :], ACT.Copy)\
                            .then_inc(turn_copied, 1)
                    if scans and n == 3:
                        act.wait_ge(c_full, u + 1)
                        at_least(act, c_ready, u - 1)
                        a.activation(c_col[:, k % 2, :], bank[6][:, 0:NJ], ACT.Copy)\
                            .then_inc(c_copied, 1)
                    if ahead and n == 6:
                        pre(*at(b, k, 1))
                    if ahead and n == 9:
                        part(*at(b, k, 1))

            pre(0, 0)
            part(0, 0)
            for k in range(NU):
                unit(0, k, back=k >= 1)
            with act.Fori(1, NB - 1) as b:
                for k in range(NU):
                    unit(b, k)
            for k in range(NU):
                unit(NB - 1, k, ahead=k < NU - 1)
            unit(NB, 0, ahead=False, scans=False)
            act.wait_ge(turn_copied, NG * NU * NB)
            end_phase(act, 2)

            with act.Fori(0, NB) as b:
                act.wait_ge(v3, P3_OPS * b + 7)
                a.activation(stat[:, 4, :], stat[:, 3, :], ACT.Sqrt).then_inc(root3, 1)
                for i in range(3):
                    act.wait_ge(t3, 3 * b + i + 1)
                    for odd in range(2):
                        a.activation(tiles_of(xl_t, i, odd), paired(bank[i], odd), ACT.Copy)\
                            .then_inc(xt3, 1)
                for i in range(3):
                    act.wait_ge(w3, 3 * b + i + 1)
                    a.activation(w_row[:, i * 512:(i + 1) * 512], bank[3 + i][:, :], ACT.Copy)\
                        .then_inc(wc3, 1)
                for i in range(6):
                    hg, c = i // 3, i % 3
                    act.wait_ge(h3, 6 * b + i + 1)
                    a.activation(hid[:, hg, c * 512:(c + 1) * 512], bank[6 + i % 2][:, :],
                                 ACT.Gelu_apprx_tanh, bias=b_1[:, hg:hg + 1]).then_inc(g3, 1)

        @block.tensor
        def _(pe):
            t_ = nc.tensor

            def mm(o, lhsT, rhs, start=True, stop=True, **kw):
                return t_.matmul(o, lhsT, rhs, start=start, stop=stop, **kw)

            pe.wait_ge(s_id, 2)
            pe.wait_ge(wl, 16 * WEIGHTS)
            pe.wait_ge(const, 1)
            for d in range(2):
                i = 7 * d
                bk = [bank[4 + (i + e) % 4] for e in range(7)]

                def ready(e, i=i):
                    at_least(pe, prep_a, i + e - 3)
                pe.wait_ge(prep_v, 4 * d + 4)
                for p in range(2):
                    ready(p)
                    t_.transpose(bk[p][:, 0:P], tap_w[:, d, 2 * p:2 * p + 2, :].rearrange("p k i -> p (k i)"),
                                 ident[:, :]).then_inc(prep_p, 1)
                ready(2)
                t_.transpose(bk[2][0:DM, 0:P], in_w[:, d, 1, :], ident[:, :]).then_inc(prep_p, 1)
                ready(3)
                nx = RK + 2 * NS
                t_.transpose(bk[3][:, 0:nx], xp_w[:, d, :], ident[0:nx, 0:nx]).then_inc(prep_p, 1)
                ready(4)
                t_.transpose(bk[4][0:RK, 0:P], dt_w[:, d, :], ident[:, :]).then_inc(prep_p, 1)
                pe.wait_ge(prep_a, i + 5)
                mm(bk[5][:, 0:P], xp_w[0:RK, d, :], dtw_t[:, d, :]).then_inc(prep_p, 1)
                ready(6)
                t_.transpose(bk[6][:, 0:DM], op_w[:, d, :], ident[0:DM, 0:DM]).then_inc(prep_p, 1)
            at_least(pe, prep_a, 14 - 3)
            mm(bank[4 + 14 % 4][:, 0:1], ones_row[:, :], slope_in[:, :]).then_inc(prep_p, 1)
            for t in range(NI):
                pe.wait_ge(gamma_ld[t % 2], 16 * (t // 2 + 1))
                for h in range(2):
                    if t >= 2:
                        pe.wait_ge((gamma_a, gamma_v)[h], t - 1)
                    for s in range(4):
                        last = t_.transpose(bank[(2 * t + h) % 4][:, s * P:(s + 1) * P],
                                            gamma_in[:, t % 2, (4 * h + s) * P:(4 * h + s + 1) * P],
                                            ident[:, :])
                    last.then_inc(gamma_turned, 1)
            pe.wait_ge(prep_a, PREP)
            pe.wait_ge(const, 7)
            pe.wait_ge(masks, 2)
            pe.wait_ge(gamma_a, NI)
            pe.wait_ge(gamma_v, NI)

            def head(b):
                pe.wait_ge(x_loaded, 16 * (b + 1))
                for k in range(2):
                    wait_bank(pe, b, k)
                    for i in range(2):
                        t = 4 * k + 2 * i
                        last = t_.transpose(G[k % 3][:, i * P:(i + 1) * P],
                                            x_in[:, t:t + 2, :].rearrange("p t d -> p (t d)"), ident[:, :])
                    last.then_inc(g_full, 1)
                for k in range(2, 4):
                    c = k - 2
                    wait_bank(pe, b, k)
                    pe.wait_ge(act_read, act_value(b, f"x{c}u"))
                    mm(G[k % 3][:, :], w_qk[:, :], x_t[0:DM + 1, c * 512:(c + 1) * 512]).then_inc(g_full, 1)
                wait_bank(pe, b, 4)
                for i in range(NI):
                    last = mm(G[4 % 3][:, i * DM:(i + 1) * DM], x_t[0:DM + 1, i * P:(i + 1) * P], w_v[:, :])
                last.then_inc(g_full, 1)

            def mixer(b):
                pe.wait_ge(act_read, act_value(b, "v"))
                for j in range(2 * NI + 2):
                    if j < 2 * NI:
                        h, s = divmod(j, NI)
                        at_least(pe, mix_done, 2 * NI * b + j - 3)
                        mm(bank[j % 4][:, :], k_t[:, s * P:(s + 1) * P], q_t[:, h * 512:(h + 1) * 512])\
                            .then_inc(sc_full, 1)
                    if j >= 2:
                        i = j - 2
                        h, s = divmod(i, NI)
                        if s == 0:
                            if h:
                                pe.wait_ge(act_read, act_value(b, "r0"))
                            elif not (isinstance(b, int) and b == 0):
                                pe.wait_ge(act_read, act_value(b - 1, "r1"))
                        pe.wait_ge(mix_done, 2 * NI * b + i + 1)
                        mm(RT[0:DM, :], v_sb[:, s, :], mixed[:, i % 4, :], start=s == 0, stop=s == NI - 1)\
                            .then_inc(ret_mm, 1)

            def tail(b, prev):
                pe.wait_ge(ln, LN_OPS * prev + 15)
                for i in range(3):
                    k = 5 + i
                    wait_bank(pe, b, k)
                    for q in range(4):
                        last = t_.transpose(G[k % 3][:, q * P:(q + 1) * P],
                                            x_rms[:, 4 * i + q, :, :].rearrange("p a d -> p (a d)"), ident[:, :])
                    last.then_inc(g_full, 1)
                pe.wait_ge(act_read, act_value(b, "X2u"))
                for q in range(12):
                    k, d, c, z = 8 + q, q // 6, (q % 6) // 2, q % 2
                    wait_bank(pe, b, k)
                    if z:
                        last = mm(G[k % 3][:, :], gate_t[:, d, :], x_pair[0:DM, c * 512 + 3:c * 512 + 515])
                    else:
                        o = c * 512 + (0 if d == 0 else 3)
                        mm(G[k % 3][:, :], conv_t[:, d, 0, :], x_pair[:, o:o + 512], stop=False)
                        last = mm(G[k % 3][:, :], conv_t[:, d, 1, :], x_pair[:, o + 2:o + 514], start=False)
                    last.then_inc(g_full, 1)

            def proj(b):
                k = PROJ[0]
                wait_bank(pe, b, k)
                pe.wait_ge(act_read, act_value(b, "r1"))
                for i in range(NI):
                    last = mm(G[k % 3][:, i * DM:(i + 1) * DM], r_t[0:DM + 1, i * P:(i + 1) * P], w_o[:, :])
                last.then_inc(g_full, 1)

            head(0)
            mixer(0)
            proj(0)
            head(1)
            mixer(1)
            tail(1, 0)
            proj(1)
            with pe.Fori(2, NB) as b:
                head(b)
                mixer(b)
                tail(b, b - 1)
                proj(b)
            tail(NB, NB - 1)
            pe.wait_ge(g_full, g_index(NB, 19) + 1)
            end_phase(pe, 1)

            def delta_mm(b, k):
                u, d = num(b, k), k // NC
                pe.wait_ge(xc_ld[k], 16 * (b + 1))
                at_least(pe, added, u - 3)
                mm(bank[7][:, :], delta_t[:, d, :], xc_in[:, k, :]).then_inc(raw_full, 1)

            def brep_mm(b, k):
                u, d = num(b, k), k // NC
                at_least(pe, c_copied, u)
                mm(bank[6][0:96, :], b_rep[:, d, :], xc_in[:, k, :]).then_inc(brep_full, 1)

            def c_mm(b, k):
                u, d = num(b, k), k // NC
                pe.wait_ge(rest_done, u + 1)
                for e in range(BL):
                    last = mm(bank[6][:, 0:NJ], c_sel[:, d, e, :], xc_in[:, k, e * NJ:(e + 1) * NJ],
                              start=e == 0, stop=e == BL - 1)
                last.then_inc(c_full, 1)

            def out_mm(b, k, later=1):
                u, d = num(b, k), k // NC
                pe.wait_ge(gated, u + 1)
                if later:
                    pe.wait_ge(relu_done, u + 4)
                else:
                    at_least(pe, added, u)
                for i in range(4):
                    last = mm(bank[7][:, i * DM:(i + 1) * DM], y_gated[:, k % 2, i * P:(i + 1) * P], out_t[:, d, :])
                last.then_inc(out_full, 1)

            def turn(b, k, n):
                u = num(b, k)
                i = NG * u + n
                if n == 0:
                    pe.wait_ge(scanned, NS * (u + 1))
                at_least(pe, turn_copied, i - 1)
                for q in range(4):
                    last = t_.transpose(bank[2 + n % 2][:, q * P:(q + 1) * P],
                                        arena[:, k % 2, 4 * n + q:NS * CH:NJ], ident[:, :])
                last.then_inc(turned, 1)

            def contract(b, k, n):
                u = num(b, k)
                i = NG * u + n
                pe.wait_ge(turn_copied, i + 1)
                if n == 0:
                    pe.wait_ge(c_ready, u + 1)
                    at_least(pe, skip_done, u - 1)
                for q in range(4):
                    j = 4 * n + q
                    last = mm(bank[4 + k % 2][:, j:CH:NJ], h_t[:, n % 4, q * P:(q + 1) * P],
                              c_mat[:, k % 2, j, :])
                last.then_inc(contracted, 1)

            def spread(b, k, n):
                u = num(b, k)
                i = NS * u + n
                if n == 0:
                    pe.wait_ge(parts_ready, u + 1)
                at_least(pe, drive_done, i - 1)
                mm(bank[n % 2][:, :], pick[:, n, :], b_parts[:, k % 2, :]).then_inc(b_full, 1)

            def unit(b, k, back=True, back2=True, ahead=True, scans=True, later=True):
                for n in range(NS):
                    if scans:
                        spread(b, k, n)
                    if back:
                        turn(*at(b, k, -1), n)
                    if n == 0 and back2:
                        contract(*at(b, k, -2), NG - 1)
                    if n >= 1 and back:
                        contract(*at(b, k, -1), n - 1)
                    if n == 2 and scans:
                        c_mm(b, k)
                    if n == 5 and ahead:
                        delta_mm(*at(b, k, 1))
                    if n == 8 and ahead:
                        brep_mm(*at(b, k, 1))
                    if n == 11 and back2:
                        out_mm(*at(b, k, -2), later=later)

            delta_mm(0, 0)
            brep_mm(0, 0)
            for k in range(NU):
                unit(0, k, back=k >= 1, back2=k >= 2)
            with pe.Fori(1, NB - 1) as b:
                for k in range(NU):
                    unit(b, k)
            for k in range(NU):
                unit(NB - 1, k, ahead=k < NU - 1, later=k < NU - 1)
            unit(NB, 0, ahead=False, scans=False, later=False)
            contract(NB - 1, NU - 1, NG - 1)
            out_mm(NB - 1, NU - 1, later=False)
            pe.wait_ge(out_full, NU * NB)
            end_phase(pe, 2)

            pe.wait_ge(masks, 3)
            with pe.Fori(0, NB) as b:
                pe.wait_ge(v3, P3_OPS * b + 9)
                for i in range(3):
                    for q in range(2):
                        t = 4 * i + 2 * q
                        last = t_.transpose(bank[i][:, q * P:(q + 1) * P],
                                            xl[:, t:t + 2, :].rearrange("p t d -> p (t d)"), ident[:, :])
                    last.then_inc(t3, 1)
                for i in range(3):
                    pe.wait_ge(xt3, 6 * b + 2 * i + 2)
                    mm(bank[3 + i][:, :], w_rr[:, :], xl_t[0:DM + 1, i * 512:(i + 1) * 512]).then_inc(w3, 1)
                for i in range(6):
                    hg, c = i // 3, i % 3
                    if i >= 2:
                        pe.wait_ge(g3, 6 * b + i - 1)
                    mm(bank[6 + i % 2][:, :], w_1[:, hg * P:(hg + 1) * P], xl_t[0:DM, c * 512:(c + 1) * 512])\
                        .then_inc(h3, 1)
                pe.wait_ge(g3, 6 * b + 6)
                for t in range(NT):
                    o = bank[t // 8][:, (t % 8) * DM:(t % 8 + 1) * DM]
                    mm(o, ones_row[:, :], b_2[:, :], stop=False)
                    mm(o, hid[:, 0, t * P:(t + 1) * P], w_2[:, 0, :], start=False, stop=False)
                    last = mm(o, hid[:, 1, t * P:(t + 1) * P], w_2[:, 1, :], start=False)
                last.then_inc(y3, 1)
                mm(bank[2][:, 0:NT], ones_b[:, :], zero_b[:, :], stop=False, skip_group_check=True)
                for j in range(NT):
                    pe.wait_ge(v3, P3_OPS * b + 11 + (0 if j == 0 else 4 * j - 1) + (3 if j in (0, NT - 1) else 4))
                    for t in range(NT):
                        last = mm(bank[2][:, t:t + 1], higher_of(j)[:, t * P:(t + 1) * P], ones_b[:, 0:1],
                                  start=False, stop=j == NT - 1, skip_group_check=True)
                last.then_inc(rk3, 1)

        @block.vector
        def _(dve):
            v = nc.vector
            v.memset(x_t[DM:DM + 1, :], 1.0)
            v.memset(r_t[DM:DM + 1, :], 1.0)
            v.memset(part_mask[0:96, 0:1], 1.0)
            v.memset(part_mask[0:96, 1:2], 0.0).then_inc(masks, 1)
            dve.wait_ge(masks, 1)
            v.memset(part_mask[0:32, 0:1], 0.0)
            v.memset(part_mask[64:96, 1:2], 1.0).then_inc(masks, 1)
            dve.wait_ge(wl, 16 * WEIGHTS)
            for d in range(2):
                for j in range(4):
                    tap = j if d == 0 else 3 - j
                    v.tensor_scalar(tap_w[:, d, j, :], in_w[:, d, 0, :], conv_w[:, d, tap:tap + 1], None,
                                    ALU.mult).then_inc(prep_v, 1)
            dve.wait_ge(const, 3)
            v.tensor_reduce(block_mask[:, :], decay[:, 0, 0:P].rearrange("p (n e) -> p e n", n=NS),
                            AX_X, ALU.add).then_inc(prep_v, 1)
            v.tensor_copy(w_rr[:, :], w_r[:, 0:1].to_broadcast([DM + 1, P])).then_inc(prep_v, 1)
            dve.wait_ge(prep_e, 1)
            v.tensor_scalar(a_neg[:, :, :], a_neg[:, :, :], -1.0, None, ALU.mult).then_inc(prep_v, 1)
            dve.wait_ge(prep_a, PREP)
            for t in range(NI):
                dve.wait_ge(gamma_turned, 2 * t + 2)
                v.tensor_copy(gamma_t[:, 4:8, t * P:(t + 1) * P],
                              bank[(2 * t + 1) % 4][:, :].rearrange("p (s t) -> p s t", s=4))\
                    .then_inc(gamma_v, 1)
            dve.wait_ge(gamma_a, NI)
            dve.wait_ge(txt_loaded, 16 * NB)

            def over(ap, n=DM):
                return ap.rearrange("p (t o) -> p t o", o=1).to_broadcast([P, NT, n])

            def prelu(b):
                dve.wait_ge(g_full, g_index(b, PROJ[0]) + 1)
                y = G[PROJ[0] % 3]
                v.tensor_scalar(neg_part[:, :], y[:, :], 0.0, slope[:, 0:1], ALU.min, ALU.mult).then_inc(neg_done, 1)
                dve.wait_ge(neg_done, b + 1)
                dst = tok(b)[:, 0:NI, :]
                v.scalar_tensor_tensor(dst, y[:, :].rearrange("p (t d) -> p t d", t=NI), 0.0,
                                       neg_part[:, :].rearrange("p (t d) -> p t d", t=NI), ALU.max, ALU.add)\
                    .then_inc(prelu_done, 1)

            S1, MEAN, VAR, VE, SD, RSTD, RR, ME, SD2, R2 = range(10)

            def st(i):
                return stat[:, i, :]

            def norm_step(b, i):
                if i == -1:
                    dve.wait_ge(prelu_done, b + 1)
                else:
                    dve.wait_ge(ln, LN_OPS * b + i + 1)
                x = tok(b)
                if i == -1:
                    ins = v.tensor_scalar(x_mid, x, 1.0, None, ALU.mult)
                elif i == 0:
                    ins = v.tensor_reduce(st(S1), x_mid, AX_X, ALU.add)
                elif i == 1:
                    ins = v.tensor_scalar(st(MEAN), st(S1), 1.0 / DM, None, ALU.mult)
                elif i == 2:
                    ins = v.tensor_tensor(x_mid, x, over(st(MEAN)), ALU.subtract)
                elif i == 3:
                    ins = v.tensor_tensor(x_sq, x_mid, x_mid, ALU.mult)
                elif i == 4:
                    ins = v.tensor_reduce(st(S1), x_sq, AX_X, ALU.add)
                elif i == 5:
                    ins = v.tensor_scalar(st(VAR), st(S1), 1.0 / DM, None, ALU.mult)
                elif i == 6:
                    ins = v.tensor_scalar(st(VE), st(VAR), EPS, None, ALU.add)
                elif i == 7:
                    dve.wait_ge(sq_root, 2 * b + 1)
                    ins = v.reciprocal(st(RSTD), st(SD))
                elif i == 8:
                    ins = v.tensor_tensor(st(RR), st(RSTD), st(RSTD), ALU.mult)
                elif i == 9:
                    ins = v.tensor_tensor(st(RR), st(RR), st(VAR), ALU.mult)
                elif i == 10:
                    ins = v.tensor_scalar(st(ME), st(RR), EPS, None, ALU.add)
                elif i == 11:
                    dve.wait_ge(sq_root, 2 * b + 2)
                    ins = v.reciprocal(st(R2), st(SD2))
                elif i == 12:
                    ins = v.tensor_tensor(x_sq, x_mid, over(st(RSTD)), ALU.mult)
                elif i == 13:
                    for half in range(2):
                        ins = v.tensor_tensor(x_rms[:, :, half, :], x_sq, over(st(R2)), ALU.mult)
                else:
                    ins = v.scalar_tensor_tensor(x, x_sq, 2.0, x, ALU.mult, ALU.add)
                ins.then_inc(ln, 1)

            NORM_AT = {0: [-1, 0], 1: [1, 2], 2: [3], 3: [4], 4: [5, 6], 5: [7, 8, 9, 10], 7: [11, 12], 9: [13], 11: [14]}

            def mixer(b, prev=None):
                for j in range(2 * NI):
                    h, s = divmod(j, NI)
                    dve.wait_ge(sc_full, 2 * NI * b + j + 1)
                    at_least(dve, ret_mm, 2 * NI * b + j - 3)
                    v.tensor_tensor(mixed[:, j % 4, :], gamma_t[:, s, h * 512:(h + 1) * 512], bank[j % 4][:, :],
                                    ALU.mult).then_inc(mix_done, 1)
                    if prev is not None:
                        for i in NORM_AT.get(j, []):
                            norm_step(prev, i)

            mixer(0)
            prelu(0)
            mixer(1, 0)
            with dve.Fori(2, NB) as b:
                prelu(b - 1)
                mixer(b, b - 1)
            prelu(NB - 1)
            for i in range(-1, LN_OPS - 1):
                norm_step(NB - 1, i)
            dve.wait_ge(ln, LN_OPS * NB)
            end_phase(dve, 1)

            def pre(b, k):
                u, d = num(b, k), k // NC
                dve.wait_ge(abs_done, u + 1)
                at_least(dve, delta_ready, u)
                v.tensor_scalar(relu[:, :], bank[7][:, :], vecs[:, d, DTB:DTB + 1], 0.0, ALU.add, ALU.max)\
                    .then_inc(relu_done, 1)

            def rest(b, k):
                u = num(b, k)
                dve.wait_ge(part1, u + 1)
                at_least(dve, parts_ready, u)
                v.tensor_tensor(b_rest[:, :], bank[6][0:96, :], b_high[:, :], ALU.subtract)\
                    .then_inc(rest_done, 1)

            def product(b, k, n):
                u = num(b, k)
                if n == 0:
                    dve.wait_ge(du_ready, u + 1)
                dve.wait_ge(b_full, NS * u + n + 1)
                v.tensor_tensor(drive[:, n % 4, :], du[:, k % 2, :], bank[n % 2][:, :], ALU.mult)\
                    .then_inc(drive_done, 1)

            def scan(b, k, n):
                u = num(b, k)
                i = NS * u + n
                if n == 0:
                    at_least(dve, turned, NG * (u - 1))
                dve.wait_ge(decay_ready, i + 1)
                dve.wait_ge(drive_done, i + 1)
                h = arena[:, k % 2, :].rearrange("p (n t) -> p n t", n=NS)
                h_before = arena[:, (k + 1) % 2, :].rearrange("p (n t) -> p n t", n=NS)
                if k < NC:
                    o, x0, x1, edge = h[:, n, :], decay[:, n % 4, :], drive[:, n % 4, :], h_before[:, n, CH - 1:CH]
                else:
                    o, x0, x1 = h[:, n, ::-1], decay[:, n % 4, ::-1], drive[:, n % 4, ::-1]
                    edge = h_before[:, n, 0:1]
                v.tensor_tensor_scan(o, x0, x1, 0.0 if k % NC == 0 else edge, ALU.mult, ALU.add)\
                    .then_inc(scanned, 1)

            def skip(b, k):
                u, d = num(b, k), k // NC
                dve.wait_ge(contracted, NG * (u + 1))
                at_least(dve, gated, u - 1)
                v.scalar_tensor_tensor(y_skip[:, k % 2, :], xc_in[:, k, :], vecs[:, d, DSK:DSK + 1],
                                       bank[4 + k % 2][:, :], ALU.mult, ALU.add).then_inc(skip_done, 1)

            def add_out(b, k):
                u = num(b, k)
                d, c = unit_of(k)
                dve.wait_ge(out_full, u + 1)
                x = tok(b)[:, 4 * c:4 * c + 4, :]
                v.tensor_tensor(x, x, bank[7][:, 0:4 * DM].rearrange("p (t d) -> p t d", t=4), ALU.add)\
                    .then_inc(added, 1)

            def unit(b, k, back=True, back2=True, ahead=True, scans=True):
                for n in range(NS):
                    if scans:
                        product(b, k, n)
                    if n >= 1 and scans:
                        scan(b, k, n - 1)
                    if n == 0 and back:
                        scan(*at(b, k, -1), NS - 1)
                    if n == 2 and back2:
                        skip(*at(b, k, -2))
                    if n == 7 and ahead:
                        pre(*at(b, k, 1))
                    if n == 10 and ahead:
                        rest(*at(b, k, 1))
                    if n == 13 and back2:
                        add_out(*at(b, k, -2))

            pre(0, 0)
            rest(0, 0)
            for k in range(NU):
                unit(0, k, back=k >= 1, back2=k >= 2)
            with dve.Fori(1, NB - 1) as b:
                for k in range(NU):
                    unit(b, k)
            for k in range(NU):
                unit(NB - 1, k, ahead=k < NU - 1)
            unit(NB, 0, ahead=False, scans=False)
            skip(NB - 1, NU - 1)
            add_out(NB - 1, NU - 1)
            dve.wait_ge(added, NU * NB)
            end_phase(dve, 2)

            v.memset(xl_t[DM:DM + 1, :], 1.0).then_inc(masks, 1)
            with dve.Fori(0, NB) as b:
                step = [0]

                def then(ins, hold=True):
                    step[0] += 1
                    ins.then_inc(v3, 1)
                    if hold:
                        dve.wait_ge(v3, P3_OPS * b + step[0])

                x = tok(b)
                then(v.tensor_scalar(xl, x, 1.0, None, ALU.mult))
                then(v.tensor_reduce(st(S1), xl, AX_X, ALU.add))
                then(v.tensor_scalar(st(MEAN), st(S1), 1.0 / DM, None, ALU.mult))
                then(v.tensor_tensor(xl, x, over(st(MEAN)), ALU.subtract))
                then(v.tensor_tensor(sq3, xl, xl, ALU.mult))
                then(v.tensor_reduce(st(S1), sq3, AX_X, ALU.add))
                then(v.tensor_scalar(st(VE), st(S1), 1.0 / DM, EPS, ALU.mult, ALU.add))
                dve.wait_ge(root3, b + 1)
                then(v.reciprocal(st(RSTD), st(SD)))
                then(v.tensor_tensor(xl, xl, over(st(RSTD)), ALU.mult))
                dve.wait_ge(wc3, 3 * b + 3)
                then(v.tensor_tensor(w_diag.rearrange("p (t q) -> p t q", t=NT),
                                     w_row.rearrange("p (t q) -> p t q", t=NT),
                                     ident[:, :].rearrange("p (o q) -> p o q", o=1).to_broadcast([P, NT, P]),
                                     ALU.mult))
                then(v.tensor_reduce(st(MEAN), w_diag.rearrange("p (t q) -> p t q", t=NT), AX_X, ALU.add))
                for j in range(NT):
                    hi, w = higher_of(j), stat[:, MEAN, j:j + 1]
                    lo, up = j * P, (j + 1) * P
                    if j:
                        then(v.tensor_scalar(hi[:, 0:lo], w_row[:, 0:lo], w, None, ALU.is_lt), False)
                    if j < NT - 1:
                        then(v.tensor_scalar(hi[:, up:L], w_row[:, up:L], w, None, ALU.is_le), False)
                    then(v.scalar_tensor_tensor(w_eq[:, j % 2, :], w_row[:, lo:up], w, before[:, :],
                                                ALU.is_equal, ALU.mult))
                    then(v.scalar_tensor_tensor(hi[:, lo:up], w_row[:, lo:up], w, w_eq[:, j % 2, :],
                                                ALU.is_lt, ALU.add), False)
                dve.wait_ge(rk3, b + 1)
                then(v.scalar_tensor_tensor(st(R2), bank[2][:, 0:NT], float(KK), st(MEAN), ALU.is_lt, ALU.mult))
                dve.wait_ge(y3, b + 1)
                dve.wait_ge(o3, 16 * b + 1)
                for lo, up in ((0, 8), (8, NT)):
                    then(v.tensor_tensor(y_out[:, lo:up, :],
                                         bank[lo // 8][:, 0:(up - lo) * DM].rearrange("p (t d) -> p t d", d=DM),
                                         stat[:, R2, lo:up].rearrange("p (t o) -> p t o", o=1)
                                         .to_broadcast([P, up - lo, DM]), ALU.mult))
                then(v.tensor_tensor(y_out, y_out, xl, ALU.add))
                then(v.tensor_tensor(y_out, y_out, x, ALU.add))
                assert step[0] == P3_OPS


INPUTS = ["x", "txt", "L0_tok_d_gamma_batched"] + [f"L0_tok_{n}" for n in
    ("Wq", "bq", "Wk", "bk", "Wv", "bv", "Wo", "bo", "prelu_a")] + [
    f"L0_attn_{d}_{n}" for d in ("fw", "bw") for n in
    ("norm", "in_proj", "conv_w", "conv_b", "x_proj", "dt_w", "dt_b", "A_log", "D", "out_proj")] + [
    f"L0_ffn_{n}" for n in ("wr", "br", "w1", "b1", "w2", "b2")]


def kernel(**inputs):
    import numpy as np
    import concourse.bacc as bacc
    from concourse.bass_utils import run_bass_kernel_spmd

    nc = bacc.Bacc("TRN2", target_bir_lowering=False, num_devices=1)
    arrays, handles = {}, {}
    for name in INPUTS:
        a = np.ascontiguousarray(inputs[name])
        if a.ndim == 0:
            a = a.reshape(1, 1)
        arrays[f"in_{name}"] = a
        handles[name] = nc.dram_tensor(f"in_{name}", a.shape, mybir.dt.from_np(a.dtype), kind="ExternalInput").ap()
    out = nc.dram_tensor("out", (NB, L, DM), F32, kind="ExternalOutput").ap()
    build(nc, handles, out)
    return run_bass_kernel_spmd(nc, [arrays], core_ids=[0]).results[0]["out"]
```

```python
from contextlib import ExitStack

import concourse.bass as bass
import concourse.mybir as mybir
from concourse.alu_op_type import AluOpType as ALU

F32 = mybir.dt.float32
BF16 = mybir.dt.bfloat16
ACT = mybir.ActivationFunctionType
AX_X = mybir.AxisListType.X

P = 128
NB = 8
DM = 64
TI = 1024
TX = 512
L = TI + TX
NT = L // P
NI = TI // P
DI = 128
NS = 16
RK = 4
CH = 512
NC = L // CH
NU = 2 * NC
LAG = 4
VC = (8,)
PC = [n for n in range(NS) if n not in VC]
HID = 4 * DM
KK = L // 2 - 1
EPS = 1e-5

HEAD, TAIL, PROJ = list(range(5)), list(range(5, 20)), [20]
ACT_HEAD = ["x0", "x0u", "x1", "x1u", "q0", "k0", "q1", "k1", "v", "r0", "r1"]
ACT_TAIL = [f"X{i}{h}" for i in range(3) for h in "lu"] + [f"s{i}" for i in range(12)]
LAST_READ = {0: "x0u", 1: "x1u", 2: "k0", 3: "k1", 4: "v", **{5 + i: f"X{i}u" for i in range(3)},
             **{8 + i: f"s{i}" for i in range(12)}}
LN_OPS = 16
RANK_OPS = 4 * NT - 2
P3_OPS = 11 + RANK_OPS + 5
PREP = 15


def at_least(eng, sem, value):
    if isinstance(value, int) and value <= 0:
        return
    eng.wait_ge(sem, value)


def uses(where):
    return {"first": HEAD + PROJ, "mid": HEAD + TAIL + PROJ, "after": TAIL}[where]


def where_is(b):
    return {0: "first", NB: "after"}.get(b, "mid") if isinstance(b, int) else "mid"


def g_index(b, k):
    w = where_is(b)
    before = 0 if w == "first" else len(uses("first")) + len(uses("mid")) * (b - 1)
    return before + uses(w).index(k)


def act_value(b, name):
    w = where_is(b)
    if w == "first":
        return ACT_HEAD.index(name) + 1
    base = len(ACT_HEAD) + (len(ACT_HEAD) + len(ACT_TAIL)) * (b - 1)
    names = ACT_TAIL if w == "after" else ACT_HEAD + ACT_TAIL
    return base + names.index(name) + 1


def unit_of(k):
    d, c = divmod(k % NU, NC)
    return d, (c if d == 0 else NC - 1 - c)


def build(nc, T, out):
    with ExitStack() as ctx:
        def sb(name, shape, dt=F32):
            return ctx.enter_context(nc.sbuf_tensor(name, shape, dt))

        def sem(name):
            return ctx.enter_context(nc.semaphore(name))

        bank = [ctx.enter_context(nc.psum_tensor(f"bank{i}", [P, 512], F32)) for i in range(8)]
        conv_dram = nc.dram_tensor("conv_scratch", (NB, 2, DI, L), F32, kind="Internal").ap()
        gate_dram = nc.dram_tensor("gate_scratch", (NB, 2, DI, L), F32, kind="Internal").ap()

        resid = sb("resid", [P, NB, NT, DM])
        ident = sb("ident", [P, P])
        arena = sb("arena", [P, 2, NS * CH])
        w_qk = sb("w_qk", [DM + 1, 2 * DM])
        w_v = sb("w_v", [DM + 1, DM])
        w_o = sb("w_o", [DM + 1, DM])
        slope = sb("slope", [P, 1])
        ones_row = sb("ones_row", [1, P])
        conv_t = sb("conv_t", [P, 2, 2, DI])
        gate_t = sb("gate_t", [DM, 2, DI])
        bc_rep = sb("bc_rep", [DI, 2, 96])
        delta_t = sb("delta_t", [DI, 2, DI])
        out_t = sb("out_t", [DI, 2, DM])
        a_neg = sb("a_neg", [DI, 2, NS])
        vecs = sb("vecs", [P, 2, 8])
        CB, DTB, DSK, NRM, CW = range(5)
        pick = sb("pick", [96, 2 * NS, P], BF16)
        w_1 = sb("w_1", [DM, HID])
        b_1 = sb("b_1", [P, 2])
        w_2 = sb("w_2", [P, 2, DM])
        b_2 = sb("b_2", [1, DM])
        w_r = sb("w_r", [DM + 1, 1])
        w_rr = sb("w_rr", [DM + 1, P])
        before = sb("before", [P, P])
        ones_b = sb("ones_b", [P, P], BF16)
        xc_in = sb("xc_in", [P, NU, CH])
        zs_in = sb("zs_in", [P, 3, CH])
        delta = sb("delta", [P, 2, CH])
        du = sb("du", [P, 2, CH])
        soft = sb("soft", [P, CH])
        relu = sb("relu", [P, CH])
        parts = sb("parts", [96, 2, CH], BF16)
        rest = sb("rest", [96, CH])
        high = sb("high", [96, CH], BF16)
        part_mask = sb("part_mask", [96, 2])
        decay = sb("decay", [P, 4, CH])
        drive = sb("drive", [P, 4, CH])
        c_all = sb("c_all", [P, 4, CH])
        y_part = sb("y_part", [P, 4, CH])
        y_skip = sb("y_skip", [P, 2, CH])
        y_gated = sb("y_gated", [P, 2, CH])
        gamma_t = arena[:, 0, :].rearrange("p (s t) -> p s t", s=NI)
        A1 = arena[:, 1, :]
        x_t = A1[:, 0:1024]
        q_t = A1[0:DM, 1024:2048]
        k_t = A1[0:DM, 2048:3072]
        v_sb = A1[:, 3072:3584].rearrange("p (t d) -> p t d", t=NI)
        mixed = A1[:, 3584:5632].rearrange("p (r t) -> p r t", r=4)
        r_t = A1[:, 5632:6656]
        x_in = A1[:, 6656:7168].rearrange("p (t d) -> p t d", t=NI)
        staged = decay
        drive_flat = drive[:, :, :].rearrange("p r t -> p (r t)")
        gamma_in = drive_flat.rearrange("p (r t) -> p r t", r=2)
        x_mid = drive_flat[:, 0:768].rearrange("p (t d) -> p t d", t=NT)
        x_sq = drive_flat[:, 768:1536].rearrange("p (t d) -> p t d", t=NT)
        x_rms = y_part[:, :, :].rearrange("p r t -> p (r t)")[:, 0:NT * 2 * DM].rearrange(
            "p (t a d) -> p t a d", t=NT, a=2)
        x_pair = sb("x_pair", [P, L + 8])
        zero_b = sb("zero_b", [P, NT], BF16)
        stat = sb("stat", [P, 10, NT])
        neg_part = sb("neg_part", [P, NI * DM])
        in_w = sb("in_w", [P, 2, 2, DM])
        tap_w = sb("tap_w", [P, 2, 4, DM])
        xp_w = sb("xp_w", [RK + 2 * NS, 2, DI])
        dt_w = sb("dt_w", [DI, 2, RK])
        dtw_t = sb("dtw_t", [RK, 2, DI])
        op_w = sb("op_w", [DM, 2, DI])
        a_log = sb("a_log", [DI, 2, NS])
        conv_w = sb("conv_w", [P, 2, 4])
        slope_in = sb("slope_in", [1, 1])
        A0 = arena[:, 0, :]
        xl = A0[:, 0:768].rearrange("p (t d) -> p t d", t=NT)
        sq3 = A0[:, 768:1536].rearrange("p (t d) -> p t d", t=NT)
        xl_t = A0[:, 1536:3072]
        w_row = A0[:, 3072:4608]
        w_diag = A0[:, 4608:6144]
        y_out = A0[:, 6144:6912].rearrange("p (t d) -> p t d", t=NT)
        hid = xc_in[:, :, :].rearrange("p r t -> p (r t)").rearrange("p (g t) -> p g t", g=2)
        w_eq = sb("w_eq", [P, 2, P])
        A1b = arena[:, 1, :].bitcast(BF16)
        higher_a = A1b[:, 0:10 * L].rearrange("p (j t) -> p j t", j=10)
        higher_b = decay[:, :, :].rearrange("p r t -> p (r t)").bitcast(BF16)[:, 0:2 * L].rearrange(
            "p (j t) -> p j t", j=2)

        def higher_of(j):
            return higher_a[:, j, :] if j < 10 else higher_b[:, j - 10, :]

        wl = sem("weights_loaded")
        s_id = sem("ident_ready")
        const = sem("constants_ready")
        prep_v = sem("prep_vector")
        prep_a = sem("prep_scalar")
        prep_p = sem("prep_tensor")
        prep_e = sem("prep_exp")
        masks = sem("masks_ready")
        gamma_ld = [sem(f"gamma_loaded{i}") for i in range(2)]
        x_loaded = sem("x_loaded")
        txt_loaded = sem("txt_loaded")
        g_full = sem("generic_bank_full")
        act_read = sem("act_read")
        sc_full = sem("scores_full")
        mix_done = sem("mixed_ready")
        ret_mm = sem("retained_added")
        prelu_done = sem("prelu_done")
        ln = sem("norm_step")
        sq_root = sem("square_root")
        neg_done = sem("prelu_negative_part")
        gamma_turned = sem("gamma_turned")
        gamma_a = sem("gamma_copied_scalar")
        gamma_v = sem("gamma_copied_vector")
        stored = [sem(f"stored{i}") for i in range(4)]
        phase_end = sem("phase_end")
        xc_ld = [sem(f"xc_loaded{i}") for i in range(NU)]
        zs_ld = [sem(f"zs_loaded{i}") for i in range(3)]
        raw_full = sem("raw_delta_full")
        abs_done = sem("abs_done")
        exp_done = sem("softplus_exp_done")
        ln_done = sem("softplus_ln_done")
        relu_done = sem("relu_done")
        delta_ready = sem("delta_ready")
        du_ready = sem("du_ready")
        rep_full = sem("bc_rep_full")
        part1 = sem("first_part")
        rest_done = sem("rest")
        part2 = sem("second_part")
        parts_ready = sem("parts_ready")
        c_full = sem("c_broadcast")
        c_copied = sem("c_copied")
        b_full = sem("b_broadcast")
        decay_ready = sem("decay_ready")
        drive_done = sem("drive_done")
        scanned = sem("scanned")
        part_pool = sem("c_product_gpsimd")
        part_vec = sem("c_product_vector")
        summed = sem("state_summed")
        skip_done = sem("skip_added")
        gated = sem("gated")
        out_full = sem("out_full")
        added = sem("added")
        v3 = sem("vector_step3")
        root3 = sem("root3")
        t3 = sem("turned3")
        xt3 = sem("xl_turned_copied")
        w3 = sem("router_full")
        wc3 = sem("router_copied")
        h3 = sem("hidden_full")
        g3 = sem("gelu_done")
        y3 = sem("ffn_full")
        rk3 = sem("rank_full")
        o3 = sem("out_stored")

        block = ctx.enter_context(nc.Block())

        def tok(b):
            if isinstance(b, int):
                return resid[:, b, :, :]
            return resid[:, bass.ds(b, 1), :, :].rearrange("p o t d -> p (o t) d")

        def dram_batch(ap, b):
            if isinstance(b, int):
                return ap[b]
            return ap[bass.ds(b, 1)].rearrange("o a p t -> (o a) p t")

        def dram_b3(ap, b):
            if isinstance(b, int):
                return ap[b]
            return ap[bass.ds(b, 1)].rearrange("o t d -> (o t) d")

        def end_phase(eng, n):
            eng.sem_inc(phase_end, 1)
            eng.wait_ge(phase_end, 5 * n)

        G = bank[5:8]
        RT = bank[4]

        def wait_bank(eng, b, k):
            w = where_is(b)
            earlier = [j for j in uses(w) if j < k and j % 3 == k % 3]
            if earlier:
                bb, j = b, earlier[-1]
            elif w == "first":
                return
            else:
                bb = b - 1
                ww = "first" if (w == "mid" and isinstance(b, int) and b == 1) else "mid"
                j = [i for i in uses(ww) if i % 3 == k % 3][-1]
            if j == PROJ[0]:
                at_least(eng, prelu_done, bb + 1)
            else:
                at_least(eng, act_read, act_value(bb, LAST_READ[j]))

        PRE = ("fw", "bw")
        WEIGHTS = 38

        def at(b, k, step):
            return b + (k + step) // NU, (k + step) % NU

        def num(b, k):
            return NU * b + k

        def products(b, k, n, states):
            return len(states) * num(b, k) + len([m for m in states if m <= n])

        def earlier_state(b, k, n, back):
            m = n - back
            return (*at(b, k, m // NS), m % NS)

        def wait_products(eng, b, k, n):
            if n in VC:
                at_least(eng, part_vec, products(b, k, n, VC))
            else:
                at_least(eng, part_pool, products(b, k, n, PC))

        def free_c_slot(eng, b, k, n):
            at_least(eng, part_pool, products(*earlier_state(b, k, n, 4), PC))

        @block.sync
        def _(sp):
            jobs = [
                (w_qk[0:DM, 0:DM], T["L0_tok_Wq"]), (w_qk[0:DM, DM:2 * DM], T["L0_tok_Wk"]),
                (w_qk[DM:DM + 1, 0:DM], T["L0_tok_bq"].rearrange("(a d) -> a d", a=1)),
                (w_qk[DM:DM + 1, DM:2 * DM], T["L0_tok_bk"].rearrange("(a d) -> a d", a=1)),
                (w_v[0:DM, :], T["L0_tok_Wv"]),
                (w_v[DM:DM + 1, :], T["L0_tok_bv"].rearrange("(a d) -> a d", a=1)),
                (w_o[0:DM, :], T["L0_tok_Wo"]),
                (w_o[DM:DM + 1, :], T["L0_tok_bo"].rearrange("(a d) -> a d", a=1)),
                (slope_in[:, :], T["L0_tok_prelu_a"]),
                (w_1[:, :], T["L0_ffn_w1"]),
                (b_1[:, 0:1], T["L0_ffn_b1"][0:P].rearrange("(p a) -> p a", a=1)),
                (b_1[:, 1:2], T["L0_ffn_b1"][P:HID].rearrange("(p a) -> p a", a=1)),
                (w_2[:, :, :], T["L0_ffn_w2"].rearrange("(g p) d -> p g d", p=P)),
                (b_2[:, :], T["L0_ffn_b2"].rearrange("(a d) -> a d", a=1)),
                (w_r[0:DM, :], T["L0_ffn_wr"]),
                (w_r[DM:DM + 1, :], T["L0_ffn_br"].rearrange("(a d) -> a d", a=1)),
            ]
            for d, pre in enumerate(PRE):
                def t(name):
                    return T[f"L0_attn_{pre}_{name}"]

                def col(ap):
                    return ap.rearrange("(p a) -> p a", a=1)

                jobs += [
                    (in_w[:, d, :, :], t("in_proj").rearrange("(h p) i -> p h i", p=DI)),
                    (conv_w[:, d, :], t("conv_w")),
                    (vecs[:, d, CB:CB + 1], col(t("conv_b"))),
                    (vecs[:, d, DTB:DTB + 1], col(t("dt_b"))),
                    (vecs[:, d, DSK:DSK + 1], col(t("D"))),
                    (vecs[0:DM, d, NRM:NRM + 1], col(t("norm"))),
                    (vecs[DM:P, d, NRM:NRM + 1], col(t("norm"))),
                    (a_log[:, d, :], t("A_log")),
                    (xp_w[:, d, :], t("x_proj")),
                    (dt_w[:, d, :], t("dt_w")),
                    (op_w[:, d, :], t("out_proj")),
                ]
            for dst, src in jobs:
                sp.dma_start(dst, src).then_inc(wl, 16)
            assert len(jobs) == WEIGHTS
            for t in range(NI):
                if t >= 2:
                    sp.wait_ge(gamma_turned, 2 * (t - 1))
                sp.dma_start(gamma_in[:, t % 2, :], T["L0_tok_d_gamma_batched"][t * P:(t + 1) * P, :])\
                    .then_inc(gamma_ld[t % 2], 16)

            def x_load(b):
                src = T["x"][b, 0] if isinstance(b, int) else \
                    T["x"][bass.ds(b, 1)].rearrange("o a t d -> (o a t) d")
                if not (isinstance(b, int) and b == 0):
                    sp.wait_ge(g_full, g_index(b - 1, 1) + 1)
                sp.dma_start(x_in, src.rearrange("(t p) d -> p t d", p=P)).then_inc(x_loaded, 16)

            def stores(b):
                for q in range(12):
                    d, c, z = q // 6, (q % 6) // 2, q % 2
                    sp.wait_ge(act_read, act_value(b + 1, f"s{q}"))
                    dst = dram_batch(gate_dram if z else conv_dram, b)[d, :, c * CH:(c + 1) * CH]
                    sp.dma_start(dst, staged[:, q % 4, :]).then_inc(stored[q % 4], 16)

            x_load(0)
            x_load(1)
            x_load(2)
            stores(0)
            with sp.Fori(3, NB) as b:
                x_load(b)
                stores(b - 2)
            stores(NB - 2)
            stores(NB - 1)
            for s in stored:
                sp.wait_ge(s, 16 * 3 * NB)
            end_phase(sp, 1)

            def unit_load(b, k):
                d, c = unit_of(k)
                at_least(sp, skip_done, num(b, k) - NU + 1)
                sp.dma_start(xc_in[:, k, :], dram_batch(conv_dram, b)[d, :, c * CH:(c + 1) * CH])\
                    .then_inc(xc_ld[k], 16)

            def gate_load(b, k):
                d, c = unit_of(k)
                at_least(sp, gated, num(b, k) - 2)
                sp.dma_start(zs_in[:, k % 3, :], dram_batch(gate_dram, b)[d, :, c * CH:(c + 1) * CH])\
                    .then_inc(zs_ld[k % 3], 16)

            for k in range(3):
                unit_load(0, k)
            for k in range(NU):
                gate_load(0, k)
                unit_load(*at(0, k, 3))
            with sp.Fori(1, NB - 1) as b:
                for k in range(NU):
                    gate_load(b, k)
                    unit_load(*at(b, k, 3))
            for k in range(NU):
                gate_load(NB - 1, k)
                if k < 3:
                    unit_load(NB - 1, k + 3)
            end_phase(sp, 2)

            sp.sem_inc(o3, 1)
            with sp.Fori(0, NB) as b:
                sp.wait_ge(v3, P3_OPS * b + P3_OPS)
                sp.dma_start(dram_b3(out, b).rearrange("(t p) d -> p t d", p=P), y_out)\
                    .then_inc(o3, 16)
            sp.wait_ge(o3, 16 * NB + 1)

        @block.gpsimd
        def _(pool):
            g = nc.gpsimd
            g.memset(ident[:, :], 0.0).then_inc(s_id, 1)
            pool.wait_ge(s_id, 1)
            g.affine_select(out=ident[:, :], in_=ident[:, :], compare_op=ALU.not_equal, fill=1.0,
                            base=0, pattern=[[-1, P]], channel_multiplier=1).then_inc(s_id, 1)
            for b in range(NB):
                pool.dma_start(resid[:, b, NI:NT, :], T["txt"][b].rearrange("(t p) d -> p t d", p=P))\
                    .then_inc(txt_loaded, 16)
            g.memset(ones_row[:, :], 1.0).then_inc(const, 1)
            g.memset(x_pair[:, :], 0.0)
            g.memset(ones_b[:, :], 1.0)
            g.memset(zero_b[:, :], 0.0)
            g.memset(pick[:, :, :], 0.0)
            g.memset(before[:, :], 1.0).then_inc(const, 1)
            pool.wait_ge(const, 2)
            g.affine_select(out=before[:, :], in_=before[:, :], compare_op=ALU.is_gt, fill=0.0,
                            base=0, pattern=[[1, P]], channel_multiplier=-1).then_inc(const, 1)
            for part in range(3):
                g.affine_select(out=pick[:, :, :], in_=pick[:, :, :], compare_op=ALU.not_equal,
                                fill=1.0, base=-32 * part, pattern=[[-1, 2 * NS], [0, P]],
                                channel_multiplier=1).then_inc(const, 1)
                pool.wait_ge(const, 4 + part)
            pool.wait_ge(txt_loaded, 16 * NB)
            end_phase(pool, 1)

            def pre(b, k):
                u = num(b, k)
                pool.wait_ge(rest_done, u + 1)
                g.tensor_tensor(high[:, :], rest[:, :], part_mask[:, 1:2].to_broadcast([96, CH]),
                                ALU.mult).then_inc(part2, 1)
                pool.wait_ge(part2, u + 1)
                at_least(pool, c_full, NS * (u - 1))
                g.tensor_tensor(parts[:, k % 2, :], rest[:, :], high[:, :], ALU.subtract)\
                    .then_inc(parts_ready, 1)

            def gate(b, k):
                u = num(b, k)
                pool.wait_ge(skip_done, u + 1)
                pool.wait_ge(zs_ld[k % 3], 16 * (2 * b + k // 3 + 1))
                at_least(pool, out_full, u - 1)
                g.tensor_tensor(y_gated[:, k % 2, :], y_skip[:, k % 2, :], zs_in[:, k % 3, :],
                                ALU.mult).then_inc(gated, 1)

            def c_product(b, k, n):
                u = num(b, k)
                i = NS * u + n
                pool.wait_ge(scanned, i + 1)
                pool.wait_ge(c_copied, len(PC) * u + PC.index(n) + 1)
                at_least(pool, summed, i - 3)
                h = arena[:, k % 2, :].rearrange("p (n t) -> p n t", n=NS)
                g.tensor_tensor(y_part[:, n % 4, :], h[:, n, :], c_all[:, n % 4, :],
                                ALU.mult).then_inc(part_pool, 1)

            def unit(b, k, back=True, ahead=True):
                for n in range(NS):
                    if n in PC:
                        c_product(b, k, n)
                    if n == 6 and back:
                        gate(*at(b, k, -1))
                    if n == 11 and ahead:
                        pre(*at(b, k, 1))

            pre(0, 0)
            for k in range(NU):
                unit(0, k, back=k >= 1)
            with pool.Fori(1, NB - 1) as b:
                for k in range(NU):
                    unit(b, k)
            for k in range(NU):
                unit(NB - 1, k, ahead=k < NU - 1)
            gate(NB - 1, NU - 1)
            pool.wait_ge(gated, NU * NB)
            end_phase(pool, 2)

        @block.scalar
        def _(act):
            a = nc.scalar
            act.wait_ge(wl, 16 * WEIGHTS)
            act.wait_ge(masks, 2)
            a.activation(a_neg[:, :, :], a_log[:, :, :], ACT.Exp).then_inc(prep_e, 1)
            act.wait_ge(const, 1)

            def tiles_of(ap, i, odd):
                return ap[0:DM, i * 512:(i + 1) * 512].rearrange("p (t o q) -> p t o q", o=2, q=P)[:, :, odd, :]

            def paired(ps, odd):
                return ps[DM * odd:DM * (odd + 1), 0:2 * P].rearrange("p (t q) -> p t q", q=P)

            def item(i, dst, src, scale=None):
                act.wait_ge(prep_p, i + 1)
                if scale is None:
                    return a.activation(dst, src, ACT.Copy)
                return a.activation(dst, src, ACT.Copy, scale=scale)

            for d in range(2):
                i = 7 * d
                bk = [bank[4 + (i + e) % 4] for e in range(7)]
                for p in range(2):
                    item(i + p, conv_t[:, d, p, :], bk[p][:, 0:P], vecs[:, d, NRM:NRM + 1]).then_inc(prep_a, 1)
                item(i + 2, gate_t[:, d, :], bk[2][0:DM, 0:P], vecs[0:DM, d, NRM:NRM + 1]).then_inc(prep_a, 1)
                for part in range(3):
                    last = item(i + 3, bc_rep[:, d, 32 * part:32 * (part + 1)], bk[3][:, RK:RK + 2 * NS])
                last.then_inc(prep_a, 1)
                item(i + 4, dtw_t[:, d, :], bk[4][0:RK, 0:P]).then_inc(prep_a, 1)
                item(i + 5, delta_t[:, d, :], bk[5][:, 0:P]).then_inc(prep_a, 1)
                item(i + 6, out_t[:, d, :], bk[6][:, 0:DM]).then_inc(prep_a, 1)
            item(14, slope[:, :], bank[4 + 14 % 4][:, 0:1]).then_inc(prep_a, 1)
            for t in range(NI):
                act.wait_ge(gamma_turned, 2 * t + 1)
                a.activation(gamma_t[:, 0:4, t * P:(t + 1) * P],
                             bank[2 * t % 4][:, :].rearrange("p (s t) -> p s t", s=4), ACT.Copy)\
                    .then_inc(gamma_a, 1)

            def head(b):
                for k in range(2):
                    act.wait_ge(g_full, g_index(b, k) + 1)
                    for odd in range(2):
                        a.activation(tiles_of(x_t, k, odd), paired(G[k % 3], odd), ACT.Copy)\
                            .then_inc(act_read, 1)
                for k in range(2, 4):
                    c = k - 2
                    act.wait_ge(g_full, g_index(b, k) + 1)
                    a.activation(q_t[:, c * 512:(c + 1) * 512], G[k % 3][0:DM, :], ACT.Copy)\
                        .then_inc(act_read, 1)
                    a.activation(k_t[:, c * 512:(c + 1) * 512], G[k % 3][DM:P, :], ACT.Copy)\
                        .then_inc(act_read, 1)
                act.wait_ge(g_full, g_index(b, 4) + 1)
                a.activation(v_sb, G[4 % 3][:, :].rearrange("p (t d) -> p t d", t=NI), ACT.Copy)\
                    .then_inc(act_read, 1)

            def roots(b):
                act.wait_ge(ln, LN_OPS * b + 8)
                a.activation(stat[:, 4, :], stat[:, 3, :], ACT.Sqrt).then_inc(sq_root, 1)
                act.wait_ge(ln, LN_OPS * b + 12)
                a.activation(stat[:, 8, :], stat[:, 7, :], ACT.Sqrt).then_inc(sq_root, 1)

            def retained(b):
                for h in range(2):
                    act.wait_ge(ret_mm, 2 * NI * b + NI * (h + 1))
                    a.activation(r_t[0:DM, h * 512:(h + 1) * 512], RT[0:DM, :], ACT.Copy)\
                        .then_inc(act_read, 1)

            def tail(b, prev):
                for i in range(3):
                    k = 5 + i
                    act.wait_ge(g_full, g_index(b, k) + 1)
                    a.activation(x_pair[0:DM, 3 + i * 512:3 + (i + 1) * 512], G[k % 3][0:DM, :], ACT.Copy)\
                        .then_inc(act_read, 1)
                    a.activation(x_pair[DM:P, 2 + i * 512:2 + (i + 1) * 512], G[k % 3][DM:P, :], ACT.Copy)\
                        .then_inc(act_read, 1)
                for q in range(12):
                    k, d = 8 + q, q // 6
                    act.wait_ge(g_full, g_index(b, k) + 1)
                    at_least(act, stored[q % 4], 16 * (3 * prev + q // 4))
                    bias = 0.0 if q % 2 else vecs[:, d, CB:CB + 1]
                    a.activation(staged[:, q % 4, :], G[k % 3][:, :], ACT.Silu, bias=bias)\
                        .then_inc(act_read, 1)

            head(0)
            retained(0)
            head(1)
            roots(0)
            retained(1)
            tail(1, 0)
            with act.Fori(2, NB) as b:
                head(b)
                roots(b - 1)
                retained(b)
                tail(b, b - 1)
            roots(NB - 1)
            tail(NB, NB - 1)
            act.wait_ge(act_read, act_value(NB, "s11"))
            end_phase(act, 1)

            def pre(b, k):
                u, d = num(b, k), k // NC
                act.wait_ge(raw_full, u + 1)
                at_least(act, delta_ready, u)
                a.activation(soft[:, :], bank[7][:, :], ACT.Abs, bias=vecs[:, d, DTB:DTB + 1])\
                    .then_inc(abs_done, 1)
                a.activation(relu[:, :], bank[7][:, :], ACT.Relu, bias=vecs[:, d, DTB:DTB + 1])\
                    .then_inc(relu_done, 1)
                act.wait_ge(abs_done, u + 1)
                a.activation(soft[:, :], soft[:, :], ACT.Exp, scale=-1.0).then_inc(exp_done, 1)
                act.wait_ge(exp_done, u + 1)
                a.activation(soft[:, :], soft[:, :], ACT.Ln, bias=1.0).then_inc(ln_done, 1)

            def part(b, k):
                u = num(b, k)
                act.wait_ge(rep_full, u + 1)
                at_least(act, parts_ready, u)
                a.activation(high[:, :], bank[6][0:96, :], ACT.Copy, scale=part_mask[:, 0:1])\
                    .then_inc(part1, 1)

            def unit(b, k, ahead=True):
                u, d = num(b, k), k // NC
                for n in range(NS):
                    i = NS * u + n
                    if n == 0:
                        act.wait_ge(delta_ready, u + 1)
                    at_least(act, scanned, i - 3)
                    a.activation(decay[:, n % 4, :], delta[:, k % 2, :], ACT.Exp,
                                 scale=a_neg[:, d, n:n + 1]).then_inc(decay_ready, 1)
                    if n in PC:
                        act.wait_ge(c_full, i + 1)
                        free_c_slot(act, b, k, n)
                        a.activation(c_all[:, n % 4, :], bank[2 + n % 2][:, :], ACT.Copy)\
                            .then_inc(c_copied, 1)
                    if ahead and n == 3:
                        pre(*at(b, k, 1))
                    if ahead and n == 7:
                        part(*at(b, k, 1))

            pre(0, 0)
            part(0, 0)
            for k in range(NU):
                unit(0, k)
            with act.Fori(1, NB - 1) as b:
                for k in range(NU):
                    unit(b, k)
            for k in range(NU):
                unit(NB - 1, k, ahead=k < NU - 1)
            act.wait_ge(c_copied, len(PC) * NU * NB)
            end_phase(act, 2)

            with act.Fori(0, NB) as b:
                act.wait_ge(v3, P3_OPS * b + 7)
                a.activation(stat[:, 4, :], stat[:, 3, :], ACT.Sqrt).then_inc(root3, 1)
                for i in range(3):
                    act.wait_ge(t3, 3 * b + i + 1)
                    for odd in range(2):
                        a.activation(tiles_of(xl_t, i, odd), paired(bank[i], odd), ACT.Copy)\
                            .then_inc(xt3, 1)
                for i in range(3):
                    act.wait_ge(w3, 3 * b + i + 1)
                    a.activation(w_row[:, i * 512:(i + 1) * 512], bank[3 + i][:, :], ACT.Copy)\
                        .then_inc(wc3, 1)
                for i in range(6):
                    hg, c = i // 3, i % 3
                    act.wait_ge(h3, 6 * b + i + 1)
                    a.activation(hid[:, hg, c * 512:(c + 1) * 512], bank[6 + i % 2][:, :],
                                 ACT.Gelu_apprx_tanh, bias=b_1[:, hg:hg + 1]).then_inc(g3, 1)

        @block.tensor
        def _(pe):
            t_ = nc.tensor

            def mm(o, lhsT, rhs, start=True, stop=True, **kw):
                return t_.matmul(o, lhsT, rhs, start=start, stop=stop, **kw)

            pe.wait_ge(s_id, 2)
            pe.wait_ge(wl, 16 * WEIGHTS)
            pe.wait_ge(const, 1)
            for d in range(2):
                i = 7 * d
                bk = [bank[4 + (i + e) % 4] for e in range(7)]

                def ready(e, i=i):
                    at_least(pe, prep_a, i + e - 3)
                pe.wait_ge(prep_v, 4 * d + 4)
                for p in range(2):
                    ready(p)
                    t_.transpose(bk[p][:, 0:P], tap_w[:, d, 2 * p:2 * p + 2, :].rearrange("p k i -> p (k i)"),
                                 ident[:, :]).then_inc(prep_p, 1)
                ready(2)
                t_.transpose(bk[2][0:DM, 0:P], in_w[:, d, 1, :], ident[:, :]).then_inc(prep_p, 1)
                ready(3)
                nx = RK + 2 * NS
                t_.transpose(bk[3][:, 0:nx], xp_w[:, d, :], ident[0:nx, 0:nx]).then_inc(prep_p, 1)
                ready(4)
                t_.transpose(bk[4][0:RK, 0:P], dt_w[:, d, :], ident[:, :]).then_inc(prep_p, 1)
                pe.wait_ge(prep_a, i + 5)
                mm(bk[5][:, 0:P], xp_w[0:RK, d, :], dtw_t[:, d, :]).then_inc(prep_p, 1)
                ready(6)
                t_.transpose(bk[6][:, 0:DM], op_w[:, d, :], ident[0:DM, 0:DM]).then_inc(prep_p, 1)
            at_least(pe, prep_a, 14 - 3)
            mm(bank[4 + 14 % 4][:, 0:1], ones_row[:, :], slope_in[:, :]).then_inc(prep_p, 1)
            for t in range(NI):
                pe.wait_ge(gamma_ld[t % 2], 16 * (t // 2 + 1))
                for h in range(2):
                    if t >= 2:
                        pe.wait_ge((gamma_a, gamma_v)[h], t - 1)
                    for s in range(4):
                        last = t_.transpose(bank[(2 * t + h) % 4][:, s * P:(s + 1) * P],
                                            gamma_in[:, t % 2, (4 * h + s) * P:(4 * h + s + 1) * P],
                                            ident[:, :])
                    last.then_inc(gamma_turned, 1)
            pe.wait_ge(prep_a, PREP)
            pe.wait_ge(const, 6)
            pe.wait_ge(masks, 2)
            pe.wait_ge(gamma_a, NI)
            pe.wait_ge(gamma_v, NI)

            def head(b):
                pe.wait_ge(x_loaded, 16 * (b + 1))
                for k in range(2):
                    wait_bank(pe, b, k)
                    for i in range(2):
                        t = 4 * k + 2 * i
                        last = t_.transpose(G[k % 3][:, i * P:(i + 1) * P],
                                            x_in[:, t:t + 2, :].rearrange("p t d -> p (t d)"), ident[:, :])
                    last.then_inc(g_full, 1)
                for k in range(2, 4):
                    c = k - 2
                    wait_bank(pe, b, k)
                    pe.wait_ge(act_read, act_value(b, f"x{c}u"))
                    mm(G[k % 3][:, :], w_qk[:, :], x_t[0:DM + 1, c * 512:(c + 1) * 512]).then_inc(g_full, 1)
                wait_bank(pe, b, 4)
                for i in range(NI):
                    last = mm(G[4 % 3][:, i * DM:(i + 1) * DM], x_t[0:DM + 1, i * P:(i + 1) * P], w_v[:, :])
                last.then_inc(g_full, 1)

            def mixer(b):
                pe.wait_ge(act_read, act_value(b, "v"))
                for j in range(2 * NI + 2):
                    if j < 2 * NI:
                        h, s = divmod(j, NI)
                        at_least(pe, mix_done, 2 * NI * b + j - 3)
                        mm(bank[j % 4][:, :], k_t[:, s * P:(s + 1) * P], q_t[:, h * 512:(h + 1) * 512])\
                            .then_inc(sc_full, 1)
                    if j >= 2:
                        i = j - 2
                        h, s = divmod(i, NI)
                        if s == 0:
                            if h:
                                pe.wait_ge(act_read, act_value(b, "r0"))
                            elif not (isinstance(b, int) and b == 0):
                                pe.wait_ge(act_read, act_value(b - 1, "r1"))
                        pe.wait_ge(mix_done, 2 * NI * b + i + 1)
                        mm(RT[0:DM, :], v_sb[:, s, :], mixed[:, i % 4, :], start=s == 0, stop=s == NI - 1)\
                            .then_inc(ret_mm, 1)

            def tail(b, prev):
                pe.wait_ge(ln, LN_OPS * prev + 15)
                for i in range(3):
                    k = 5 + i
                    wait_bank(pe, b, k)
                    for q in range(4):
                        last = t_.transpose(G[k % 3][:, q * P:(q + 1) * P],
                                            x_rms[:, 4 * i + q, :, :].rearrange("p a d -> p (a d)"), ident[:, :])
                    last.then_inc(g_full, 1)
                pe.wait_ge(act_read, act_value(b, "X2u"))
                for q in range(12):
                    k, d, c, z = 8 + q, q // 6, (q % 6) // 2, q % 2
                    wait_bank(pe, b, k)
                    if z:
                        last = mm(G[k % 3][:, :], gate_t[:, d, :], x_pair[0:DM, c * 512 + 3:c * 512 + 515])
                    else:
                        o = c * 512 + (0 if d == 0 else 3)
                        mm(G[k % 3][:, :], conv_t[:, d, 0, :], x_pair[:, o:o + 512], stop=False)
                        last = mm(G[k % 3][:, :], conv_t[:, d, 1, :], x_pair[:, o + 2:o + 514], start=False)
                    last.then_inc(g_full, 1)

            def proj(b):
                k = PROJ[0]
                wait_bank(pe, b, k)
                pe.wait_ge(act_read, act_value(b, "r1"))
                for i in range(NI):
                    last = mm(G[k % 3][:, i * DM:(i + 1) * DM], r_t[0:DM + 1, i * P:(i + 1) * P], w_o[:, :])
                last.then_inc(g_full, 1)

            head(0)
            mixer(0)
            proj(0)
            head(1)
            mixer(1)
            tail(1, 0)
            proj(1)
            with pe.Fori(2, NB) as b:
                head(b)
                mixer(b)
                tail(b, b - 1)
                proj(b)
            tail(NB, NB - 1)
            pe.wait_ge(g_full, g_index(NB, 19) + 1)
            end_phase(pe, 1)

            def delta_mm(b, k):
                u, d = num(b, k), k // NC
                pe.wait_ge(xc_ld[k], 16 * (b + 1))
                at_least(pe, added, u - 2)
                mm(bank[7][:, :], delta_t[:, d, :], xc_in[:, k, :]).then_inc(raw_full, 1)

            def rep_mm(b, k):
                u, d = num(b, k), k // NC
                at_least(pe, rest_done, u)
                mm(bank[6][0:96, :], bc_rep[:, d, :], xc_in[:, k, :]).then_inc(rep_full, 1)

            def out_mm(b, k, ahead=True):
                u, d = num(b, k), k // NC
                pe.wait_ge(gated, u + 1)
                if ahead:
                    pe.wait_ge(relu_done, u + 3)
                else:
                    at_least(pe, added, u)
                for i in range(4):
                    last = mm(bank[7][:, i * DM:(i + 1) * DM], y_gated[:, k % 2, i * P:(i + 1) * P], out_t[:, d, :])
                last.then_inc(out_full, 1)

            def spread(b, k, n):
                u = num(b, k)
                i = NS * u + n
                if n == 0:
                    pe.wait_ge(parts_ready, u + 1)
                at_least(pe, drive_done, i - 1)
                mm(bank[n % 2][:, :], pick[:, n, :], parts[:, k % 2, :]).then_inc(b_full, 1)
                bb, kk, m = earlier_state(b, k, n, 2)
                if m in VC:
                    at_least(pe, part_vec, products(bb, kk, m, VC))
                else:
                    at_least(pe, c_copied, products(bb, kk, m, PC))
                mm(bank[2 + n % 2][:, :], pick[:, NS + n, :], parts[:, k % 2, :]).then_inc(c_full, 1)

            def add_state(b, k, n):
                u = num(b, k)
                wait_products(pe, b, k, n)
                if n == 0:
                    at_least(pe, skip_done, u - 1)
                mm(bank[4 + k % 2][:, :], ident[:, :], y_part[:, n % 4, :], start=n == 0, stop=n == NS - 1)\
                    .then_inc(summed, 1)

            def unit(b, k, back=True, ahead=True, scans=True):
                for n in range(NS if scans else LAG):
                    if scans:
                        spread(b, k, n)
                    if n >= LAG or back:
                        add_state(*earlier_state(b, k, n, LAG))
                    if n == 1 and ahead:
                        delta_mm(*at(b, k, 1))
                    if n == 4 and ahead:
                        rep_mm(*at(b, k, 1))
                    if n == 10 and back:
                        out_mm(*at(b, k, -1), ahead=ahead)

            delta_mm(0, 0)
            rep_mm(0, 0)
            for k in range(NU):
                unit(0, k, back=k >= 1)
            with pe.Fori(1, NB - 1) as b:
                for k in range(NU):
                    unit(b, k)
            for k in range(NU):
                unit(NB - 1, k, ahead=k < NU - 1)
            unit(NB, 0, ahead=False, scans=False)
            out_mm(NB - 1, NU - 1, ahead=False)
            pe.wait_ge(out_full, NU * NB)
            end_phase(pe, 2)

            pe.wait_ge(masks, 3)
            with pe.Fori(0, NB) as b:
                pe.wait_ge(v3, P3_OPS * b + 9)
                for i in range(3):
                    for q in range(2):
                        t = 4 * i + 2 * q
                        last = t_.transpose(bank[i][:, q * P:(q + 1) * P],
                                            xl[:, t:t + 2, :].rearrange("p t d -> p (t d)"), ident[:, :])
                    last.then_inc(t3, 1)
                for i in range(3):
                    pe.wait_ge(xt3, 6 * b + 2 * i + 2)
                    mm(bank[3 + i][:, :], w_rr[:, :], xl_t[0:DM + 1, i * 512:(i + 1) * 512]).then_inc(w3, 1)
                for i in range(6):
                    hg, c = i // 3, i % 3
                    if i >= 2:
                        pe.wait_ge(g3, 6 * b + i - 1)
                    mm(bank[6 + i % 2][:, :], w_1[:, hg * P:(hg + 1) * P], xl_t[0:DM, c * 512:(c + 1) * 512])\
                        .then_inc(h3, 1)
                pe.wait_ge(g3, 6 * b + 6)
                for t in range(NT):
                    o = bank[t // 8][:, (t % 8) * DM:(t % 8 + 1) * DM]
                    mm(o, ones_row[:, :], b_2[:, :], stop=False)
                    mm(o, hid[:, 0, t * P:(t + 1) * P], w_2[:, 0, :], start=False, stop=False)
                    last = mm(o, hid[:, 1, t * P:(t + 1) * P], w_2[:, 1, :], start=False)
                last.then_inc(y3, 1)
                mm(bank[2][:, 0:NT], ones_b[:, :], zero_b[:, :], stop=False, skip_group_check=True)
                for j in range(NT):
                    pe.wait_ge(v3, P3_OPS * b + 11 + (0 if j == 0 else 4 * j - 1) + (3 if j in (0, NT - 1) else 4))
                    for t in range(NT):
                        last = mm(bank[2][:, t:t + 1], higher_of(j)[:, t * P:(t + 1) * P], ones_b[:, 0:1],
                                  start=False, stop=j == NT - 1, skip_group_check=True)
                last.then_inc(rk3, 1)

        @block.vector
        def _(dve):
            v = nc.vector
            v.memset(x_t[DM:DM + 1, :], 1.0)
            v.memset(r_t[DM:DM + 1, :], 1.0)
            v.memset(part_mask[0:96, 0:1], 1.0)
            v.memset(part_mask[0:96, 1:2], 0.0).then_inc(masks, 1)
            dve.wait_ge(masks, 1)
            v.memset(part_mask[0:32, 0:1], 0.0)
            v.memset(part_mask[64:96, 1:2], 1.0).then_inc(masks, 1)
            dve.wait_ge(wl, 16 * WEIGHTS)
            for d in range(2):
                for j in range(4):
                    tap = j if d == 0 else 3 - j
                    v.tensor_scalar(tap_w[:, d, j, :], in_w[:, d, 0, :], conv_w[:, d, tap:tap + 1], None,
                                    ALU.mult).then_inc(prep_v, 1)
            v.tensor_copy(w_rr[:, :], w_r[:, 0:1].to_broadcast([DM + 1, P])).then_inc(prep_v, 1)
            dve.wait_ge(prep_e, 1)
            v.tensor_scalar(a_neg[:, :, :], a_neg[:, :, :], -1.0, None, ALU.mult).then_inc(prep_v, 1)
            dve.wait_ge(prep_a, PREP)
            for t in range(NI):
                dve.wait_ge(gamma_turned, 2 * t + 2)
                v.tensor_copy(gamma_t[:, 4:8, t * P:(t + 1) * P],
                              bank[(2 * t + 1) % 4][:, :].rearrange("p (s t) -> p s t", s=4))\
                    .then_inc(gamma_v, 1)
            dve.wait_ge(gamma_a, NI)
            dve.wait_ge(txt_loaded, 16 * NB)

            def over(ap, n=DM):
                return ap.rearrange("p (t o) -> p t o", o=1).to_broadcast([P, NT, n])

            def prelu(b):
                dve.wait_ge(g_full, g_index(b, PROJ[0]) + 1)
                y = G[PROJ[0] % 3]
                v.tensor_scalar(neg_part[:, :], y[:, :], 0.0, slope[:, 0:1], ALU.min, ALU.mult).then_inc(neg_done, 1)
                dve.wait_ge(neg_done, b + 1)
                dst = tok(b)[:, 0:NI, :]
                v.scalar_tensor_tensor(dst, y[:, :].rearrange("p (t d) -> p t d", t=NI), 0.0,
                                       neg_part[:, :].rearrange("p (t d) -> p t d", t=NI), ALU.max, ALU.add)\
                    .then_inc(prelu_done, 1)

            S1, MEAN, VAR, VE, SD, RSTD, RR, ME, SD2, R2 = range(10)

            def st(i):
                return stat[:, i, :]

            def norm_step(b, i):
                if i == -1:
                    dve.wait_ge(prelu_done, b + 1)
                else:
                    dve.wait_ge(ln, LN_OPS * b + i + 1)
                x = tok(b)
                if i == -1:
                    ins = v.tensor_scalar(x_mid, x, 1.0, None, ALU.mult)
                elif i == 0:
                    ins = v.tensor_reduce(st(S1), x_mid, AX_X, ALU.add)
                elif i == 1:
                    ins = v.tensor_scalar(st(MEAN), st(S1), 1.0 / DM, None, ALU.mult)
                elif i == 2:
                    ins = v.tensor_tensor(x_mid, x, over(st(MEAN)), ALU.subtract)
                elif i == 3:
                    ins = v.tensor_tensor(x_sq, x_mid, x_mid, ALU.mult)
                elif i == 4:
                    ins = v.tensor_reduce(st(S1), x_sq, AX_X, ALU.add)
                elif i == 5:
                    ins = v.tensor_scalar(st(VAR), st(S1), 1.0 / DM, None, ALU.mult)
                elif i == 6:
                    ins = v.tensor_scalar(st(VE), st(VAR), EPS, None, ALU.add)
                elif i == 7:
                    dve.wait_ge(sq_root, 2 * b + 1)
                    ins = v.reciprocal(st(RSTD), st(SD))
                elif i == 8:
                    ins = v.tensor_tensor(st(RR), st(RSTD), st(RSTD), ALU.mult)
                elif i == 9:
                    ins = v.tensor_tensor(st(RR), st(RR), st(VAR), ALU.mult)
                elif i == 10:
                    ins = v.tensor_scalar(st(ME), st(RR), EPS, None, ALU.add)
                elif i == 11:
                    dve.wait_ge(sq_root, 2 * b + 2)
                    ins = v.reciprocal(st(R2), st(SD2))
                elif i == 12:
                    ins = v.tensor_tensor(x_sq, x_mid, over(st(RSTD)), ALU.mult)
                elif i == 13:
                    for half in range(2):
                        ins = v.tensor_tensor(x_rms[:, :, half, :], x_sq, over(st(R2)), ALU.mult)
                else:
                    ins = v.scalar_tensor_tensor(x, x_sq, 2.0, x, ALU.mult, ALU.add)
                ins.then_inc(ln, 1)

            NORM_AT = {0: [-1, 0], 1: [1, 2], 2: [3], 3: [4], 4: [5, 6], 5: [7, 8, 9, 10], 7: [11, 12], 9: [13], 11: [14]}

            def mixer(b, prev=None):
                for j in range(2 * NI):
                    h, s = divmod(j, NI)
                    dve.wait_ge(sc_full, 2 * NI * b + j + 1)
                    at_least(dve, ret_mm, 2 * NI * b + j - 3)
                    v.tensor_tensor(mixed[:, j % 4, :], gamma_t[:, s, h * 512:(h + 1) * 512], bank[j % 4][:, :],
                                    ALU.mult).then_inc(mix_done, 1)
                    if prev is not None:
                        for i in NORM_AT.get(j, []):
                            norm_step(prev, i)

            mixer(0)
            prelu(0)
            mixer(1, 0)
            with dve.Fori(2, NB) as b:
                prelu(b - 1)
                mixer(b, b - 1)
            prelu(NB - 1)
            for i in range(-1, LN_OPS - 1):
                norm_step(NB - 1, i)
            dve.wait_ge(ln, LN_OPS * NB)
            end_phase(dve, 1)

            def pre(b, k):
                u = num(b, k)
                dve.wait_ge(ln_done, u + 1)
                at_least(dve, decay_ready, NS * (u - 1))
                v.tensor_tensor(delta[:, k % 2, :], relu[:, :], soft[:, :], ALU.add).then_inc(delta_ready, 1)
                dve.wait_ge(delta_ready, u + 1)
                dve.wait_ge(xc_ld[k], 16 * (b + 1))
                v.tensor_tensor(du[:, k % 2, :], delta[:, k % 2, :], xc_in[:, k, :], ALU.mult).then_inc(du_ready, 1)

            def less_first(b, k):
                u = num(b, k)
                dve.wait_ge(part1, u + 1)
                at_least(dve, parts_ready, u)
                v.tensor_tensor(rest[:, :], bank[6][0:96, :], high[:, :], ALU.subtract).then_inc(rest_done, 1)

            def product(b, k, n):
                u = num(b, k)
                if n == 0:
                    dve.wait_ge(du_ready, u + 1)
                dve.wait_ge(b_full, NS * u + n + 1)
                v.tensor_tensor(drive[:, n % 4, :], du[:, k % 2, :], bank[n % 2][:, :], ALU.mult)\
                    .then_inc(drive_done, 1)

            def states(k):
                return arena[:, k % 2, :].rearrange("p (n t) -> p n t", n=NS)

            def scan(b, k, n):
                u = num(b, k)
                i = NS * u + n
                wait_products_of_old(b, k, n)
                dve.wait_ge(decay_ready, i + 1)
                dve.wait_ge(drive_done, i + 1)
                if k < NC:
                    o, x0, x1 = states(k)[:, n, :], decay[:, n % 4, :], drive[:, n % 4, :]
                    edge = states(k + 1)[:, n, CH - 1:CH]
                else:
                    o, x0, x1 = states(k)[:, n, ::-1], decay[:, n % 4, ::-1], drive[:, n % 4, ::-1]
                    edge = states(k + 1)[:, n, 0:1]
                v.tensor_tensor_scan(o, x0, x1, 0.0 if k % NC == 0 else edge, ALU.mult, ALU.add)\
                    .then_inc(scanned, 1)

            def wait_products_of_old(b, k, n):
                if n == 0:
                    at_least(dve, part_pool, len(PC) * (num(b, k) - 1))

            def c_product(b, k, n):
                i = NS * num(b, k) + n
                dve.wait_ge(scanned, i + 1)
                dve.wait_ge(c_full, i + 1)
                at_least(dve, summed, i - 3)
                v.tensor_tensor(y_part[:, n % 4, :], states(k)[:, n, :], bank[2 + n % 2][:, :], ALU.mult)\
                    .then_inc(part_vec, 1)

            def skip(b, k):
                u, d = num(b, k), k // NC
                dve.wait_ge(summed, NS * (u + 1))
                at_least(dve, gated, u - 1)
                v.scalar_tensor_tensor(y_skip[:, k % 2, :], xc_in[:, k, :], vecs[:, d, DSK:DSK + 1],
                                       bank[4 + k % 2][:, :], ALU.mult, ALU.add).then_inc(skip_done, 1)

            def add_out(b, k):
                u = num(b, k)
                d, c = unit_of(k)
                dve.wait_ge(out_full, u + 1)
                x = tok(b)[:, 4 * c:4 * c + 4, :]
                v.tensor_tensor(x, x, bank[7][:, 0:4 * DM].rearrange("p (t d) -> p t d", t=4), ALU.add)\
                    .then_inc(added, 1)

            def unit(b, k, back=True, ahead=True):
                for n in range(NS):
                    product(b, k, n)
                    if n >= 1 or back:
                        scan(*earlier_state(b, k, n, 1))
                    if n >= 2 and n - 2 in VC:
                        c_product(b, k, n - 2)
                    if n == 5 and back:
                        skip(*at(b, k, -1))
                    if n == 7 and ahead:
                        pre(*at(b, k, 1))
                    if n == 9 and ahead:
                        less_first(*at(b, k, 1))
                    if n == 12 and back:
                        add_out(*at(b, k, -1))

            pre(0, 0)
            less_first(0, 0)
            for k in range(NU):
                unit(0, k, back=k >= 1)
            with dve.Fori(1, NB - 1) as b:
                for k in range(NU):
                    unit(b, k)
            for k in range(NU):
                unit(NB - 1, k, ahead=k < NU - 1)
            scan(NB - 1, NU - 1, NS - 1)
            skip(NB - 1, NU - 1)
            add_out(NB - 1, NU - 1)
            dve.wait_ge(added, NU * NB)
            end_phase(dve, 2)

            v.memset(xl_t[DM:DM + 1, :], 1.0).then_inc(masks, 1)
            with dve.Fori(0, NB) as b:
                step = [0]

                def then(ins, hold=True):
                    step[0] += 1
                    ins.then_inc(v3, 1)
                    if hold:
                        dve.wait_ge(v3, P3_OPS * b + step[0])

                x = tok(b)
                then(v.tensor_scalar(xl, x, 1.0, None, ALU.mult))
                then(v.tensor_reduce(st(S1), xl, AX_X, ALU.add))
                then(v.tensor_scalar(st(MEAN), st(S1), 1.0 / DM, None, ALU.mult))
                then(v.tensor_tensor(xl, x, over(st(MEAN)), ALU.subtract))
                then(v.tensor_tensor(sq3, xl, xl, ALU.mult))
                then(v.tensor_reduce(st(S1), sq3, AX_X, ALU.add))
                then(v.tensor_scalar(st(VE), st(S1), 1.0 / DM, EPS, ALU.mult, ALU.add))
                dve.wait_ge(root3, b + 1)
                then(v.reciprocal(st(RSTD), st(SD)))
                then(v.tensor_tensor(xl, xl, over(st(RSTD)), ALU.mult))
                dve.wait_ge(wc3, 3 * b + 3)
                then(v.tensor_tensor(w_diag.rearrange("p (t q) -> p t q", t=NT),
                                     w_row.rearrange("p (t q) -> p t q", t=NT),
                                     ident[:, :].rearrange("p (o q) -> p o q", o=1).to_broadcast([P, NT, P]),
                                     ALU.mult))
                then(v.tensor_reduce(st(MEAN), w_diag.rearrange("p (t q) -> p t q", t=NT), AX_X, ALU.add))
                for j in range(NT):
                    hi, w = higher_of(j), stat[:, MEAN, j:j + 1]
                    lo, up = j * P, (j + 1) * P
                    if j:
                        then(v.tensor_scalar(hi[:, 0:lo], w_row[:, 0:lo], w, None, ALU.is_lt), False)
                    if j < NT - 1:
                        then(v.tensor_scalar(hi[:, up:L], w_row[:, up:L], w, None, ALU.is_le), False)
                    then(v.scalar_tensor_tensor(w_eq[:, j % 2, :], w_row[:, lo:up], w, before[:, :],
                                                ALU.is_equal, ALU.mult))
                    then(v.scalar_tensor_tensor(hi[:, lo:up], w_row[:, lo:up], w, w_eq[:, j % 2, :],
                                                ALU.is_lt, ALU.add), False)
                dve.wait_ge(rk3, b + 1)
                then(v.scalar_tensor_tensor(st(R2), bank[2][:, 0:NT], float(KK), st(MEAN), ALU.is_lt, ALU.mult))
                dve.wait_ge(y3, b + 1)
                dve.wait_ge(o3, 16 * b + 1)
                for lo, up in ((0, 8), (8, NT)):
                    then(v.tensor_tensor(y_out[:, lo:up, :],
                                         bank[lo // 8][:, 0:(up - lo) * DM].rearrange("p (t d) -> p t d", d=DM),
                                         stat[:, R2, lo:up].rearrange("p (t o) -> p t o", o=1)
                                         .to_broadcast([P, up - lo, DM]), ALU.mult))
                then(v.tensor_tensor(y_out, y_out, xl, ALU.add))
                then(v.tensor_tensor(y_out, y_out, x, ALU.add))
                assert step[0] == P3_OPS


INPUTS = ["x", "txt", "L0_tok_d_gamma_batched"] + [f"L0_tok_{n}" for n in
    ("Wq", "bq", "Wk", "bk", "Wv", "bv", "Wo", "bo", "prelu_a")] + [
    f"L0_attn_{d}_{n}" for d in ("fw", "bw") for n in
    ("norm", "in_proj", "conv_w", "conv_b", "x_proj", "dt_w", "dt_b", "A_log", "D", "out_proj")] + [
    f"L0_ffn_{n}" for n in ("wr", "br", "w1", "b1", "w2", "b2")]


def kernel(**inputs):
    import numpy as np
    import concourse.bacc as bacc
    from concourse.bass_utils import run_bass_kernel_spmd

    nc = bacc.Bacc("TRN2", target_bir_lowering=False, num_devices=1)
    arrays, handles = {}, {}
    for name in INPUTS:
        a = np.ascontiguousarray(inputs[name])
        if a.ndim == 0:
            a = a.reshape(1, 1)
        arrays[f"in_{name}"] = a
        handles[name] = nc.dram_tensor(f"in_{name}", a.shape, mybir.dt.from_np(a.dtype), kind="ExternalInput").ap()
    out = nc.dram_tensor("out", (NB, L, DM), F32, kind="ExternalOutput").ap()
    build(nc, handles, out)
    return run_bass_kernel_spmd(nc, [arrays], core_ids=[0]).results[0]["out"]
```

```python
from contextlib import ExitStack

import concourse.bass as bass
import concourse.mybir as mybir
from concourse.alu_op_type import AluOpType as ALU

F32 = mybir.dt.float32
BF16 = mybir.dt.bfloat16
ACT = mybir.ActivationFunctionType
AX_X = mybir.AxisListType.X

P = 128
NB = 8
DM = 64
TI = 1024
TX = 512
L = TI + TX
NT = L // P
NI = TI // P
DI = 128
NS = 16
RK = 4
CH = 512
NC = L // CH
PS = NC * NS
LAG = 3
GATE_AT, OUT_AT, DELTA_AT, SOFT_AT, SPLIT_AT = LAG, 5, 7, 9, 11
DECAY_AT = 1
SKIP_AT = {(LAG - 1, 2): 0, (LAG, 0): 1, (LAG, 1): 2}
HID = 4 * DM
KK = L // 2 - 1
EPS = 1e-5

NORMED, CONVS = ["X0", "X1", "X2"], [f"s{i}" for i in range(12)]
SEQUENCE = NORMED + ["P"] + CONVS[:4] + ["x0", "x1"] + CONVS[4:7] + ["q0", "q1"] + CONVS[7:]
READS = {**{u: [u + "l", u + "u"] for u in NORMED + ["x0", "x1"]}, **{u: [u] for u in CONVS},
         "q0": ["q0", "k0"], "q1": ["q1", "k1"], "P": []}
PARTS = {"start": "xq", "first": "Pxq", "mid": "XPsxq", "last": "XPs", "after": "Xs"}
LN_OPS = 16
NORM3_OPS = 8
FINAL_OPS = 6
RING3 = 12
TURN_AT = 8
TURNED = (0, 1, 4)
PREP = 17


def at_least(eng, sem, value):
    if isinstance(value, int) and value <= 0:
        return
    eng.wait_ge(sem, value)


def where_is(b):
    return {-1: "start", 0: "first", NB - 1: "last", NB: "after"}.get(b, "mid") if isinstance(b, int) else "mid"


def uses(where):
    return [u for u in SEQUENCE if u[0] in PARTS[where]]


def reads(where):
    mixer = [] if where in ("start", "after") else ["r0", "r1"]
    return mixer + [r for u in uses(where) for r in READS[u]]


def count_before(b, items):
    n = {w: len(items(w)) for w in PARTS}
    if isinstance(b, int) and b <= 0:
        return 0 if b < 0 else n["start"]
    before = n["start"] + n["first"] + n["mid"] * (b - 1)
    return before - n["mid"] + n["last"] if isinstance(b, int) and b == NB else before


def g_value(b, use):
    return count_before(b, uses) + uses(where_is(b)).index(use) + 1


def act_value(b, name):
    return count_before(b, reads) + reads(where_is(b)).index(name) + 1


def build(nc, T, out):
    with ExitStack() as ctx:
        def sb(name, shape, dt=F32):
            return ctx.enter_context(nc.sbuf_tensor(name, shape, dt))

        def sem(name):
            return ctx.enter_context(nc.semaphore(name))

        psum = ctx.enter_context(nc.psum_tensor("psum", [P, 8, 512], F32))
        bank = [psum[:, i, :] for i in range(8)]
        conv_dram = nc.dram_tensor("conv_scratch", (NB, 2, DI, L), F32, kind="Internal").ap()
        gate_dram = nc.dram_tensor("gate_scratch", (NB, 2, DI, L), F32, kind="Internal").ap()

        resid = sb("resid", [P, NB, NT, DM])
        ident = sb("ident", [P, P])
        w_qk = sb("w_qk", [DM + 1, 2 * DM])
        w_v = sb("w_v", [DM + 1, DM])
        w_vt = sb("w_vt", [DM, DM + 1])
        w_o = sb("w_o", [DM, DM])
        w_vo = sb("w_vo", [DM + 2, DM])
        slope = sb("slope", [P, 1])
        ones_row = sb("ones_row", [1, P])
        conv_t = sb("conv_t", [P, 2, 2, DI])
        gate_t = sb("gate_t", [DM, 2, DI])
        bc_rep = sb("bc_rep", [DI, 2, 96])
        delta_t = sb("delta_t", [DI, 2, DI])
        out_t = sb("out_t", [DI, 2, DM])
        a_neg = sb("a_neg", [DI, 2, NS])
        vecs = sb("vecs", [P, 2, 4])
        CB, DTB, DSK, NRM = range(4)
        pick = sb("pick", [96, 2 * NS, P], BF16)
        w_1 = sb("w_1", [DM, HID])
        b_1 = sb("b_1", [P, 2])
        w_2 = sb("w_2", [P, 2, 2 * DM])
        b_2 = sb("b_2", [P, 1])
        w_r = sb("w_r", [DM + 1, 1])
        w_rr = sb("w_rr", [DM + 1, P])
        before = sb("before", [P, P])
        ones_b = sb("ones_b", [P, P], BF16)
        rings = sb("rings", [P, 12, L])
        decay, drive, h, c_all = (rings[:, 2 * i:2 * i + 2, :] for i in range(4))
        y_part = rings[:, 8:12, :]
        xc_in = sb("xc_in", [P, 2, L])
        zs_in = sb("zs_in", [P, L])
        delta = sb("delta", [P, 2, L])
        du = sb("du", [P, 2, L])
        soft = sb("soft", [P, L])
        parts = sb("parts", [96, 2, L], BF16)
        rest = sb("rest", [96, 2, CH])
        high = sb("high", [96, 2, CH], BF16)
        part_mask = sb("part_mask", [96, 2])
        y_skip = sb("y_skip", [P, L])
        flat = rings[:, :, :].rearrange("p r t -> p (r t)")

        def carve(ap, start, *dims):
            size = 1
            for n in dims:
                size *= n
            part = ap[:, start:start + size]
            if len(dims) == 2:
                part = part.rearrange("p (a b) -> p a b", a=dims[0])
            return part, start + size

        gamma_t, at_ = carve(flat, 0, NI, TI)
        x_t, at_ = carve(flat, at_, TI)
        q_t, at_ = carve(flat, at_, TI)
        k_t, at_ = carve(flat, at_, TI)
        q_t, k_t = q_t[0:DM, :], k_t[0:DM, :]
        x_keys, at_ = carve(flat, at_, NI, DM + 1)
        mixed, at_ = carve(flat, at_, 4, 512)
        r_t, at_ = carve(flat, at_, TI)
        x_in, at_ = carve(flat, at_, NI, DM)
        staged, at_ = carve(flat, at_, 4, 512)
        gamma_in, _ = carve(xc_in[:, :, :].rearrange("p r t -> p (r t)"), 0, 2, TI)
        du_flat = du[:, :, :].rearrange("p r t -> p (r t)")
        x_mid, at_ = carve(du_flat, 0, NT, DM)
        x_sq, at_ = carve(du_flat, at_, NT, DM)
        x_rms = du_flat[:, at_:at_ + NT * 2 * DM].rearrange("p (t a d) -> p t a d", t=NT, a=2)
        x_pair = delta[:, :, :].rearrange("p r t -> p (r t)")[:, 0:L + 8]
        zero_b = sb("zero_b", [P, NT], BF16)
        stat = sb("stat", [P, 10, NT])
        neg_part = sb("neg_part", [P, NI * DM])
        in_w = sb("in_w", [P, 2, 2, DM])
        tap_w = sb("tap_w", [P, 2, 4, DM])
        xp_w = sb("xp_w", [RK + 2 * NS, 2, DI])
        dt_w = sb("dt_w", [DI, 2, RK])
        dtw_t = sb("dtw_t", [RK, 2, DI])
        op_w = sb("op_w", [DM, 2, DI])
        a_log = sb("a_log", [DI, 2, NS])
        conv_w = sb("conv_w", [P, 2, 4])
        slope_in = sb("slope_in", [1, 1])
        def two(ap, start=0):
            return [carve(ap, start + i * NT * DM, NT, DM)[0] for i in range(2)]

        x3 = two(flat, 0)
        x_sum = two(flat, 2 * NT * DM)
        sq3, at_ = carve(flat, 4 * NT * DM, NT, DM)
        higher = flat[:, at_:at_ + NT * L // 2].bitcast(BF16).rearrange("p (j t) -> p j t", j=NT)
        xl = two(du_flat, 0)
        y_out = two(du_flat, 2 * NT * DM)
        w_row = [delta[:, i, :] for i in range(2)]
        xl_t = soft
        y_t = zs_in
        hid = xc_in
        stat3 = sb("stat3", [P, 2, 6, NT])
        row_sum = sb("row_sum", [P, 2, NT])
        threshold = sb("threshold", [P, NT])
        later = sb("later", [P, 1])

        S1, MEAN, VE, SD, RSTD, VAR, RR, ME, SD2, R2 = range(10)
        WT = VAR

        wl = sem("weights_loaded")
        s_id = sem("ident_ready")
        const = sem("constants_ready")
        prep_v = sem("prep_vector")
        prep_a = sem("prep_scalar")
        prep_p = sem("prep_tensor")
        prep_e = sem("prep_exp")
        masks = sem("masks_ready")
        gamma_ld = [sem(f"gamma_loaded{i}") for i in range(2)]
        x_loaded = sem("x_loaded")
        txt_loaded = sem("txt_loaded")
        g_full = sem("generic_bank_full")
        act_read = sem("act_read")
        sc_full = sem("scores_full")
        mix_done = sem("mixed_ready")
        ret_mm = sem("retained_added")
        prelu_done = sem("prelu_done")
        ln = sem("norm_step")
        sq_root = sem("square_root")
        neg_done = sem("prelu_negative_part")
        gamma_turned = sem("gamma_turned")
        keys_copied = sem("keys_copied")
        gamma_a = sem("gamma_copied_scalar")
        gamma_v = sem("gamma_copied_vector")
        stored = [sem(f"stored{i}") for i in range(4)]
        phase_end = sem("phase_end")
        xc_ld = [sem(f"xc_loaded{i}") for i in range(2)]
        zs_ld = sem("zs_loaded")
        raw_full = sem("raw_delta_full")
        abs_done = sem("abs_done")
        relu_done = sem("relu_done")
        exp_done = sem("softplus_exp_done")
        ln_done = sem("softplus_ln_done")
        delta_ready = sem("delta_ready")
        du_ready = sem("du_ready")
        rep_full = sem("bc_rep_full")
        part1 = sem("first_part")
        rest_done = sem("rest")
        part2 = sem("second_part")
        parts_ready = sem("parts_ready")
        b_full = sem("b_broadcast")
        c_full = sem("c_broadcast")
        c_copied = sem("c_copied")
        decay_ready = sem("decay_ready")
        drive_done = sem("drive_done")
        scanned = sem("scanned")
        part_done = sem("c_product")
        summed = sem("state_summed")
        skip_done = sem("skip_added")
        gated = sem("gated")
        out_full = sem("out_full")
        added = sem("added")
        n3 = sem("norm_step3")
        sq_done = sem("squared3")
        root3 = sem("root3")
        t3 = sem("turned3")
        xt3 = sem("xl_turned_copied")
        m3 = sem("ring_full3")
        r3 = sem("ring_read3")
        wt3 = sem("weights_turned3")
        wc3 = sem("weights_column3")
        cmp3 = sem("compared3")
        rk3 = sem("ranks_full3")
        y3 = sem("ffn_turned3")
        f3 = sem("final_step3")
        sum3 = sem("residual_sum3")
        out3 = sem("out_ready3")
        thr3 = sem("threshold_step3")
        o3 = [sem(f"out_stored{i}") for i in range(2)]

        block = ctx.enter_context(nc.Block())

        def tok(b):
            if isinstance(b, int):
                return resid[:, b, :, :]
            return resid[:, bass.ds(b, 1), :, :].rearrange("p o t d -> p (o t) d")

        def dram_batch(ap, b):
            if isinstance(b, int):
                return ap[b]
            return ap[bass.ds(b, 1)].rearrange("o a p t -> (o a) p t")

        def dram_b3(ap, b):
            if isinstance(b, int):
                return ap[b]
            return ap[bass.ds(b, 1)].rearrange("o t d -> (o t) d")

        def end_phase(eng, n):
            eng.sem_inc(phase_end, 1)
            eng.wait_ge(phase_end, 5 * n)

        G = {u: bank[5 + i % 3] for i, u in enumerate(SEQUENCE)}
        RT = bank[4]

        def wait_bank(eng, b, use):
            sequence = uses(where_is(b))
            for body, earlier in ((b, sequence[:sequence.index(use)]), (b - 1, uses(where_is(b - 1)))):
                same = [u for u in earlier if G[u] is G[use]]
                if same and same[-1] == "P":
                    return at_least(eng, prelu_done, body + 1)
                if same:
                    return at_least(eng, act_read, act_value(body, READS[same[-1]][-1]))
                if isinstance(b, int) and b == -1:
                    return

        PRE = ("fw", "bw")
        WEIGHTS = 40

        def nth(b, d):
            return 2 * b + d

        def at(b, d, step):
            return b + (d + step) // 2, (d + step) % 2

        def state_before(b, d, n, back):
            m = n - back
            return (*at(b, d, m // NS), m % NS)

        def side_bank(b, d, at_first):
            return bank[at_first] if isinstance(b, int) and (b, d) == (0, 0) else bank[7]

        @block.sync
        def _(sp):
            jobs = [
                (w_qk[0:DM, 0:DM], T["L0_tok_Wq"]), (w_qk[0:DM, DM:2 * DM], T["L0_tok_Wk"]),
                (w_qk[DM:DM + 1, 0:DM], T["L0_tok_bq"].rearrange("(a d) -> a d", a=1)),
                (w_qk[DM:DM + 1, DM:2 * DM], T["L0_tok_bk"].rearrange("(a d) -> a d", a=1)),
                (w_v[0:DM, :], T["L0_tok_Wv"]),
                (w_v[DM:DM + 1, :], T["L0_tok_bv"].rearrange("(a d) -> a d", a=1)),
                (w_o[:, :], T["L0_tok_Wo"]),
                (w_vo[DM + 1:DM + 2, :], T["L0_tok_bo"].rearrange("(a d) -> a d", a=1)),
                (slope_in[:, :], T["L0_tok_prelu_a"]),
                (w_1[:, :], T["L0_ffn_w1"]),
                (b_1[:, 0:1], T["L0_ffn_b1"][0:P].rearrange("(p a) -> p a", a=1)),
                (b_1[:, 1:2], T["L0_ffn_b1"][P:HID].rearrange("(p a) -> p a", a=1)),
                (w_2[:, :, 0:DM], T["L0_ffn_w2"].rearrange("(g p) d -> p g d", p=P)),
                (w_2[:, :, DM:P], T["L0_ffn_w2"].rearrange("(g p) d -> p g d", p=P)),
                (b_2[0:DM, :], T["L0_ffn_b2"].rearrange("(p a) -> p a", a=1)),
                (b_2[DM:P, :], T["L0_ffn_b2"].rearrange("(p a) -> p a", a=1)),
                (w_r[0:DM, :], T["L0_ffn_wr"]),
                (w_r[DM:DM + 1, :], T["L0_ffn_br"].rearrange("(a d) -> a d", a=1)),
            ]
            for d, pre in enumerate(PRE):
                def t(name):
                    return T[f"L0_attn_{pre}_{name}"]

                def col(ap):
                    return ap.rearrange("(p a) -> p a", a=1)

                jobs += [
                    (in_w[:, d, :, :], t("in_proj").rearrange("(h p) i -> p h i", p=DI)),
                    (conv_w[:, d, :], t("conv_w")),
                    (vecs[:, d, CB:CB + 1], col(t("conv_b"))),
                    (vecs[:, d, DTB:DTB + 1], col(t("dt_b"))),
                    (vecs[:, d, DSK:DSK + 1], col(t("D"))),
                    (vecs[0:DM, d, NRM:NRM + 1], col(t("norm"))),
                    (vecs[DM:P, d, NRM:NRM + 1], col(t("norm"))),
                    (a_log[:, d, :], t("A_log")),
                    (xp_w[:, d, :], t("x_proj")),
                    (dt_w[:, d, :], t("dt_w")),
                    (op_w[:, d, :], t("out_proj")),
                ]
            assert len(jobs) == WEIGHTS
            for t in range(NI):
                if t >= 2:
                    sp.wait_ge(gamma_turned, 2 * (t - 1))
                sp.dma_start(gamma_in[:, t % 2, :], T["L0_tok_d_gamma_batched"][t * P:(t + 1) * P, :])\
                    .then_inc(gamma_ld[t % 2], 16)
                for dst, src in jobs[t * WEIGHTS // NI:(t + 1) * WEIGHTS // NI]:
                    sp.dma_start(dst, src).then_inc(wl, 16)

            def x_load(b):
                src = T["x"][b, 0] if isinstance(b, int) else \
                    T["x"][bass.ds(b, 1)].rearrange("o a t d -> (o a t) d")
                if not (isinstance(b, int) and b == 0):
                    sp.wait_ge(g_full, g_value(b - 2, "x1"))
                    sp.wait_ge(keys_copied, b)
                sp.dma_start(x_in, src.rearrange("(t p) d -> p t d", p=P)).then_inc(x_loaded, 16)

            def stores(body):
                for q in range(12):
                    d, c, z = q // 6, (q % 6) // 2, q % 2
                    sp.wait_ge(act_read, act_value(body, f"s{q}"))
                    dst = dram_batch(gate_dram if z else conv_dram, body - 1)[d, :, c * CH:(c + 1) * CH]
                    sp.dma_start(dst, staged[:, q % 4, :]).then_inc(stored[q % 4], 16)

            for b in range(3):
                x_load(b)
            stores(1)
            x_load(3)
            with sp.Fori(4, NB) as b:
                stores(b - 2)
                x_load(b)
            for body in range(NB - 2, NB + 1):
                stores(body)
            def xc_load(b, d):
                at_least(sp, skip_done, NC * (nth(b, d) - 1))
                sp.dma_start(xc_in[:, d, :], dram_batch(conv_dram, b)[d]).then_inc(xc_ld[d], 16)

            def zs_load(b, d):
                at_least(sp, gated, nth(b, d))
                sp.dma_start(zs_in[:, :], dram_batch(gate_dram, b)[d]).then_inc(zs_ld, 16)

            for s in stored:
                sp.wait_ge(s, 16 * 3 * NB)
            xc_load(0, 0)
            xc_load(0, 1)
            end_phase(sp, 1)
            for d in range(2):
                zs_load(0, d)
                xc_load(1, d)
            with sp.Fori(1, NB - 1) as b:
                for d in range(2):
                    zs_load(b, d)
                    xc_load(b + 1, d)
            for d in range(2):
                zs_load(NB - 1, d)
            end_phase(sp, 2)

            def store(p, u):
                sp.wait_ge(out3, 2 * p + u + 1)
                sp.dma_start(dram_b3(out, 2 * p + u).rearrange("(t p) d -> p t d", p=P), y_out[u])\
                    .then_inc(o3[u], 16)

            with sp.Fori(0, NB // 2) as p:
                for u in range(2):
                    store(p, u)
            for u in range(2):
                sp.wait_ge(o3[u], 16 * NB // 2)

        @block.gpsimd
        def _(pool):
            g = nc.gpsimd
            g.memset(ident[:, :], 0.0).then_inc(s_id, 1)
            pool.wait_ge(s_id, 1)
            g.affine_select(out=ident[:, :], in_=ident[:, :], compare_op=ALU.not_equal, fill=1.0,
                            base=0, pattern=[[-1, P]], channel_multiplier=1).then_inc(s_id, 1)
            for b in range(NB):
                pool.dma_start(resid[:, b, NI:NT, :], T["txt"][b].rearrange("(t p) d -> p t d", p=P))\
                    .then_inc(txt_loaded, 16)
            g.memset(ones_row[:, :], 1.0).then_inc(const, 1)
            g.memset(x_pair[:, :], 0.0)
            g.memset(ones_b[:, :], 1.0)
            g.memset(zero_b[:, :], 0.0)
            g.memset(pick[:, :, :], 0.0)
            g.memset(before[:, :], 1.0).then_inc(const, 1)
            pool.wait_ge(const, 2)
            g.affine_select(out=before[:, :], in_=before[:, :], compare_op=ALU.is_gt, fill=0.0,
                            base=0, pattern=[[1, P]], channel_multiplier=-1).then_inc(const, 1)
            for part in range(3):
                g.affine_select(out=pick[:, :, :], in_=pick[:, :, :], compare_op=ALU.not_equal,
                                fill=1.0, base=-32 * part, pattern=[[-1, 2 * NS], [0, P]],
                                channel_multiplier=1).then_inc(const, 1)
                pool.wait_ge(const, 4 + part)
            pool.wait_ge(txt_loaded, 16 * NB)
            end_phase(pool, 1)

            def split(b, d, c):
                i = NC * nth(b, d) + c
                slot = (d + c) % 2
                pool.wait_ge(rest_done, i + 1)
                g.tensor_tensor(high[:, slot, :], rest[:, slot, :], part_mask[:, 1:2].to_broadcast([96, CH]),
                                ALU.mult).then_inc(part2, 1)
                pool.wait_ge(part2, i + 1)
                at_least(pool, c_full, PS * (nth(b, d) - 1))
                g.tensor_tensor(parts[:, d, c * CH:(c + 1) * CH], rest[:, slot, :], high[:, slot, :],
                                ALU.subtract)\
                    .then_inc(parts_ready, 1)

            def gate(b, d):
                i = nth(b, d)
                pool.wait_ge(skip_done, NC * (i + 1))
                pool.wait_ge(zs_ld, 16 * (i + 1))
                g.tensor_tensor(y_skip[:, :], y_skip[:, :], zs_in[:, :], ALU.mult).then_inc(gated, 1)

            def c_product(b, d, n):
                i = NS * nth(b, d) + n
                pool.wait_ge(scanned, i + 1)
                pool.wait_ge(c_copied, NC * (i + 1))
                at_least(pool, summed, NC * (i - 3))
                g.tensor_tensor(y_part[:, n % 4, :], h[:, n % 2, :], c_all[:, n % 2, :], ALU.mult)\
                    .then_inc(part_done, 1)

            def direction(b, d, back=True, ahead=True):
                for n in range(NS):
                    if n - SPLIT_AT - 1 in range(NC) and ahead:
                        split(*at(b, d, 1), n - SPLIT_AT - 1)
                    if n == GATE_AT and back:
                        gate(*at(b, d, -1))
                    c_product(b, d, n)

            def squares(p, u):
                b = 2 * p + u
                pool.wait_ge(n3, NORM3_OPS * b + 4)
                g.tensor_tensor(sq3, xl[u], xl[u], ALU.mult).then_inc(sq_done, 1)

            def residual_sum(p, u):
                b = 2 * p + u
                pool.wait_ge(n3, NORM3_OPS * (b + 1))
                g.tensor_tensor(x_sum[u], x3[u], xl[u], ALU.add).then_inc(sum3, 1)

            for c in range(NC):
                split(0, 0, c)
            direction(0, 0, back=False)
            direction(0, 1)
            with pool.Fori(1, NB - 1) as b:
                for d in range(2):
                    direction(b, d)
            direction(NB - 1, 0)
            direction(NB - 1, 1, ahead=False)
            squares(0, 0)
            gate(NB - 1, 1)
            residual_sum(0, 0)
            pool.wait_ge(gated, 2 * NB)
            end_phase(pool, 2)

            def output(p, u):
                b = 2 * p + u
                pool.wait_ge(f3, FINAL_OPS * (b + 1))
                pool.wait_ge(sum3, b + 1)
                g.tensor_tensor(y_out[u], y_out[u], x_sum[u], ALU.add).then_inc(out3, 1)

            def pair(p, last=False):
                for u in range(2):
                    if not (last and u):
                        squares(p + u, 1 - u)
                        residual_sum(p + u, 1 - u)
                    output(p, u)

            pair(0)
            with pool.Fori(1, NB // 2 - 1) as p:
                pair(p)
            pair(NB // 2 - 1, last=True)

        @block.scalar
        def _(act):
            a = nc.scalar
            for t in range(NI):
                act.wait_ge(gamma_turned, 2 * t + 1)
                a.activation(gamma_t[:, 0:4, t * P:(t + 1) * P],
                             bank[2 * t % 4][:, :].rearrange("p (s t) -> p s t", s=4), ACT.Copy)\
                    .then_inc(gamma_a, 1)

            act.wait_ge(wl, 16 * WEIGHTS)
            act.wait_ge(masks, 2)
            a.activation(a_neg[:, :, :], a_log[:, :, :], ACT.Exp).then_inc(prep_e, 1)
            act.wait_ge(const, 1)

            def tiles_of(ap, i, odd):
                return ap[0:DM, i * 512:(i + 1) * 512].rearrange("p (t o q) -> p t o q", o=2, q=P)[:, :, odd, :]

            def paired(ps, odd):
                return ps[DM * odd:DM * (odd + 1), 0:2 * P].rearrange("p (t q) -> p t q", q=P)

            def item(i, dst, src, scale=None):
                act.wait_ge(prep_p, i + 1)
                if scale is None:
                    return a.activation(dst, src, ACT.Copy)
                return a.activation(dst, src, ACT.Copy, scale=scale)

            for d in range(2):
                i = 7 * d
                bk = [bank[4 + (i + e) % 4] for e in range(7)]
                for p in range(2):
                    item(i + p, conv_t[:, d, p, :], bk[p][:, 0:P], vecs[:, d, NRM:NRM + 1]).then_inc(prep_a, 1)
                item(i + 2, gate_t[:, d, :], bk[2][0:DM, 0:P], vecs[0:DM, d, NRM:NRM + 1]).then_inc(prep_a, 1)
                for part in range(3):
                    last = item(i + 3, bc_rep[:, d, 32 * part:32 * (part + 1)], bk[3][:, RK:RK + 2 * NS])
                last.then_inc(prep_a, 1)
                item(i + 4, dtw_t[:, d, :], bk[4][0:RK, 0:P]).then_inc(prep_a, 1)
                item(i + 5, delta_t[:, d, :], bk[5][:, 0:P]).then_inc(prep_a, 1)
                item(i + 6, out_t[:, d, :], bk[6][:, 0:DM]).then_inc(prep_a, 1)
            item(14, slope[:, :], bank[4 + 14 % 4][:, 0:1]).then_inc(prep_a, 1)
            item(15, w_vt[:, :], bank[4 + 15 % 4][0:DM, 0:DM + 1]).then_inc(prep_a, 1)
            item(16, w_vo[0:DM + 1, :], bank[4 + 16 % 4][0:DM + 1, 0:DM]).then_inc(prep_a, 1)
            def read(b, use, *copies):
                act.wait_ge(g_full, g_value(b, use))
                for dst, src in copies:
                    a.activation(dst, src, ACT.Copy).then_inc(act_read, 1)

            def turned(b, i):
                u = f"x{i}"
                read(b, u, *((tiles_of(x_t, i, odd), paired(G[u], odd)) for odd in range(2)))

            def queries_keys(b, c):
                u, cols = f"q{c}", slice(c * 512, (c + 1) * 512)
                read(b, u, (q_t[:, cols], G[u][0:DM, :]), (k_t[:, cols], G[u][DM:P, :]))

            def roots(b):
                act.wait_ge(ln, LN_OPS * b + 8)
                a.activation(stat[:, SD, :], stat[:, VE, :], ACT.Sqrt).then_inc(sq_root, 1)
                act.wait_ge(ln, LN_OPS * b + 12)
                a.activation(stat[:, SD2, :], stat[:, ME, :], ACT.Sqrt).then_inc(sq_root, 1)

            def retained(b):
                for h in range(2):
                    act.wait_ge(ret_mm, 2 * NI * b + NI * (h + 1))
                    a.activation(r_t[0:DM + 1, h * 512:(h + 1) * 512], RT[0:DM + 1, :], ACT.Copy)\
                        .then_inc(act_read, 1)

            def normed(b):
                for i, u in enumerate(NORMED):
                    read(b, u, (x_pair[0:DM, 3 + i * 512:3 + (i + 1) * 512], G[u][0:DM, :]),
                         (x_pair[DM:P, 2 + i * 512:2 + (i + 1) * 512], G[u][DM:P, :]))

            def silu(b, q):
                u, d = CONVS[q], q // 6
                act.wait_ge(g_full, g_value(b, u))
                at_least(act, stored[q % 4], 16 * (3 * (b - 1) + q // 4))
                bias = 0.0 if q % 2 else vecs[:, d, CB:CB + 1]
                a.activation(staged[:, q % 4, :], G[u][:, :], ACT.Silu, bias=bias).then_inc(act_read, 1)

            def body(b):
                where = where_is(b)
                if "X" in PARTS[where]:
                    roots(b - 1)
                if "P" in PARTS[where]:
                    retained(b)
                if "X" in PARTS[where]:
                    normed(b)
                for u in uses(where):
                    {"x": turned, "q": queries_keys, "s": silu}.get(u[0], lambda *_: None)(b, int(u[1:] or 0))

            for b in (-1, 0, 1):
                body(b)
            with act.Fori(2, NB - 1) as b:
                body(b)
            for b in (NB - 1, NB):
                body(b)
            act.wait_ge(act_read, act_value(NB, "s11"))
            end_phase(act, 1)

            def root(p, u):
                act.wait_ge(n3, NORM3_OPS * (2 * p + u) + 6)
                a.activation(stat3[:, u, SD, :], stat3[:, u, VE, :], ACT.Sqrt).then_inc(root3, 1)

            def raw_abs(b, d, c):
                i = NC * nth(b, d) + c
                act.wait_ge(raw_full, i + 1)
                at_least(act, delta_ready, NC * nth(b, d))
                a.activation(soft[:, c * CH:(c + 1) * CH], side_bank(b, d, 4 + c)[:, :], ACT.Abs,
                             bias=vecs[:, d, DTB:DTB + 1]).then_inc(abs_done, 1)

            def raw_relu(b, d, c):
                a.activation(delta[:, d, c * CH:(c + 1) * CH], side_bank(b, d, 4 + c)[:, :], ACT.Relu,
                             bias=vecs[:, d, DTB:DTB + 1]).then_inc(relu_done, 1)

            def soft_exp(b, d, c):
                act.wait_ge(abs_done, NC * nth(b, d) + c + 1)
                a.activation(soft[:, c * CH:(c + 1) * CH], soft[:, c * CH:(c + 1) * CH], ACT.Exp, scale=-1.0)\
                    .then_inc(exp_done, 1)

            def soft_log(b, d, c):
                act.wait_ge(exp_done, NC * nth(b, d) + c + 1)
                a.activation(soft[:, c * CH:(c + 1) * CH], soft[:, c * CH:(c + 1) * CH], ACT.Ln, bias=1.0)\
                    .then_inc(ln_done, 1)

            def first_part(b, d, c):
                i = NC * nth(b, d) + c
                act.wait_ge(rep_full, i + 1)
                at_least(act, parts_ready, i - 1)
                a.activation(high[:, (d + c) % 2, :], side_bank(b, d, 1 + c)[0:96, :], ACT.Copy,
                             scale=part_mask[:, 0:1])\
                    .then_inc(part1, 1)

            def decays(b, d, n):
                i = NS * nth(b, d) + n
                act.wait_ge(delta_ready, NC * (nth(b, d) + 1))
                at_least(act, scanned, i - 1)
                a.activation(decay[:, n % 2, :], delta[:, d, :], ACT.Exp, scale=a_neg[:, d, n:n + 1])\
                    .then_inc(decay_ready, 1)

            def direction(b, d, ahead=True):
                for n in range(NS):
                    i = NS * nth(b, d) + n
                    for c in range(NC):
                        j = NC * i + c
                        act.wait_ge(c_full, j + 1)
                        at_least(act, part_done, i - 1)
                        a.activation(c_all[:, n % 2, c * CH:(c + 1) * CH], bank[2 + (NC * n + c) % 2][:, :],
                                     ACT.Copy).then_inc(c_copied, 1)
                        if c == DECAY_AT:
                            if n + 1 < NS:
                                decays(b, d, n + 1)
                            elif ahead:
                                decays(*at(b, d, 1), 0)
                        if not ahead:
                            continue
                        if c == 0 and n - DELTA_AT - 1 in range(NC):
                            raw_relu(*at(b, d, 1), n - DELTA_AT - 1)
                        if c == 0 and n - SOFT_AT in range(NC):
                            soft_exp(*at(b, d, 1), n - SOFT_AT)
                        if c == 1 and n - SOFT_AT in range(NC):
                            soft_log(*at(b, d, 1), n - SOFT_AT)
                        if c == 2 and n - DELTA_AT in range(NC):
                            raw_abs(*at(b, d, 1), n - DELTA_AT)
                        if c == 2 and n - SPLIT_AT in range(NC):
                            first_part(*at(b, d, 1), n - SPLIT_AT)

            nc.scalar.preload_act_table_set("natural_log_exp_and_others")
            for c in range(NC):
                raw_abs(0, 0, c)
                raw_relu(0, 0, c)
                first_part(0, 0, c)
                soft_exp(0, 0, c)
                soft_log(0, 0, c)
            decays(0, 0, 0)
            direction(0, 0)
            direction(0, 1)
            with act.Fori(1, NB - 1) as b:
                for d in range(2):
                    direction(b, d)
            direction(NB - 1, 0)
            direction(NB - 1, 1, ahead=False)
            root(0, 0)
            act.wait_ge(c_copied, PS * 2 * NB)
            end_phase(act, 2)

            def front(p, u):
                b = 2 * p + u
                for i in range(3):
                    act.wait_ge(t3, 3 * b + i + 1)
                    for odd in range(2):
                        a.activation(tiles_of(xl_t, i, odd), paired(bank[TURNED[i]], odd), ACT.Copy).then_inc(xt3, 1)
                for k in range(9):
                    act.wait_ge(m3, RING3 * b + k + 1)
                    if k < 3:
                        if k == 0:
                            at_least(act, cmp3, NT * (b - 1))
                        a.activation(w_row[u][:, k * 512:(k + 1) * 512], bank[2 + k % 3][:, :], ACT.Copy)\
                            .then_inc(r3, 1)
                    else:
                        c, hg = divmod(k - 3, 2)
                        a.activation(hid[:, hg, c * 512:(c + 1) * 512], bank[2 + k % 3][:, :],
                                     ACT.Gelu_apprx_tanh, bias=b_1[:, hg:hg + 1]).then_inc(r3, 1)

            def back(p, u):
                b = 2 * p + u
                for k in range(9, RING3):
                    c = k - 9
                    act.wait_ge(m3, RING3 * b + k + 1)
                    for odd in range(2):
                        rows = slice(DM * odd, DM * (odd + 1))
                        last = a.activation(
                            y_t[rows, c * 256:(c + 1) * 256].rearrange("p (t q) -> p t q", q=P),
                            bank[2 + k % 3][rows, :].rearrange("p (t o q) -> p t o q", o=2, q=P)[:, :, odd, :],
                            ACT.Identity, bias=b_2[rows, 0:1])
                    last.then_inc(r3, 1)

            def pair(p, last=False):
                for u in range(1 if last else 2):
                    front(p + u, 1 - u)
                    if not last:
                        root(p + 1, u)
                    back(p + u, 1 - u)

            front(0, 0)
            root(0, 1)
            back(0, 0)
            pair(0)
            with act.Fori(1, NB // 2 - 1) as p:
                pair(p)
            pair(NB // 2 - 1, last=True)

        @block.tensor
        def _(pe):
            t_ = nc.tensor

            def mm(o, lhsT, rhs, start=True, stop=True, **kw):
                return t_.matmul(o, lhsT, rhs, start=start, stop=stop, **kw)

            pe.wait_ge(s_id, 2)
            for t in range(NI):
                pe.wait_ge(gamma_ld[t % 2], 16 * (t // 2 + 1))
                for h in range(2):
                    if t >= 2:
                        pe.wait_ge((gamma_a, gamma_v)[h], t - 1)
                    for s in range(4):
                        last = t_.transpose(bank[(2 * t + h) % 4][:, s * P:(s + 1) * P],
                                            gamma_in[:, t % 2, (4 * h + s) * P:(4 * h + s + 1) * P],
                                            ident[:, :])
                    last.then_inc(gamma_turned, 1)
            pe.wait_ge(wl, 16 * WEIGHTS)
            pe.wait_ge(const, 1)
            for d in range(2):
                i = 7 * d
                bk = [bank[4 + (i + e) % 4] for e in range(7)]

                def ready(e, i=i):
                    at_least(pe, prep_a, i + e - 3)
                pe.wait_ge(prep_v, 4 * d + 4)
                for p in range(2):
                    ready(p)
                    t_.transpose(bk[p][:, 0:P], tap_w[:, d, 2 * p:2 * p + 2, :].rearrange("p k i -> p (k i)"),
                                 ident[:, :]).then_inc(prep_p, 1)
                ready(2)
                t_.transpose(bk[2][0:DM, 0:P], in_w[:, d, 1, :], ident[:, :]).then_inc(prep_p, 1)
                ready(3)
                nx = RK + 2 * NS
                t_.transpose(bk[3][:, 0:nx], xp_w[:, d, :], ident[0:nx, 0:nx]).then_inc(prep_p, 1)
                ready(4)
                t_.transpose(bk[4][0:RK, 0:P], dt_w[:, d, :], ident[:, :]).then_inc(prep_p, 1)
                pe.wait_ge(prep_a, i + 5)
                mm(bk[5][:, 0:P], xp_w[0:RK, d, :], dtw_t[:, d, :]).then_inc(prep_p, 1)
                ready(6)
                t_.transpose(bk[6][:, 0:DM], op_w[:, d, :], ident[0:DM, 0:DM]).then_inc(prep_p, 1)
            at_least(pe, prep_a, 14 - 3)
            mm(bank[4 + 14 % 4][:, 0:1], ones_row[:, :], slope_in[:, :]).then_inc(prep_p, 1)
            pe.wait_ge(prep_a, 15 - 3)
            t_.transpose(bank[4 + 15 % 4][0:DM, 0:DM + 1], w_v[:, :], ident[0:DM + 1, 0:DM + 1]).then_inc(prep_p, 1)
            pe.wait_ge(prep_a, 16)
            mm(bank[4 + 16 % 4][0:DM + 1, 0:DM], w_vt[:, :], w_o[:, :]).then_inc(prep_p, 1)
            pe.wait_ge(prep_a, PREP)
            pe.wait_ge(const, 6)
            pe.wait_ge(masks, 2)
            pe.wait_ge(gamma_a, NI)
            pe.wait_ge(gamma_v, NI)

            def turned(b, i):
                u = f"x{i}"
                pe.wait_ge(x_loaded, 16 * (b + 2))
                wait_bank(pe, b, u)
                for k in range(2):
                    t = 4 * i + 2 * k
                    last = t_.transpose(G[u][:, k * P:(k + 1) * P],
                                        x_in[:, t:t + 2, :].rearrange("p t d -> p (t d)"), ident[:, :])
                last.then_inc(g_full, 1)

            def queries_keys(b, c):
                u = f"q{c}"
                wait_bank(pe, b, u)
                pe.wait_ge(act_read, act_value(b, f"x{c}u"))
                mm(G[u][:, :], w_qk[:, :], x_t[0:DM + 1, c * 512:(c + 1) * 512]).then_inc(g_full, 1)

            def mixer(b):
                pe.wait_ge(act_read, act_value(b - 1, "k1"))
                pe.wait_ge(keys_copied, b + 1)
                for j in range(2 * NI + 2):
                    if j < 2 * NI:
                        h, s = divmod(j, NI)
                        at_least(pe, mix_done, 2 * NI * b + j - 3)
                        mm(bank[j % 4][:, :], k_t[:, s * P:(s + 1) * P], q_t[:, h * 512:(h + 1) * 512])\
                            .then_inc(sc_full, 1)
                    if j >= 2:
                        i = j - 2
                        h, s = divmod(i, NI)
                        if s == 0:
                            if h:
                                pe.wait_ge(act_read, act_value(b, "r0"))
                            elif not (isinstance(b, int) and b == 0):
                                pe.wait_ge(act_read, act_value(b - 1, "r1"))
                        pe.wait_ge(mix_done, 2 * NI * b + i + 1)
                        mm(RT[0:DM + 1, :], x_keys[:, s, :], mixed[:, i % 4, :], start=s == 0, stop=s == NI - 1)\
                            .then_inc(ret_mm, 1)

            def normed(b, i):
                u = NORMED[i]
                pe.wait_ge(ln, LN_OPS * (b - 1) + 15)
                wait_bank(pe, b, u)
                for q in range(4):
                    last = t_.transpose(G[u][:, q * P:(q + 1) * P],
                                        x_rms[:, 4 * i + q, :, :].rearrange("p a d -> p (a d)"), ident[:, :])
                last.then_inc(g_full, 1)

            def conv(b, q):
                u, d, c, z = CONVS[q], q // 6, (q % 6) // 2, q % 2
                wait_bank(pe, b, u)
                pe.wait_ge(act_read, act_value(b, "X2u"))
                if z:
                    last = mm(G[u][:, :], gate_t[:, d, :], x_pair[0:DM, c * 512 + 3:c * 512 + 515])
                else:
                    o = c * 512 + (0 if d == 0 else 3)
                    mm(G[u][:, :], conv_t[:, d, 0, :], x_pair[:, o:o + 512], stop=False)
                    last = mm(G[u][:, :], conv_t[:, d, 1, :], x_pair[:, o + 2:o + 514], start=False)
                last.then_inc(g_full, 1)

            def proj(b, _):
                wait_bank(pe, b, "P")
                pe.wait_ge(act_read, act_value(b, "r1"))
                for i in range(NI):
                    last = mm(G["P"][:, i * DM:(i + 1) * DM], r_t[0:DM + 2, i * P:(i + 1) * P], w_vo[:, :])
                last.then_inc(g_full, 1)

            def body(b):
                if "P" in PARTS[where_is(b)]:
                    mixer(b)
                for u in uses(where_is(b)):
                    {"X": normed, "P": proj, "s": conv, "x": turned, "q": queries_keys}[u[0]](b, int(u[1:] or 0))

            for b in (-1, 0, 1):
                body(b)
            with pe.Fori(2, NB - 1) as b:
                body(b)
            for b in (NB - 1, NB):
                body(b)
            pe.wait_ge(g_full, g_value(NB, "s11"))
            end_phase(pe, 1)

            def delta_mm(b, d, c):
                i, o = nth(b, d), side_bank(b, d, 4 + c)
                if c == 0:
                    pe.wait_ge(xc_ld[d], 16 * (b + 1))
                    at_least(pe, added, 2 * (i - 1))
                elif o is bank[7]:
                    pe.wait_ge(relu_done, NC * i + c)
                mm(o[:, :], delta_t[:, d, :], xc_in[:, d, c * CH:(c + 1) * CH]).then_inc(raw_full, 1)

            def rep_mm(b, d, c):
                i, o = nth(b, d), side_bank(b, d, 1 + c)
                if c == 0 and o is bank[7]:
                    pe.wait_ge(relu_done, NC * (i + 1))
                elif o is bank[7]:
                    pe.wait_ge(rest_done, NC * i + c)
                mm(o[0:96, :], bc_rep[:, d, :], xc_in[:, d, c * CH:(c + 1) * CH]).then_inc(rep_full, 1)

            def out_mm(b, d, part):
                i = nth(b, d)
                if part == 0:
                    pe.wait_ge(gated, i + 1)
                    last = isinstance(b, int) and i == 2 * NB - 1
                    pe.wait_ge(rest_done, NC * 2 * NB if last else NC * (i + 2))
                else:
                    pe.wait_ge(added, 2 * i + 1)
                for t in range(8 * part, min(8 * part + 8, NT)):
                    last = mm(bank[7][:, t % 8 * DM:(t % 8 + 1) * DM], y_skip[:, t * P:(t + 1) * P], out_t[:, d, :])
                last.then_inc(out_full, 1)

            def spread_b(b, d, j):
                i = nth(b, d)
                n, c = divmod(j, NC)
                if n == 0:
                    pe.wait_ge(parts_ready, NC * i + c + 1)
                at_least(pe, drive_done, PS * i + j - 1)
                mm(bank[j % 2][:, :], pick[:, n, :], parts[:, d, c * CH:(c + 1) * CH]).then_inc(b_full, 1)

            def spread_c(b, d, j):
                i = nth(b, d)
                n, c = divmod(j, NC)
                at_least(pe, c_copied, PS * i + j - 1)
                mm(bank[2 + j % 2][:, :], pick[:, NS + n, :], parts[:, d, c * CH:(c + 1) * CH]).then_inc(c_full, 1)

            def add_state(b, d, n, c):
                i = nth(b, d)
                if n == 0:
                    at_least(pe, skip_done, NC * (i - 1) + c + 1)
                if c == 0:
                    pe.wait_ge(part_done, NS * i + n + 1)
                mm(bank[4 + c][:, :], ident[:, :], y_part[:, n % 4, c * CH:(c + 1) * CH],
                   start=n == 0, stop=n == NS - 1).then_inc(summed, 1)

            def direction(b, d, back=True, ahead=True, scans=True):
                for n in range(NS if scans else LAG):
                    for c in range(NC):
                        j = NC * n + c
                        if scans and j + 1 < PS:
                            spread_b(b, d, j + 1)
                        elif scans and ahead:
                            spread_b(*at(b, d, 1), 0)
                        if scans:
                            spread_c(b, d, j)
                        if n >= LAG or back:
                            add_state(*state_before(b, d, n, LAG), c)
                        if c == 1 and n in (OUT_AT, OUT_AT + 1) and back and scans:
                            out_mm(*at(b, d, -1), n - OUT_AT)
                        if c == 1 and n - DELTA_AT in range(NC) and ahead:
                            delta_mm(*at(b, d, 1), n - DELTA_AT)
                        if c == 1 and n - SPLIT_AT in range(NC) and ahead:
                            rep_mm(*at(b, d, 1), n - SPLIT_AT)

            for c in range(NC):
                delta_mm(0, 0, c)
                rep_mm(0, 0, c)
            spread_b(0, 0, 0)
            direction(0, 0, back=False)
            direction(0, 1)
            with pe.Fori(1, NB - 1) as b:
                for d in range(2):
                    direction(b, d)
            direction(NB - 1, 0)
            direction(NB - 1, 1, ahead=False)
            direction(NB, 0, ahead=False, scans=False)
            for part in range(2):
                out_mm(NB - 1, 1, part)
            pe.wait_ge(out_full, 2 * 2 * NB)
            end_phase(pe, 2)

            def front(p, u):
                b = 2 * p + u
                pe.wait_ge(n3, NORM3_OPS * (b + 1))
                at_least(pe, wc3, b)
                at_least(pe, r3, RING3 * b)
                for i in range(3):
                    for q in range(2):
                        t = 4 * i + 2 * q
                        last = t_.transpose(bank[TURNED[i]][:, q * P:(q + 1) * P],
                                            xl[u][:, t:t + 2, :].rearrange("p t d -> p (t d)"), ident[:, :])
                    last.then_inc(t3, 1)
                for i in range(3):
                    pe.wait_ge(xt3, 6 * b + 2 * i + 2)
                    at_least(pe, r3, RING3 * b + i - 2)
                    mm(bank[2 + i][:, :], w_rr[:, :], xl_t[0:DM + 1, i * 512:(i + 1) * 512]).then_inc(m3, 1)

            def weights(p, u):
                b = 2 * p + u
                for t in range(NT):
                    if t % 4 == 0:
                        pe.wait_ge(r3, RING3 * b + t // 4 + 1)
                    last = t_.transpose(bank[1][:, 256 + t:256 + t + P], w_row[u][:, t * P:(t + 1) * P],
                                        ident[:, :])
                last.then_inc(wt3, 1)

            def ranks(p, u, tiles):
                b = 2 * p + u
                if 0 in tiles:
                    at_least(pe, f3, FINAL_OPS * (b - 1) + 3)
                    mm(bank[5][:, 0:NT], ones_b[:, :], zero_b[:, :], stop=False, skip_group_check=True)
                for j in tiles:
                    pe.wait_ge(cmp3, NT * b + j + 1)
                    for t in range(j, NT):
                        last = mm(bank[5][:, t:t + 1], higher[:, j, :][:, t * P:(t + 1) * P], ones_b[:, 0:1],
                                  start=False, stop=j == NT - 1, skip_group_check=True)
                if NT - 1 in tiles:
                    last.then_inc(rk3, 1)

            def back(p, u):
                b = 2 * p + u
                for k in range(3, 9):
                    c, hg = divmod(k - 3, 2)
                    pe.wait_ge(r3, RING3 * b + k - 2)
                    mm(bank[2 + k % 3][:, :], w_1[:, hg * P:(hg + 1) * P], xl_t[0:DM, c * 512:(c + 1) * 512])\
                        .then_inc(m3, 1)
                for k in range(9, RING3):
                    c, o = k - 9, bank[2 + k % 3][:, :]
                    pe.wait_ge(r3, RING3 * b + k - 2)
                    mm(o, w_2[:, 0, :], hid[:, 0, c * 512:(c + 1) * 512], stop=False)
                    mm(o, w_2[:, 1, :], hid[:, 1, c * 512:(c + 1) * 512], start=False).then_inc(m3, 1)
                at_least(pe, f3, FINAL_OPS * b)
                for t in range(0, NT, 2):
                    if t % 4 == 0:
                        pe.wait_ge(r3, RING3 * b + 10 + t // 4)
                    last = t_.transpose(bank[6 + t // 8][:, t % 8 * DM:(t % 8 + 2) * DM],
                                        y_t[:, t * DM:(t + 2) * DM], ident[:, :])
                last.then_inc(y3, 1)

            def pair(p, last=False):
                for u in range(2):
                    ranks(p, u, range(0, TURN_AT))
                    if not (last and u):
                        front(p + u, 1 - u)
                    ranks(p, u, range(TURN_AT, NT))
                    if not (last and u):
                        weights(p + u, 1 - u)
                        back(p + u, 1 - u)

            pe.wait_ge(masks, 3)
            front(0, 0)
            weights(0, 0)
            back(0, 0)
            pair(0)
            with pe.Fori(1, NB // 2 - 1) as p:
                pair(p)
            pair(NB // 2 - 1, last=True)

        @block.vector
        def _(dve):
            v = nc.vector
            v.memset(x_t[DM:DM + 1, :], 1.0)
            v.memset(r_t[DM:DM + 2, :], 1.0)
            v.memset(x_keys[:, :, DM:DM + 1], 1.0)
            v.memset(part_mask[0:96, 0:1], 1.0)
            v.memset(part_mask[0:96, 1:2], 0.0).then_inc(masks, 1)
            dve.wait_ge(masks, 1)
            v.memset(part_mask[0:32, 0:1], 0.0)
            v.memset(part_mask[64:96, 1:2], 1.0).then_inc(masks, 1)
            for t in range(NI):
                dve.wait_ge(gamma_turned, 2 * t + 2)
                v.tensor_copy(gamma_t[:, 4:8, t * P:(t + 1) * P],
                              bank[(2 * t + 1) % 4][:, :].rearrange("p (s t) -> p s t", s=4))\
                    .then_inc(gamma_v, 1)
            dve.wait_ge(wl, 16 * WEIGHTS)
            for d in range(2):
                for j in range(4):
                    tap = j if d == 0 else 3 - j
                    v.tensor_scalar(tap_w[:, d, j, :], in_w[:, d, 0, :], conv_w[:, d, tap:tap + 1], None,
                                    ALU.mult).then_inc(prep_v, 1)
            v.tensor_copy(w_rr[:, :], w_r[:, 0:1].to_broadcast([DM + 1, P])).then_inc(prep_v, 1)
            dve.wait_ge(prep_e, 1)
            v.tensor_scalar(a_neg[:, :, :], a_neg[:, :, :], -1.0, None, ALU.mult).then_inc(prep_v, 1)
            v.memset(row_sum[:, :, :], 0.0)
            dve.wait_ge(const, 3)
            v.tensor_reduce(later[:, :], before[:, :], AX_X, ALU.add).then_inc(thr3, 1)
            dve.wait_ge(thr3, 1)
            for j in range(NT):
                v.tensor_scalar(threshold[:, j:j + 1], later[:, :], -1.0, float(KK - (NT - 1 - j) * P),
                                ALU.mult, ALU.add).then_inc(thr3, 1)
            dve.wait_ge(thr3, 1 + NT)
            dve.wait_ge(prep_a, PREP)
            dve.wait_ge(gamma_a, NI)
            dve.wait_ge(txt_loaded, 16 * NB)

            def over(ap, n=DM):
                return ap.rearrange("p (t o) -> p t o", o=1).to_broadcast([P, NT, n])

            def prelu(b):
                dve.wait_ge(g_full, g_value(b, "P"))
                y = G["P"]
                v.tensor_scalar(neg_part[:, :], y[:, :], 0.0, slope[:, 0:1], ALU.min, ALU.mult).then_inc(neg_done, 1)
                dve.wait_ge(neg_done, b + 1)
                dst = tok(b)[:, 0:NI, :]
                v.scalar_tensor_tensor(dst, y[:, :].rearrange("p (t d) -> p t d", t=NI), 0.0,
                                       neg_part[:, :].rearrange("p (t d) -> p t d", t=NI), ALU.max, ALU.add)\
                    .then_inc(prelu_done, 1)


            def st(i):
                return stat[:, i, :]

            def norm_step(b, i):
                if i == -1:
                    dve.wait_ge(prelu_done, b + 1)
                else:
                    dve.wait_ge(ln, LN_OPS * b + i + 1)
                x = tok(b)
                if i == -1:
                    ins = v.tensor_scalar(x_mid, x, 1.0, None, ALU.mult)
                elif i == 0:
                    ins = v.tensor_reduce(st(S1), x_mid, AX_X, ALU.add)
                elif i == 1:
                    ins = v.tensor_scalar(st(MEAN), st(S1), 1.0 / DM, None, ALU.mult)
                elif i == 2:
                    ins = v.tensor_tensor(x_mid, x, over(st(MEAN)), ALU.subtract)
                elif i == 3:
                    ins = v.tensor_tensor(x_sq, x_mid, x_mid, ALU.mult)
                elif i == 4:
                    ins = v.tensor_reduce(st(S1), x_sq, AX_X, ALU.add)
                elif i == 5:
                    ins = v.tensor_scalar(st(VAR), st(S1), 1.0 / DM, None, ALU.mult)
                elif i == 6:
                    ins = v.tensor_scalar(st(VE), st(VAR), EPS, None, ALU.add)
                elif i == 7:
                    dve.wait_ge(sq_root, 2 * b + 1)
                    ins = v.reciprocal(st(RSTD), st(SD))
                elif i == 8:
                    ins = v.tensor_tensor(st(RR), st(RSTD), st(RSTD), ALU.mult)
                elif i == 9:
                    ins = v.tensor_tensor(st(RR), st(RR), st(VAR), ALU.mult)
                elif i == 10:
                    ins = v.tensor_scalar(st(ME), st(RR), EPS, None, ALU.add)
                elif i == 11:
                    dve.wait_ge(sq_root, 2 * b + 2)
                    ins = v.reciprocal(st(R2), st(SD2))
                elif i == 12:
                    ins = v.tensor_tensor(x_sq, x_mid, over(st(RSTD)), ALU.mult)
                elif i == 13:
                    for half in range(2):
                        ins = v.tensor_tensor(x_rms[:, :, half, :], x_sq, over(st(R2)), ALU.mult)
                else:
                    ins = v.scalar_tensor_tensor(x, x_sq, 2.0, x, ALU.mult, ALU.add)
                ins.then_inc(ln, 1)

            NORM_AT = {0: [-1, 0], 1: [1, 2], 2: [3], 3: [4], 4: [5, 6], 5: [7, 8, 9, 10], 7: [11, 12], 9: [13],
                       11: [14]}

            def mixer(b, prev=None):
                for j in range(2 * NI):
                    h, s = divmod(j, NI)
                    dve.wait_ge(sc_full, 2 * NI * b + j + 1)
                    at_least(dve, ret_mm, 2 * NI * b + j - 3)
                    v.tensor_tensor(mixed[:, j % 4, :], gamma_t[:, s, h * 512:(h + 1) * 512], bank[j % 4][:, :],
                                    ALU.mult).then_inc(mix_done, 1)
                    if prev is not None:
                        for i in NORM_AT.get(j, []):
                            norm_step(prev, i)

            def keys(b):
                dve.wait_ge(x_loaded, 16 * (b + 1))
                at_least(dve, ret_mm, 2 * NI * b)
                v.tensor_copy(x_keys[:, :, 0:DM], x_in).then_inc(keys_copied, 1)

            keys(0)
            mixer(0)
            keys(1)
            prelu(0)
            mixer(1, 0)
            with dve.Fori(2, NB) as b:
                keys(b)
                prelu(b - 1)
                mixer(b, b - 1)
            prelu(NB - 1)
            for i in range(-1, LN_OPS - 1):
                norm_step(NB - 1, i)
            dve.wait_ge(ln, LN_OPS * NB)
            end_phase(dve, 1)

            def norm3(p, u, i):
                b = 2 * p + u
                at_least(dve, n3, NORM3_OPS * b + i)

                def s3(k):
                    return stat3[:, u, k, :]
                if i == 0:
                    at_least(dve, sum3, b - 1)
                    ins = v.tensor_scalar(x3[u], tok(b), 1.0, None, ALU.mult)
                elif i == 1:
                    ins = v.tensor_reduce(s3(S1), x3[u], AX_X, ALU.add)
                elif i == 2:
                    ins = v.tensor_scalar(s3(MEAN), s3(S1), 1.0 / DM, None, ALU.mult)
                elif i == 3:
                    ins = v.tensor_tensor(xl[u], x3[u], over(s3(MEAN)), ALU.subtract)
                elif i == 4:
                    dve.wait_ge(sq_done, b + 1)
                    ins = v.tensor_reduce(s3(S1), sq3, AX_X, ALU.add)
                elif i == 5:
                    ins = v.tensor_scalar(s3(VE), s3(S1), 1.0 / DM, EPS, ALU.mult, ALU.add)
                elif i == 6:
                    dve.wait_ge(root3, b + 1)
                    ins = v.reciprocal(s3(RSTD), s3(SD))
                else:
                    ins = v.tensor_tensor(xl[u], xl[u], over(s3(RSTD)), ALU.mult)
                ins.then_inc(n3, 1)

            def finish_delta(b, d, c):
                i = NC * nth(b, d) + c
                dve.wait_ge(ln_done, i + 1)
                dve.wait_ge(relu_done, i + 1)
                chunk = delta[:, d, c * CH:(c + 1) * CH]
                v.tensor_tensor(chunk, chunk, soft[:, c * CH:(c + 1) * CH], ALU.add).then_inc(delta_ready, 1)

            def delta_x(b, d, c):
                dve.wait_ge(delta_ready, NC * nth(b, d) + c + 1)
                dve.wait_ge(xc_ld[d], 16 * (b + 1))
                v.tensor_tensor(du[:, d, c * CH:(c + 1) * CH], delta[:, d, c * CH:(c + 1) * CH],
                                xc_in[:, d, c * CH:(c + 1) * CH], ALU.mult).then_inc(du_ready, 1)

            def less_first(b, d, c):
                i = NC * nth(b, d) + c
                dve.wait_ge(part1, i + 1)
                at_least(dve, parts_ready, i - 1)
                slot = (d + c) % 2
                v.tensor_tensor(rest[:, slot, :], side_bank(b, d, 1 + c)[0:96, :], high[:, slot, :], ALU.subtract)\
                    .then_inc(rest_done, 1)

            def product(b, d, n, c):
                j = NC * n + c
                if n == 0:
                    dve.wait_ge(du_ready, NC * nth(b, d) + c + 1)
                dve.wait_ge(b_full, PS * nth(b, d) + j + 1)
                v.tensor_tensor(drive[:, n % 2, c * CH:(c + 1) * CH], du[:, d, c * CH:(c + 1) * CH],
                                bank[j % 2][:, :], ALU.mult).then_inc(drive_done, 1)

            def scan(b, d, n):
                i = NS * nth(b, d) + n
                at_least(dve, part_done, i - 1)
                dve.wait_ge(decay_ready, i + 1)
                dve.wait_ge(drive_done, NC * (i + 1))
                step = 1 if d == 0 else -1
                v.tensor_tensor_scan(h[:, n % 2, ::step], decay[:, n % 2, ::step], drive[:, n % 2, ::step],
                                     0.0, ALU.mult, ALU.add).then_inc(scanned, 1)

            def skip(b, d, c):
                i = nth(b, d)
                dve.wait_ge(summed, PS * i + PS - NC + c + 1)
                at_least(dve, out_full, 2 * i)
                v.scalar_tensor_tensor(y_skip[:, c * CH:(c + 1) * CH], xc_in[:, d, c * CH:(c + 1) * CH],
                                       vecs[:, d, DSK:DSK + 1], bank[4 + c][:, :], ALU.mult, ALU.add)\
                    .then_inc(skip_done, 1)

            def add_out(b, d, part):
                dve.wait_ge(out_full, 2 * nth(b, d) + part + 1)
                lo, up = 8 * part, min(8 * part + 8, NT)
                x = tok(b)[:, lo:up, :]
                v.tensor_tensor(x, x, bank[7][:, 0:(up - lo) * DM].rearrange("p (t d) -> p t d", d=DM), ALU.add)\
                    .then_inc(added, 1)

            def direction(b, d, back=True, ahead=True):
                for n in range(NS):
                    for c in range(NC):
                        product(b, d, n, c)
                        if (n, c) in SKIP_AT and back:
                            skip(*at(b, d, -1), SKIP_AT[n, c])
                        if c == 0 and n - OUT_AT - 1 in range(2) and back:
                            add_out(*at(b, d, -1), n - OUT_AT - 1)
                        if c == 0 and n - SPLIT_AT - 1 in range(NC) and ahead:
                            less_first(*at(b, d, 1), n - SPLIT_AT - 1)
                        if c == 1 and n - SOFT_AT - 1 in range(NC) and ahead:
                            finish_delta(*at(b, d, 1), n - SOFT_AT - 1)
                        if c == 2 and n - SOFT_AT - 2 in range(NC) and ahead:
                            delta_x(*at(b, d, 1), n - SOFT_AT - 2)
                    scan(b, d, n)

            for c in range(NC):
                less_first(0, 0, c)
                finish_delta(0, 0, c)
                delta_x(0, 0, c)
            direction(0, 0, back=False)
            direction(0, 1)
            with dve.Fori(1, NB - 1) as b:
                for d in range(2):
                    direction(b, d)
            direction(NB - 1, 0)
            direction(NB - 1, 1, ahead=False)
            v.memset(xl_t[DM:DM + 1, :], 1.0).then_inc(masks, 1)
            for i in range(NORM3_OPS):
                norm3(0, 0, i)
            for c in range(NC):
                skip(NB - 1, 1, c)
            for part in range(2):
                add_out(NB - 1, 1, part)
            dve.wait_ge(added, 2 * 2 * NB)
            end_phase(dve, 2)

            def compare(p, u, j):
                w, row, hi = stat3[:, u, WT, j:j + 1], w_row[u], higher[:, j, :]
                lo, up = j * P, (j + 1) * P
                ins = v.scalar_tensor_tensor(hi[:, lo:up], row[:, lo:up], w, before[:, :], ALU.is_le, ALU.mult,
                                             accum_out=row_sum[:, 0, j:j + 1])
                if j < NT - 1:
                    ins = v.tensor_scalar(hi[:, up:L], row[:, up:L], w, 0.0, ALU.is_le, ALU.add,
                                          accum_out=row_sum[:, 1, j:j + 1])
                ins.then_inc(cmp3, 1)

            def final(p, u):
                b = 2 * p + u
                q, w = stat3[:, u, S1, :], stat3[:, u, WT, :]

                def then(k, ins):
                    ins.then_inc(f3, 1)
                    if k < 4:
                        dve.wait_ge(f3, FINAL_OPS * b + k + 1)

                dve.wait_ge(cmp3, NT * (b + 1))
                then(0, v.tensor_tensor(q, row_sum[:, 0, :], threshold[:, :], ALU.add))
                then(1, v.tensor_tensor(q, q, row_sum[:, 1, :], ALU.add))
                dve.wait_ge(rk3, b + 1)
                then(2, v.tensor_tensor(q, bank[5][:, 0:NT], q, ALU.is_lt))
                then(3, v.tensor_tensor(q, q, w, ALU.mult))
                dve.wait_ge(y3, b + 1)
                at_least(dve, o3[u], 16 * p)
                for k, (lo, up) in enumerate(((0, 8), (8, NT))):
                    then(4 + k, v.tensor_tensor(
                        y_out[u][:, lo:up, :],
                        bank[6 + k][:, 0:(up - lo) * DM].rearrange("p (t d) -> p t d", d=DM),
                        q[:, lo:up].rearrange("p (t o) -> p t o", o=1).to_broadcast([P, up - lo, DM]), ALU.mult))

            NORM3_AT = {0: [0, 1], 1: [2, 3], 4: [4, 5], 6: [6, 7]}

            def pair(p, last=False):
                for u in range(2):
                    b = 2 * p + u
                    dve.wait_ge(wt3, b + 1)
                    v.tensor_copy(stat3[:, u, WT, :], bank[1][:, 256:256 + NT]).then_inc(wc3, 1)
                    dve.wait_ge(wc3, b + 1)
                    for j in range(NT):
                        compare(p, u, j)
                        for i in NORM3_AT.get(j, []) if not (last and u) else []:
                            norm3(p + u, 1 - u, i)
                    final(p, u)

            pair(0)
            with dve.Fori(1, NB // 2 - 1) as p:
                pair(p)
            pair(NB // 2 - 1, last=True)


INPUTS = ["x", "txt", "L0_tok_d_gamma_batched"] + [f"L0_tok_{n}" for n in
    ("Wq", "bq", "Wk", "bk", "Wv", "bv", "Wo", "bo", "prelu_a")] + [
    f"L0_attn_{d}_{n}" for d in ("fw", "bw") for n in
    ("norm", "in_proj", "conv_w", "conv_b", "x_proj", "dt_w", "dt_b", "A_log", "D", "out_proj")] + [
    f"L0_ffn_{n}" for n in ("wr", "br", "w1", "b1", "w2", "b2")]


def kernel(**inputs):
    import numpy as np
    import concourse.bacc as bacc
    from concourse.bass_utils import run_bass_kernel_spmd

    nc = bacc.Bacc("TRN2", target_bir_lowering=False, num_devices=1)
    arrays, handles = {}, {}
    for name in INPUTS:
        a = np.ascontiguousarray(inputs[name])
        if a.ndim == 0:
            a = a.reshape(1, 1)
        arrays[f"in_{name}"] = a
        handles[name] = nc.dram_tensor(f"in_{name}", a.shape, mybir.dt.from_np(a.dtype), kind="ExternalInput").ap()
    out = nc.dram_tensor("out", (NB, L, DM), F32, kind="ExternalOutput").ap()
    build(nc, handles, out)
    return run_bass_kernel_spmd(nc, [arrays], core_ids=[0]).results[0]["out"]
```
